# Optimizing a Trainium2 kernel written in Bass

```python
import numpy as np
import jax
import jax.numpy as jnp

def _softmax(x, axis=-1):
    return jax.nn.softmax(x, axis=axis)

def _gelu(x):
    return jax.nn.gelu(x, approximate=True)

def _silu(x):
    return jax.nn.silu(x)

def _sigmoid(x):
    return jax.nn.sigmoid(x)

def _layernorm(x, axis=-1, eps=1e-05):
    m = jnp.mean(x, axis=axis, keepdims=True)
    v = jnp.var(x, axis=axis, keepdims=True)
    return (x - m) / jnp.sqrt(v + eps)

def _scatter_add(tgt, idx, src, axis=0):
    return tgt.at[idx].add(src)

def _segment_sum(src, seg, n):
    return jax.ops.segment_sum(src, seg, n)
kernel_name = 'mk_gps_d1_gnn_r32_1caf4e'

def setup_inputs(seed: int=0):
    np.random.seed(seed)
    _w = jnp.asarray

    def _rec_inputs():
        import jax
        import jax.numpy as jnp
        _gk = jax.random.key(seed)
        x = -0.0003713 + 1 * jax.random.normal(jax.random.fold_in(_gk, 1), (3125, 256), jnp.float32)
        src = jax.random.randint(jax.random.fold_in(_gk, 2), (50000,), 0, 3125, jnp.int32)
        dst = jnp.minimum((3125 * jax.random.uniform(jax.random.fold_in(_gk, 3), (50000,)) ** 2.0).astype(jnp.int32), 99999)
        _o = jnp.argsort(dst, stable=True)
        src = src[_o]
        dst = dst[_o]
        edge_attr_128 = -5.16925e-05 + 1.00005 * jax.random.normal(jax.random.fold_in(_gk, 11), (50000, 128), jnp.float32)
        return (x, src, dst, edge_attr_128)
    x, src, dst, edge_attr_128 = _rec_inputs()

    def _L0_gnn_setup():
        import jax, jax.numpy as jnp
        import numpy as np
        N_NODES = 50000
        N_EDGES = 25000
        IN_DIM = 256
        OUT_DIM = 256
        EDGE_DIM = 128
        BN_EPS = 1e-05
        key = jax.random.key(seed)
        ks = jax.random.split(key, 10)
        s = lambda d: 1.0 / np.sqrt(d)
        return {'x': jax.random.normal(ks[0], (N_NODES, IN_DIM), dtype=jnp.float32), 'edge_index': jax.random.randint(ks[1], (2, N_EDGES), 0, N_NODES, dtype=jnp.int64), 'edge_attr': jax.random.normal(ks[2], (N_EDGES, EDGE_DIM), dtype=jnp.float32), 'W_edge': jax.random.uniform(ks[3], (EDGE_DIM, IN_DIM), jnp.float32, -s(EDGE_DIM), s(EDGE_DIM)), 'b_edge': jnp.zeros((IN_DIM,), jnp.float32), 'W1': jax.random.uniform(ks[4], (IN_DIM, OUT_DIM), jnp.float32, -s(IN_DIM), s(IN_DIM)), 'b1': jnp.zeros((OUT_DIM,), jnp.float32), 'W2': jax.random.uniform(ks[5], (OUT_DIM, OUT_DIM), jnp.float32, -s(OUT_DIM), s(OUT_DIM)), 'b2': jnp.zeros((OUT_DIM,), jnp.float32), 'eps': jnp.float32(0.0), 'gamma': jnp.ones((OUT_DIM,), jnp.float32), 'beta': jnp.zeros((OUT_DIM,), jnp.float32)}
    _L0_gnn_all = _L0_gnn_setup()
    _L0_gnn_in = {k: v for k, v in _L0_gnn_all.items() if k in ('W_edge', 'b_edge', 'W1', 'b1', 'W2', 'b2', 'eps', 'gamma', 'beta')}
    del _L0_gnn_all

    def _L0_mix_setup():
        import jax, jax.numpy as jnp
        import numpy as np
        NUM_HEADS = 8
        key = jax.random.key(seed)
        ks = jax.random.split(key, 5)
        B, N, C = (8, 512, 256)
        x = jax.random.normal(ks[0], (B, N, C), dtype=jnp.float32)
        Wq = jax.random.normal(ks[1], (C, C), dtype=jnp.float32) * 0.02
        Wkv = jax.random.normal(ks[2], (2 * C, C), dtype=jnp.float32) * 0.02
        Wproj = jax.random.normal(ks[3], (C, C), dtype=jnp.float32) * 0.02
        bproj = jnp.zeros((C,), dtype=jnp.float32)
        return {'x': x, 'Wq': Wq, 'Wkv': Wkv, 'Wproj': Wproj, 'bproj': bproj}
    _L0_mix_all = _L0_mix_setup()
    _L0_mix_in = {k: v for k, v in _L0_mix_all.items() if k in ('Wq', 'Wkv', 'Wproj', 'bproj')}
    del _L0_mix_all

    def _L0_ffn_setup():
        import jax, jax.numpy as jnp
        import numpy as np
        TOP_K = 2
        LN_EPS = 1e-05
        key = jax.random.key(seed)
        ks = jax.random.split(key, 8)
        B, S, D, E, H = (16, 1024, 256, 8, 1024)
        x = jax.random.normal(ks[0], (B, S, D), dtype=jnp.float32)
        Wr = jax.random.normal(ks[1], (D, E), dtype=jnp.float32) * 0.1
        br = jnp.zeros((E,), dtype=jnp.float32)
        ln_g = jnp.ones((E, D), dtype=jnp.float32)
        ln_b = jnp.zeros((E, D), dtype=jnp.float32)
        W1 = jax.random.normal(ks[2], (E, D, H), dtype=jnp.float32) * (1.0 / np.sqrt(D))
        b1 = jnp.zeros((E, H), dtype=jnp.float32)
        W2 = jax.random.normal(ks[3], (E, H, D), dtype=jnp.float32) * (1.0 / np.sqrt(H))
        b2 = jnp.zeros((E, D), dtype=jnp.float32)
        return {'x': x, 'Wr': Wr, 'br': br, 'ln_g': ln_g, 'ln_b': ln_b, 'W1': W1, 'b1': b1, 'W2': W2, 'b2': b2}
    _L0_ffn_all = _L0_ffn_setup()
    _L0_ffn_in = {k: v for k, v in _L0_ffn_all.items() if k in ('Wr', 'br', 'ln_g', 'ln_b', 'W1', 'b1', 'W2', 'b2')}
    del _L0_ffn_all
    return {'x': x, 'src': src, 'dst': dst, 'edge_attr_128': edge_attr_128, 'L0_gnn_W_edge': _L0_gnn_in['W_edge'], 'L0_gnn_b_edge': _L0_gnn_in['b_edge'], 'L0_gnn_W1': _L0_gnn_in['W1'], 'L0_gnn_b1': _L0_gnn_in['b1'], 'L0_gnn_W2': _L0_gnn_in['W2'], 'L0_gnn_b2': _L0_gnn_in['b2'], 'L0_gnn_eps': _L0_gnn_in['eps'], 'L0_gnn_gamma': _L0_gnn_in['gamma'], 'L0_gnn_beta': _L0_gnn_in['beta'], 'L0_mix_Wq': _L0_mix_in['Wq'], 'L0_mix_Wkv': _L0_mix_in['Wkv'], 'L0_mix_Wproj': _L0_mix_in['Wproj'], 'L0_mix_bproj': _L0_mix_in['bproj'], 'L0_ffn_Wr': _L0_ffn_in['Wr'], 'L0_ffn_br': _L0_ffn_in['br'], 'L0_ffn_ln_g': _L0_ffn_in['ln_g'], 'L0_ffn_ln_b': _L0_ffn_in['ln_b'], 'L0_ffn_W1': _L0_ffn_in['W1'], 'L0_ffn_b1': _L0_ffn_in['b1'], 'L0_ffn_W2': _L0_ffn_in['W2'], 'L0_ffn_b2': _L0_ffn_in['b2']}

def reference(x, src, dst, edge_attr_128, L0_gnn_W_edge, L0_gnn_b_edge, L0_gnn_W1, L0_gnn_b1, L0_gnn_W2, L0_gnn_b2, L0_gnn_eps, L0_gnn_gamma, L0_gnn_beta, L0_mix_Wq, L0_mix_Wkv, L0_mix_Wproj, L0_mix_bproj, L0_ffn_Wr, L0_ffn_br, L0_ffn_ln_g, L0_ffn_ln_b, L0_ffn_W1, L0_ffn_b1, L0_ffn_W2, L0_ffn_b2):
    import jax
    import jax.numpy as jnp

    def _L0_gnn_ref(x, edge_index, edge_attr, W_edge, b_edge, W1, b1, W2, b2, eps, gamma, beta):
        import jax, jax.numpy as jnp
        import numpy as np
        N_NODES = 50000
        N_EDGES = 25000
        IN_DIM = 256
        OUT_DIM = 256
        EDGE_DIM = 128
        BN_EPS = 1e-05
        src, dst = (edge_index[0], edge_index[1])
        e = edge_attr @ W_edge + b_edge
        msg = jax.nn.relu(x[src] + e)
        agg = jax.ops.segment_sum(msg, dst, num_segments=x.shape[0])
        h = (1.0 + eps) * x + agg
        h = jax.nn.relu(h @ W1 + b1) @ W2 + b2
        mean = jnp.mean(h, axis=0)
        var = jnp.var(h, axis=0)
        h = (h - mean) * jax.lax.rsqrt(var + BN_EPS) * gamma + beta
        return jax.nn.relu(h)

    def _L0_mix_ref(x, Wq, Wkv, Wproj, bproj):
        import jax, jax.numpy as jnp
        import numpy as np
        NUM_HEADS = 8
        B, N, C = x.shape
        h = NUM_HEADS
        d = C // h
        q = jnp.einsum('bnc,oc->bno', x, Wq).reshape(B, N, h, d).transpose(0, 2, 1, 3)
        kv = jnp.einsum('bnc,oc->bno', x, Wkv).reshape(B, N, 2, h, d)
        k = kv[:, :, 0].transpose(0, 2, 1, 3)
        v = kv[:, :, 1].transpose(0, 2, 1, 3)
        q = jax.nn.elu(q) + 1.0
        k = jax.nn.elu(k) + 1.0
        k_sum = k.sum(axis=2)
        D_inv = 1.0 / jnp.maximum(jnp.einsum('bhnd,bhd->bhn', q, k_sum), 1e-06)
        context = jnp.einsum('bhnd,bhne->bhde', k, v)
        attn = jnp.einsum('bhnd,bhde->bhne', q, context) * D_inv[..., None]
        out = attn.transpose(0, 2, 1, 3).reshape(B, N, C)
        out = jnp.einsum('bnc,oc->bno', out, Wproj) + bproj
        return out

    def _L0_ffn_ref(x, Wr, br, ln_g, ln_b, W1, b1, W2, b2):
        import jax, jax.numpy as jnp
        import numpy as np
        TOP_K = 2
        LN_EPS = 1e-05
        B, S, D = x.shape
        N = B * S
        xt = x.reshape(N, D)
        logits = xt @ Wr + br
        probs = jax.nn.softmax(logits, axis=-1)
        top_p, top_idx = jax.lax.top_k(probs, TOP_K)
        weights = top_p / top_p.sum(axis=-1, keepdims=True)
        mu = xt.mean(axis=-1, keepdims=True)
        var = ((xt - mu) ** 2).mean(axis=-1, keepdims=True)
        xn = (xt - mu) * jax.lax.rsqrt(var + LN_EPS)
        xe = xn[None, :, :] * ln_g[:, None, :] + ln_b[:, None, :]
        h = jax.nn.gelu(jnp.einsum('end,edh->enh', xe, W1) + b1[:, None, :], approximate=False)
        y = jnp.einsum('enh,ehd->end', h, W2) + b2[:, None, :]
        y_tok = jnp.transpose(y, (1, 0, 2))
        sel = jnp.take_along_axis(y_tok, top_idx[:, :, None], axis=1)
        out = (weights[:, :, None] * sel).sum(axis=1)
        return out.reshape(B, S, D)
    edge_index = jnp.stack([src, dst])
    xn = _layernorm(x, axis=-1)
    x = x + _L0_gnn_ref(xn, edge_index, edge_attr_128, L0_gnn_W_edge, L0_gnn_b_edge, L0_gnn_W1, L0_gnn_b1, L0_gnn_W2, L0_gnn_b2, L0_gnn_eps, L0_gnn_gamma, L0_gnn_beta) + _L0_mix_ref(xn[None], L0_mix_Wq, L0_mix_Wkv, L0_mix_Wproj, L0_mix_bproj)[0]
    x = x + _L0_ffn_ref(_layernorm(x, axis=-1)[None], L0_ffn_Wr, L0_ffn_br, L0_ffn_ln_g, L0_ffn_ln_b, L0_ffn_W1, L0_ffn_b1, L0_ffn_W2, L0_ffn_b2)[0]
    return x

_drawn_inputs = setup_inputs


def setup_inputs(seed=0):
    import zlib

    import numpy as np

    out = dict(_drawn_inputs(seed))
    spreads = {'L0_gnn_b_edge': (0.0, 0.1),
     'L0_gnn_b1': (0.0, 0.337),
     'L0_gnn_b2': (0.0, 0.8),
     'L0_gnn_gamma': (1.0, 0.2),
     'L0_gnn_beta': (0.0, 0.1),
     'L0_mix_bproj': (0.0, 0.1),
     'L0_ffn_br': (0.0, 0.1),
     'L0_ffn_ln_g': (1.0, 0.2),
     'L0_ffn_ln_b': (0.0, 0.1),
     'L0_ffn_b1': (0.0, 0.1),
     'L0_ffn_b2': (0.0, 0.1)}
    factors = {'L0_mix_Wq': 8.0, 'L0_mix_Wkv': 5.633, 'L0_mix_Wproj': 5.581}
    for name, (base, spread) in spreads.items():
        noise = np.random.default_rng([zlib.crc32(name.encode()), seed]).standard_normal(out[name].shape)
        drawn = base * np.exp(spread * noise) if base else spread * noise
        out[name] = jnp.asarray(drawn.astype(out[name].dtype))
    for name, factor in factors.items():
        out[name] = (out[name] * factor).astype(out[name].dtype)
    return out
```

```python
import concourse.bass as bass
from concourse import mybir
from contextlib import ExitStack

F32 = mybir.dt.float32
I32 = mybir.dt.int32
ALU = mybir.AluOpType
ACT = mybir.ActivationFunctionType
AX = mybir.AxisListType
PE = mybir.EngineType.PE
DVE = mybir.EngineType.DVE

P = 128
NODES, DIM = 3125, 256
EDGES, EDGE_DIM = 50000, 128
EXPERTS, HIDDEN = 8, 1024
HEAD_DIM = 32
HALVES = DIM // P
TILE = 125
TILES = NODES // TILE
CHUNK_TILES = 5
CHUNKS = TILES // CHUNK_TILES
GT = 6
GROUP = GT * P
GROUPS = -(-EDGES // GROUP)
TAIL = EDGES - (GROUPS - 1) * GROUP
PAIRS = GT // 2
BODIES = (GROUPS - 2) // 2
WINDOW = P
WINDOWS = -(-NODES // WINDOW)
COLS = 448
COL_CHUNKS = -(-NODES // COLS)
NODES_PAD = COLS * COL_CHUNKS
H_COLS = NODES_PAD + WINDOW
SLOTS = (2 * NODES + EXPERTS * (P - 1)) // P
TOKS = 4
W_DMAS = 4
CONST_DMAS = 19
FAR = 8192
LN_EPS = 1e-5
DMA_ROWS = 112
assert GROUPS % 2 == 0 and TILES + COL_CHUNKS == BODIES


class Chain:

    def __init__(self, eng, sem, base=0):
        self.eng, self.sem, self.base, self.n = eng, sem, base, 0

    def __call__(self, ins):
        self.n += 1
        ins.then_inc(self.sem, 1)
        self.eng.wait_ge(self.sem, self.base + self.n)


def build(nc, a, out):
    with ExitStack() as ctx:
        def sb(name, shape, dt=F32):
            return ctx.enter_context(nc.sbuf_tensor(name, shape, dt))

        def sem(name):
            return ctx.enter_context(nc.semaphore(name))

        node_table = nc.dram_tensor("node_table", [NODES, DIM], F32).ap()
        token_table = nc.dram_tensor("token_table", [NODES, DIM], F32).ap()
        acc_table = nc.dram_tensor("acc_table", [NODES + P, DIM], F32).ap()

        hT = sb("hT", [P, HALVES, H_COLS])
        qT = sb("qT", [P, HALVES, NODES_PAD])
        xs = sb("xs", [P, TILES, DIM])
        work = sb("work", [P, 10752])
        wts = sb("wts", [P, 2, 5376])

        def view(t, lo, *dims):
            n = 1
            for d in dims:
                n *= d
            v = t[:, lo:lo + n]
            if len(dims) == 2:
                v = v.rearrange("p (a b) -> p a b", b=dims[1])
            if len(dims) == 3:
                v = v.rearrange("p (a b c) -> p a b c", b=dims[1], c=dims[2])
            return v

        ea = view(work, 0, 2, GT, EDGE_DIM)
        xg = view(work, 1536, 2, GT, DIM)
        eaT = view(work, 4608, 2, GT, P)
        msg = view(work, 6144, 2, GT, DIM)
        onehot = view(work, 9216, 2, GT, P)
        table_stage = view(work, 1536, 2, CHUNK_TILES, DIM)
        w_natural = view(work, 6144, 8, DIM)
        z1 = view(work, 0, 2, HALVES, COLS)
        y_cur = view(work, 1792, HALVES, CHUNK_TILES * TILE)
        xn_cur = view(work, 3072, CHUNK_TILES, DIM)
        xnT = view(work, 4352, CHUNK_TILES, HALVES, TILE)
        ob = view(work, 5632, 2, CHUNK_TILES, P)
        oa = view(work, 6912, 2 * CHUNK_TILES, 3, SLOTS)
        tok = view(work, 0, TOKS, DIM)
        xeT = view(work, 1024, 2, HALVES, P)
        hid = view(work, 1536, 2, HIDDEN)
        hidT = view(work, 3584, HIDDEN // P, P)
        ys = view(work, 4608, 2, DIM)
        early = wts[:, 1, :]
        dst_i = early[0:GROUPS, 0:GROUP].bitcast(I32)
        dst_f = early[0:GROUPS, 768:768 + GROUP]
        rel = early[0:GROUPS, 1536:1536 + GROUP]
        src_i = early[0:GROUPS, 2304:2304 + GROUP].bitcast(I32)
        src_f = early[0:GROUPS, 3072:3072 + GROUP]
        qn = view(early, 2304, HALVES, COLS)
        dinv = view(early, 3200, HALVES, COLS)

        relT = sb("relT", [P, GROUPS, GT])
        srcT = sb("srcT", [P, GROUPS, GT], I32)
        idx_cur = sb("idx_cur", [P, 2, GT], I32)
        base_row = sb("base_row", [1, P], I32)
        miss_i = sb("miss_i", [1, 1], I32)
        gstat = sb("gstat", [GROUPS, 4])
        w_edge = sb("w_edge", [P, DIM])
        w1 = sb("w1", [P, HALVES, DIM])
        w2 = sb("w2", [P, HALVES, DIM])
        wqT = sb("wqT", [P, HALVES, DIM])
        wkvT = sb("wkvT", [P, HALVES, 2 * DIM])
        wpT = sb("wpT", [P, HALVES, DIM])
        wr = sb("wr", [P, HALVES, EXPERTS])
        br = sb("br", [P, EXPERTS])
        b_edge = sb("b_edge", [P, DIM])
        cvec = sb("cvec", [P, 5, HALVES])
        B1, B2, GAMMA, BETA, BPROJ = range(5)
        eps1 = sb("eps1", [P, 1])
        ln_g = sb("ln_g", [P, EXPERTS, HALVES])
        ln_b = sb("ln_b", [P, EXPERTS, HALVES])
        iota_i = sb("iota_i", [P, P], I32)
        iota_f = sb("iota_f", [P, P])
        part_i = sb("part_i", [P, 1], I32)
        part_f = sb("part_f", [P, 1])
        ident = sb("ident", [P, P])
        below = sb("below", [P, P])
        ones = sb("ones", [P, P])
        blocks = sb("blocks", [P, P])
        st = sb("st", [P, TILES, 6])
        ln = sb("ln", [P, 8, TILES])
        xn_t = sb("xn_t", [P, DIM])
        xT_t = sb("xT_t", [P, HALVES, TILE])
        ek = sb("ek", [P, DIM])
        k_t = sb("k_t", [P, DIM])
        v_t = sb("v_t", [P, DIM])
        eq = sb("eq", [P, HALVES, TILE])
        rq = sb("rq", [P, HALVES, TILE])
        ctx_acc = sb("ctx_acc", [P, 2 * P])
        k_acc = sb("k_acc", [P, DIM])
        ctx_m = sb("ctx_m", [P, HALVES, P])
        ksum_m = sb("ksum_m", [P, HALVES, P])
        attn_w = sb("attn_w", [P, HALVES, DIM])
        bn = sb("bn", [P, HALVES, COL_CHUNKS, 6])
        mv = sb("mv", [P, HALVES, 2])
        bns = sb("bns", [P, 4, HALVES])
        logits = sb("logits", [P, TILES, EXPERTS])
        rt = sb("rt", [P, 6, TILES, EXPERTS])
        rs = sb("rs", [P, 10, TILES])
        rsi = sb("rsi", [P, 2, TILES], I32)
        ex = sb("ex", [P, 6, EXPERTS])
        exi = sb("exi", [P, EXPERTS], I32)
        tokid = sb("tokid", [P, TILES])
        tokid_i = sb("tokid_i", [P, TILES], I32)
        slot_f = sb("slot_f", [P, 3, SLOTS])
        tok_i = sb("tok_i", [P, SLOTS], I32)
        row_i = sb("row_i", [P, SLOTS], I32)
        ej = sb("ej", [P, 2, SLOTS])
        ej_i = sb("ej_i", [1, SLOTS + 8], I32)
        first_i = sb("first_i", [1, EXPERTS], I32)
        tokc = sb("tokc", [P, TOKS], I32)
        rowc = sb("rowc", [P, 2], I32)

        bank = [ctx.enter_context(nc.psum_tensor(f"bank{i}", [P, 512], F32)) for i in range(8)]

        x_in = [sem(f"x_in{c}") for c in range(CHUNKS)]
        consts_in = sem("consts_in")
        ids_in = sem("ids_in")
        pool_chain = sem("pool_chain")
        pool_passed = sem("pool_passed")
        consts_made = sem("consts_made")
        dve_chain = sem("dve_chain")
        act_chain = sem("act_chain")
        var_ready = sem("var_ready")
        sd_ready = sem("sd_ready")
        ln_ready = sem("ln_ready")
        xn_ready = sem("xn_ready")
        rows_ready = sem("rows_ready")
        rows_stored = [sem(f"rows_stored{i}") for i in range(2)]
        ids_memset = sem("ids_memset")
        rel_ready = sem("rel_ready")
        base_T = sem("base_T")
        ids_T = sem("ids_T")
        ids_used = sem("ids_used")
        tables_ready = sem("tables_ready")
        wT_ready = sem("wT_ready")
        wT_copied = sem("wT_copied")

        ea_in = [sem(f"ea_in{u}") for u in range(2)]
        ea_tail = sem("ea_tail")
        idx_ready = sem("idx_ready")
        xg_in = [[sem(f"xg_in{u}_{q}") for q in range(PAIRS)] for u in range(2)]
        eaT_ps = sem("eaT_ps")
        eaT_ready = sem("eaT_ready")
        e_ready = sem("e_ready")
        sums_done = sem("sums_done")
        msg_ready = sem("msg_ready")
        onehot_ready = sem("onehot_ready")
        agg_ready = sem("agg_ready")
        h_updates = sem("h_updates")
        agg_read = sem("agg_read")

        mx_in = sem("mx_in")
        mx_T = sem("mx_T")
        mx_xT = sem("mx_xT")
        mx_kv = sem("mx_kv")
        mx_q = sem("mx_q")
        mx_ek = sem("mx_ek")
        mx_v = sem("mx_v")
        mx_eq = sem("mx_eq")
        mx_rk = sem("mx_rk")
        mx_k = sem("mx_k")
        mx_rq = sem("mx_rq")
        mx_qT = sem("mx_qT")
        mx_ctx = sem("mx_ctx")
        mx_acc = sem("mx_acc")
        mx_kacc = sem("mx_kacc")
        ksum_ps = sem("ksum_ps")
        ctx_masked = sem("ctx_masked")
        aw_ps = sem("aw_ps")
        aw_ready = sem("aw_ready")
        den_ps = sem("den_ps")
        den_max = sem("den_max")
        den_inv = sem("den_inv")
        qn_ready = sem("qn_ready")
        ao_ps = sem("ao_ps")
        ao_ready = sem("ao_ready")

        pass_done = sem("pass_done")
        pass_tables = sem("pass_tables")
        pass_T = sem("pass_T")
        edges_done = sem("edges_done")
        x_again = sem("x_again")

        z1_ps = sem("z1_ps")
        z1_ready = sem("z1_ready")
        z2_ps = sem("z2_ps")
        z2_ready = sem("z2_ready")
        bn_var = sem("bn_var")
        bn_sd = sem("bn_sd")
        bn_ready = sem("bn_ready")
        y_relu = sem("y_relu")
        y_sum = sem("y_sum")
        y_T = sem("y_T")
        x1_ready = sem("x1_ready")
        x1_stats = sem("x1_stats")
        x1_stored = sem("x1_stored")
        trash_stored = sem("trash_stored")
        l2_var = sem("l2_var")
        l2_sd = sem("l2_sd")
        l2_var2 = sem("l2_var2")
        l2_sd2 = sem("l2_sd2")
        l2_ready = sem("l2_ready")
        tk_ready = sem("tk_ready")
        tk_stored = sem("tk_stored")
        tk_T = sem("tk_T")
        tk_xT = sem("tk_xT")
        tk_lg = sem("tk_lg")
        tk_scaled = sem("tk_scaled")
        lg_ready = sem("lg_ready")
        gate_in = sem("gate_in")
        gate_exp = sem("gate_exp")
        cnt_ready = sem("cnt_ready")
        rank_ps = sem("rank_ps")
        oh_ready = sem("oh_ready")
        list_step = sem("list_step")
        list_zero = sem("list_zero")
        lists_ready = sem("lists_ready")

        w_in = [sem(f"w_in{i}") for i in range(2)]
        cur_ready = sem("cur_ready")
        tok_in = [sem(f"tok_in{i}") for i in range(TOKS)]
        tok_T = sem("tok_T")
        xeT_half = sem("xeT_half")
        hid_ps = sem("hid_ps")
        hid_b = sem("hid_b")
        hid_g = sem("hid_g")
        hidT_ps = sem("hidT_ps")
        hidT_a = sem("hidT_a")
        hidT_v = sem("hidT_v")
        y_ps = sem("y_ps")
        y_b = sem("y_b")
        y_w = sem("y_w")
        row_ready = sem("row_ready")
        acc_in = sem("acc_in")
        out_in = sem("out_in")

        block = ctx.enter_context(nc.Block())

        def experts_of(engine, j, n):
            return nc.values_load_multi_w_load_instructions(ej_i[0:1, bass.ds(j + 3, n)], engines=(engine,), min_val=0,
                                                            max_val=EXPERTS - 1)[1]

        def node_rows(dram, sbuf, c):
            d = dram[bass.ds(c * CHUNK_TILES * TILE, CHUNK_TILES * TILE), :].rearrange("(t p) d -> p t d", p=TILE)
            return [(d[0:DMA_ROWS], sbuf[0:DMA_ROWS]), (d[DMA_ROWS:TILE], sbuf[DMA_ROWS:TILE])]


        def load_edges(sp, g, n, r, u, fresh):
            if not fresh:
                sp.wait_ge(eaT_ps, 2 * (n - 1))
            rows = a["edge_attr_128"][bass.ds(g * GROUP, GROUP), :].rearrange("(p j) d -> p (j d)", j=GT)
            sp.dma_start(ea[:, u].rearrange("p j d -> p (j d)"), rows).then_inc(ea_in[u], 16)

        def load_tail(sp, n, passes):
            full, rest = TAIL // GT, TAIL % GT
            sp.wait_ge(eaT_ps, 2 * (n - 1))
            start = (GROUPS - 1) * GROUP
            last = a["edge_attr_128"][start + full * GT:start + TAIL, :].rearrange("(p j) d -> p (j d)", j=rest)
            sp.dma_start(ea[full:full + 1, 1, 0:rest, :].rearrange("p j d -> p (j d)"), last).then_inc(ea_tail, 16)
            sp.wait_ge(ea_tail, 16 * (passes + 1))
            rows = a["edge_attr_128"][start:start + full * GT, :].rearrange("(p j) d -> p (j d)", j=GT)
            sp.dma_start(ea[0:full, 1].rearrange("p j d -> p (j d)"), rows).then_inc(ea_in[1], 16)

        def gather_nodes(pool, n, u, fresh):
            pool.wait_ge(idx_ready, n + 1)
            if not fresh:
                pool.wait_ge(sums_done, PAIRS * (n - 1))
            pool.sem_inc(pool_passed, 1)
            for j in range(GT):
                pool.indirect_dma_start(out=xg[:, u, j], out_offset=None, in_=node_table,
                                        in_offset=bass.IndirectOffsetOnAxis(ap=idx_cur[:, u, j:j + 1], axis=0)
                                        ).then_inc(xg_in[u][j // 2], 16)

        def transpose_edges(pe, n, r, u, fresh):
            pe.wait_ge(ea_in[u], 16 * (r + 1))
            for hh in range(2):
                if not fresh:
                    pe.wait_ge(eaT_ready, 2 * (n - 1) + hh + 1)
                for k in range(3):
                    last = nc.tensor.transpose(bank[hh][:, k * P:(k + 1) * P], ea[:, u, 3 * hh + k], ident[:])
                last.then_inc(eaT_ps, 1)

        def embed_edges(pe, n, r, u, fresh):
            for q in range(PAIRS):
                pe.wait_ge(eaT_ready, 2 * n + (1 if q == 0 else 2))
                if not fresh:
                    pe.wait_ge(sums_done, PAIRS * (n - 1) + q + 1)
                b = bank[2 + q]
                for k in range(2):
                    last = nc.tensor.matmul(b[:, k * DIM:(k + 1) * DIM], eaT[:, u, 2 * q + k], w_edge[:],
                                            start=True, stop=True)
                last.then_inc(e_ready, 1)

        def aggregate(pe, n, u):
            b = bank[5]
            pe.wait_ge(agg_read, n + 1)
            pe.wait_ge(onehot_ready, n + 1)
            for j in range(GT):
                if j % 2 == 0:
                    pe.wait_ge(msg_ready, PAIRS * n + j // 2 + 1)
                for h in range(HALVES):
                    last = nc.tensor.matmul(b[:, h * P:(h + 1) * P], msg[:, u, j, h * P:(h + 1) * P], onehot[:, u, j],
                                            start=(j == 0 and h == 0), stop=(j == GT - 1), skip_group_check=True)
            last.then_inc(agg_ready, 1)

        def copy_edges(act, n, u):
            for hh in range(2):
                act.wait_ge(eaT_ps, 2 * n + hh + 1)
                nc.scalar.copy(eaT[:, u, 3 * hh:3 * hh + 3], bank[hh][:, 0:3 * P].rearrange("p (k c) -> p k c", k=3)
                               ).then_inc(eaT_ready, 1)

        def relu_messages(act, g, n, r, u, more):
            if more:
                for q in range(PAIRS):
                    act.wait_ge(xg_in[u][q], 32 * (r + 1))
                nc.scalar.copy(idx_cur[:, u], srcT[:, bass.ds(g + 2, 1)].rearrange("p a j -> p (a j)")
                               ).then_inc(idx_ready, 1)
            for q in range(PAIRS):
                act.wait_ge(sums_done, PAIRS * n + q + 1)
                nc.scalar.activation(msg[:, u, 2 * q:2 * q + 2], msg[:, u, 2 * q:2 * q + 2], ACT.Relu
                                     ).then_inc(msg_ready, 1)

        def mark_window(dve, g, u):
            nc.vector.tensor_tensor(onehot[:, u], iota_f[:].unsqueeze(1).to_broadcast([P, GT, P]),
                                    relT[:, bass.ds(g, 1)].rearrange("p a j -> p (a j)").unsqueeze(2).to_broadcast([P, GT, P]),
                                    ALU.is_equal).then_inc(onehot_ready, 1)

        def add_nodes(dve, n, r, u):
            for q in range(PAIRS):
                dve.wait_ge(e_ready, PAIRS * n + q + 1)
                dve.wait_ge(xg_in[u][q], 32 * (r + 1))
                nc.vector.tensor_tensor(msg[:, u, 2 * q:2 * q + 2],
                                        bank[2 + q][:].rearrange("p (k c) -> p k c", k=2),
                                        xg[:, u, 2 * q:2 * q + 2], ALU.add).then_inc(sums_done, 1)

        def add_window(dve, n, u, start, h_count):
            dve.wait_ge(agg_ready, n + 1)
            dve.wait_ge(h_updates, h_count)
            w = hT[:, :, bass.ds(start, WINDOW)]
            nc.vector.tensor_tensor(w, bank[5][:, 0:HALVES * P].rearrange("p (h c) -> p h c", h=HALVES),
                                    w, ALU.add).then_inc(h_updates, 1)

        def load_expert(sp, e):
            s = wts[:, e % 2]
            sp.dma_start(view(s, 0, HALVES, HIDDEN), a["L0_ffn_W1"][e].rearrange("(k p) h -> p k h", p=P)
                         ).then_inc(w_in[e % 2], 16)
            sp.dma_start(view(s, 2048, HIDDEN // P, DIM), a["L0_ffn_W2"][e].rearrange("(c p) d -> p c d", p=P)
                         ).then_inc(w_in[e % 2], 16)
            sp.dma_start(s[:, 4096:4096 + HIDDEN], a["L0_ffn_b1"][e].partition_broadcast(P)).then_inc(w_in[e % 2], 16)
            sp.dma_start(s[:, 5120:5120 + DIM], a["L0_ffn_b2"][e].partition_broadcast(P)).then_inc(w_in[e % 2], 16)

        @block.sync
        def _(sp):
            for c in range(CHUNKS):
                for d, s in node_rows(a["x"], xs[:, c * CHUNK_TILES:(c + 1) * CHUNK_TILES], c):
                    sp.dma_start(s, d).then_inc(x_in[c], 16)
            sp.wait_ge(ids_memset, 2)
            for name, t in (("dst", dst_i), ("src", src_i)):
                v = a[name]
                full = (GROUPS - 1) * GROUP
                sp.dma_start(t[0:GROUPS - 1], v[0:full].rearrange("(g e) -> g e", e=GROUP)).then_inc(ids_in, 16)
                sp.dma_start(t[GROUPS - 1:GROUPS, 0:TAIL], v[full:EDGES].unsqueeze(0)).then_inc(ids_in, 16)
            load_edges(sp, 0, 0, 0, 0, True)
            load_edges(sp, 1, 1, 0, 1, True)
            for c in range(CHUNKS):
                sp.wait_ge(rows_ready, c + 1)
                for d, s in node_rows(node_table, table_stage[:, c % 2], c):
                    sp.dma_start(d, s).then_inc(rows_stored[c % 2], 16)
            load_expert(sp, 0)

            with sp.Fori(0, BODIES - 1) as i:
                load_edges(sp, 2 * i + 2, 2 * i + 2, i + 1, 0, False)
                load_edges(sp, 2 * i + 3, 2 * i + 3, i + 1, 1, False)
            load_edges(sp, GROUPS - 2, GROUPS - 2, BODIES, 0, False)
            load_tail(sp, GROUPS - 1, 0)
            sp.wait_ge(mx_in, TILES)
            for c in range(CHUNKS):
                for d, s in node_rows(a["x"], xs[:, c * CHUNK_TILES:(c + 1) * CHUNK_TILES], c):
                    sp.dma_start(s, d).then_inc(x_again, 16)

            sp.wait_ge(tables_ready, 3)
            again = sp.value_load(miss_i[0:1, 0:1], min_val=0, max_val=1)
            with sp.If(again > 0):
                with sp.Fori(0, WINDOWS) as w:
                    n0 = (w + 1) * GROUPS
                    r0 = (w + 1) * (GROUPS // 2)
                    load_edges(sp, 0, n0, r0, 0, False)
                    load_edges(sp, 1, n0 + 1, r0, 1, False)
                    with sp.Fori(0, BODIES - 1) as i:
                        load_edges(sp, 2 * i + 2, n0 + 2 * i + 2, r0 + i + 1, 0, False)
                        load_edges(sp, 2 * i + 3, n0 + 2 * i + 3, r0 + i + 1, 1, False)
                    load_edges(sp, GROUPS - 2, n0 + GROUPS - 2, r0 + BODIES, 0, False)
                    load_tail(sp, n0 + GROUPS - 1, w + 1)
            with sp.Else():
                sp.nop()
            sp.wait_ge(edges_done, 2)
            load_expert(sp, 1)
            sp.dma_start(acc_table[NODES:NODES + P, :], ek[:]).then_inc(trash_stored, 16)
            sp.wait_ge(x1_ready, 3 * CHUNKS)
            for c in range(CHUNKS):
                for d, s in node_rows(acc_table, xs[:, c * CHUNK_TILES:(c + 1) * CHUNK_TILES], c):
                    sp.dma_start(d, s).then_inc(x1_stored, 16)
            with sp.Fori(0, CHUNKS) as c:
                sp.wait_ge(tk_ready, c + 1)
                for d, s in node_rows(token_table, xn_cur, c):
                    sp.dma_start(d, s).then_inc(tk_stored, 16)
            sp.wait_ge(lists_ready, 1)
            for e in range(2, EXPERTS):
                done = sp.value_load(first_i[0:1, e - 1:e], min_val=0, max_val=SLOTS)
                sp.wait_ge(y_b, done)
                sp.wait_ge(w_in[e % 2], 16 * W_DMAS * (e // 2))
                load_expert(sp, e)
            sp.wait_ge(acc_in, 16 * SLOTS)
            sp.dma_start(out.rearrange("n d -> (n d)").rearrange("(r c) -> r c", r=80),
                         acc_table[0:NODES, :].rearrange("n d -> (n d)").rearrange("(r c) -> r c", r=80)
                         ).then_inc(out_in, 16)
            sp.wait_ge(out_in, 16)

        @block.gpsimd
        def _(pool):
            step = Chain(pool, pool_chain)
            nc.gpsimd.iota(iota_i[:], pattern=[[1, P]], base=0, channel_multiplier=0).then_inc(consts_made, 1)
            nc.gpsimd.iota(part_i[:], pattern=[[1, 1]], base=0, channel_multiplier=1).then_inc(consts_made, 1)
            nc.gpsimd.iota(tokid_i[:], pattern=[[TILE, TILES]], base=0, channel_multiplier=1).then_inc(consts_made, 1)
            step(nc.gpsimd.memset(ident[:], 0.0))
            nc.gpsimd.affine_select(out=ident[:], in_=ident[:], compare_op=ALU.not_equal, fill=1.0, base=0,
                                    pattern=[[-1, P]], channel_multiplier=1).then_inc(consts_made, 1)
            nc.gpsimd.memset(ones[:], 1.0).then_inc(consts_made, 1)
            step(nc.gpsimd.memset(below[:], 1.0))
            nc.gpsimd.affine_select(out=below[:], in_=below[:], compare_op=ALU.is_gt, fill=0.0, base=0,
                                    pattern=[[1, P]], channel_multiplier=-1).then_inc(consts_made, 1)
            step(nc.gpsimd.memset(blocks[:], 0.0))
            for b in range(P // HEAD_DIM):
                s = slice(b * HEAD_DIM, (b + 1) * HEAD_DIM)
                step(nc.gpsimd.memset(blocks[s, s], 1.0))
            nc.gpsimd.memset(hT[:], 0.0).then_inc(h_updates, 1)
            nc.gpsimd.memset(qT[:, :, NODES:NODES_PAD], 0.0).then_inc(consts_made, 1)
            nc.gpsimd.memset(ctx_acc[:], 0.0).then_inc(mx_acc, 1)
            nc.gpsimd.memset(k_acc[:], 0.0).then_inc(mx_kacc, 1)

            for c in range(2):
                pool.wait_ge(rows_stored[c], 32 * ((CHUNKS + 1 - c) // 2))
            gather_nodes(pool, 0, 0, True)
            gather_nodes(pool, 1, 1, True)
            with pool.Fori(0, BODIES) as i:
                gather_nodes(pool, 2 * i + 2, 0, False)
                gather_nodes(pool, 2 * i + 3, 1, False)
            pool.wait_ge(tables_ready, 3)
            again = pool.value_load(miss_i[0:1, 0:1], min_val=0, max_val=1)
            with pool.If(again > 0):
                with pool.Fori(0, WINDOWS) as w:
                    n0 = (w + 1) * GROUPS
                    gather_nodes(pool, n0, 0, False)
                    gather_nodes(pool, n0 + 1, 1, False)
                    with pool.Fori(0, BODIES) as i:
                        gather_nodes(pool, n0 + 2 * i + 2, 0, False)
                        gather_nodes(pool, n0 + 2 * i + 3, 1, False)
            with pool.Else():
                pool.nop()

            pool.wait_ge(tk_stored, 32 * CHUNKS)
            pool.wait_ge(x1_stored, 32 * CHUNKS)
            pool.wait_ge(trash_stored, 16)
            pool.wait_ge(lists_ready, 1)

            def fetch(j, r, u, fresh):
                pool.wait_ge(tok_in[u], 16 * r)
                nc.gpsimd.tensor_copy(tokc[:, u:u + 1], tok_i[:, bass.ds(j, 1)]).then_inc(cur_ready, 1)
                pool.wait_ge(cur_ready, j + 1)
                if not fresh:
                    pool.wait_ge(tok_T, j - TOKS + 1)
                pool.sem_inc(pool_passed, 1)
                pool.indirect_dma_start(out=tok[:, u], out_offset=None, in_=token_table,
                                        in_offset=bass.IndirectOffsetOnAxis(ap=tokc[:, u:u + 1], axis=0)
                                        ).then_inc(tok_in[u], 16)

            def put(j, u):
                pool.wait_ge(acc_in, 16 * j)
                nc.gpsimd.tensor_copy(rowc[:, u:u + 1], row_i[:, bass.ds(j, 1)]).then_inc(row_ready, 1)
                pool.wait_ge(row_ready, j + 1)
                pool.wait_ge(y_w, j + 1)
                pool.sem_inc(pool_passed, 1)
                pool.indirect_dma_start(out=acc_table, out_offset=bass.IndirectOffsetOnAxis(ap=rowc[:, u:u + 1], axis=0),
                                        in_=ys[:, u], in_offset=None, compute_op=ALU.add).then_inc(acc_in, 16)

            for k in range(TOKS):
                fetch(k, 0, k, True)
            with pool.Fori(0, SLOTS // TOKS - 1) as i:
                for k in range(TOKS):
                    fetch(TOKS * (i + 1) + k, i + 1, k, False)
                    put(TOKS * i + k, k % 2)
            for k in range(TOKS):
                put(SLOTS - TOKS + k, k % 2)

        @block.tensor
        def _(pe):
            pe.wait_ge(consts_made, 7)
            pe.wait_ge(rel_ready, 1)
            nc.tensor.transpose(bank[6][0:1, 0:GROUPS], gstat[:, 0:1], ident[0:GROUPS, 0:GROUPS])
            nc.tensor.transpose(bank[6][0:1, P:P + GROUPS], gstat[:, 1:2], ident[0:GROUPS, 0:GROUPS]).then_inc(base_T, 1)
            for j in range(GT):
                nc.tensor.transpose(bank[4][:, j * GROUPS:(j + 1) * GROUPS], rel[:, j:GROUP:GT], ident[0:GROUPS, 0:GROUPS])
            for j in range(GT):
                last = nc.tensor.transpose(bank[5][:, j * GROUPS:(j + 1) * GROUPS], src_f[:, j:GROUP:GT], ident[0:GROUPS, 0:GROUPS])
            last.then_inc(ids_T, 1)
            pe.wait_ge(consts_in, CONST_DMAS * 16)
            for rb in range(8):
                for k in range(HALVES):
                    if rb < 2:
                        o = bank[0][:, k * 256 + rb * P:k * 256 + (rb + 1) * P]
                    elif rb < 6:
                        o = bank[1 + k][:, (rb - 2) * P:(rb - 1) * P]
                    else:
                        o = bank[3][:, k * 256 + (rb - 6) * P:k * 256 + (rb - 5) * P]
                    last = nc.tensor.transpose(o, w_natural[:, rb, k * P:(k + 1) * P], ident[:])
            last.then_inc(wT_ready, 1)
            pe.wait_ge(wT_copied, 4)
            pe.wait_ge(tables_ready, 3)

            def mix_transpose(t):
                pe.wait_ge(mx_in, t + 1)
                pe.wait_ge(mx_acc, t + 1)
                for k in range(HALVES):
                    last = nc.tensor.transpose(bank[7][:, k * TILE:(k + 1) * TILE], xn_t[0:TILE, k * P:(k + 1) * P],
                                               ident[0:TILE, 0:TILE])
                last.then_inc(mx_T, 1)

            def mix_qkv(t):
                pe.wait_ge(mx_xT, t + 1)
                pe.wait_ge(mx_rk, t)
                pe.wait_ge(mx_ek, t)
                pe.wait_ge(mx_v, t)
                for k in range(HALVES):
                    last = nc.tensor.matmul(bank[6][0:TILE, :], xT_t[:, k], wkvT[:, k], start=(k == 0), stop=(k == 1))
                last.then_inc(mx_kv, 1)
                pe.wait_ge(h_updates, 3 * t + 3)
                for o in range(HALVES):
                    for k in range(HALVES):
                        last = nc.tensor.matmul(bank[7][:, o * TILE:(o + 1) * TILE], wqT[:, k, o * P:(o + 1) * P],
                                                xT_t[:, k], start=(k == 0), stop=(k == 1))
                last.then_inc(mx_q, 1)

            def mix_context(t):
                pe.wait_ge(mx_k, t + 1)
                pe.wait_ge(mx_v, t + 1)
                pe.wait_ge(mx_rq, t + 1)
                for h in range(HALVES):
                    s = slice(h * P, (h + 1) * P)
                    last = nc.tensor.matmul(bank[7][:, h * P:(h + 1) * P], v_t[0:TILE, s], k_t[0:TILE, s],
                                            start=True, stop=True)
                last.then_inc(mx_ctx, 1)

            def attn_den(c):
                pe.wait_ge(ao_ready, 2 * c)
                for h in range(HALVES):
                    last = nc.tensor.matmul(bank[6 + h][:, 0:COLS], ksum_m[:, h], qT[:, h, bass.ds(c * COLS, COLS)],
                                            start=True, stop=True)
                last.then_inc(den_ps, 1)

            def attn_out(c):
                pe.wait_ge(qn_ready, c + 1)
                for o in range(HALVES):
                    for h in range(HALVES):
                        last = nc.tensor.matmul(bank[6 + o][:, 0:COLS], attn_w[:, h, o * P:(o + 1) * P], qn[:, h],
                                                start=(h == 0), stop=(h == 1))
                    last.then_inc(ao_ps, 1)

            def edge_pass(n0, r0, fresh, phases):
                transpose_edges(pe, n0, r0, 0, fresh)
                transpose_edges(pe, n0 + 1, r0, 1, False)
                embed_edges(pe, n0, r0, 0, fresh)

                def body(i, riders):
                    n = n0 + 2 * i
                    transpose_edges(pe, n + 2, r0 + i + 1, 0, False)
                    embed_edges(pe, n + 1, r0 + i, 1, False)
                    if riders:
                        riders[0](i)
                    aggregate(pe, n, 0)
                    if riders and riders[1]:
                        riders[1](i)
                    transpose_edges(pe, n + 3, r0 + i + 1, 1, False)
                    embed_edges(pe, n + 2, r0 + i + 1, 0, False)
                    aggregate(pe, n + 1, 1)
                    if riders and riders[2]:
                        riders[2](i)

                for lo, hi, riders, between in phases:
                    with pe.Fori(lo, hi) as i:
                        body(i, riders)
                    if between:
                        between()
                n = n0 + GROUPS
                embed_edges(pe, n - 1, r0 + BODIES, 1, False)
                aggregate(pe, n - 2, 0)
                aggregate(pe, n - 1, 1)

            def attn_weights():
                pe.wait_ge(mx_kacc, TILES + 1)
                pe.wait_ge(mx_acc, TILES + 1)
                for h in range(HALVES):
                    last = nc.tensor.matmul(bank[7][:, h:h + 1], k_acc[0:TILE, h * P:(h + 1) * P], ones[0:TILE, 0:1],
                                            start=True, stop=True)
                last.then_inc(ksum_ps, 1)
                pe.wait_ge(ctx_masked, 4)
                pe.wait_ge(mx_rk, TILES)
                pe.wait_ge(mx_ek, TILES)
                pe.wait_ge(mx_v, TILES)
                for h in range(HALVES):
                    last = nc.tensor.matmul(bank[6][:, h * DIM:(h + 1) * DIM], ctx_m[:, h], wpT[:, h], start=True, stop=True)
                last.then_inc(aw_ps, 1)
                pe.wait_ge(aw_ready, 1)

            edge_pass(0, 0, True, [
                (0, TILES, (mix_transpose, mix_qkv, mix_context), attn_weights),
                (TILES, BODIES, (lambda i: attn_den(i - TILES), None, lambda i: attn_out(i - TILES)), None)])
            again = pe.value_load(miss_i[0:1, 0:1], min_val=0, max_val=1)
            with pe.If(again > 0):
                pe.wait_ge(pass_tables, 3)
                for j in range(GT):
                    last = nc.tensor.transpose(bank[4][:, j * GROUPS:(j + 1) * GROUPS], rel[:, j:GROUP:GT], ident[0:GROUPS, 0:GROUPS])
                last.then_inc(pass_T, 1)
                pe.wait_ge(pass_done, 1)
                with pe.Fori(0, WINDOWS) as w:
                    edge_pass((w + 1) * GROUPS, (w + 1) * (GROUPS // 2), False, [(0, BODIES, None, None)])
            with pe.Else():
                pe.nop()

            pe.wait_ge(edges_done, 2)

            def mlp1(c, u, fresh):
                for o in range(HALVES):
                    if not fresh:
                        pe.wait_ge(z1_ready, 2 * (c - 1) + o + 1)
                    for k in range(HALVES):
                        last = nc.tensor.matmul(bank[o][:, 0:COLS], w1[:, k, o * P:(o + 1) * P],
                                                hT[:, k, bass.ds(c * COLS, COLS)], start=(k == 0), stop=(k == 1))
                    last.then_inc(z1_ps, 1)

            def mlp2(c, u, fresh):
                pe.wait_ge(z1_ready, 2 * c + 2)
                for o in range(HALVES):
                    if not fresh:
                        pe.wait_ge(z2_ready, 2 * (c - 1) + o + 1)
                    for k in range(HALVES):
                        last = nc.tensor.matmul(bank[2 + o][:, 0:COLS], w2[:, k, o * P:(o + 1) * P], z1[:, u, k],
                                                start=(k == 0), stop=(k == 1))
                    last.then_inc(z2_ps, 1)

            mlp1(0, 0, True)
            mlp1(1, 1, False)
            mlp2(0, 0, True)
            with pe.Fori(0, (COL_CHUNKS - 3) // 2) as i:
                mlp1(2 * i + 2, 0, False)
                mlp2(2 * i + 1, 1, False)
                mlp1(2 * i + 3, 1, False)
                mlp2(2 * i + 2, 0, False)
            mlp1(COL_CHUNKS - 1, 0, False)
            mlp2(COL_CHUNKS - 2, 1, False)
            mlp2(COL_CHUNKS - 1, 0, False)

            with pe.Fori(0, CHUNKS) as c:
                pe.wait_ge(y_sum, c + 1)
                pe.wait_ge(x1_ready, 3 * c)
                for k in range(CHUNK_TILES):
                    for h in range(HALVES):
                        last = nc.tensor.transpose(bank[k // 2][0:TILE, (k % 2) * DIM + h * P:(k % 2) * DIM + (h + 1) * P],
                                                   y_cur[:, h, k * TILE:(k + 1) * TILE], ident[:])
                last.then_inc(y_T, 1)
            with pe.Fori(0, CHUNKS) as c:
                pe.wait_ge(tk_ready, c + 1)
                pe.wait_ge(tk_xT, 3 * c)
                for k in range(2 * CHUNK_TILES):
                    t, h = k // 2, k % 2
                    last = nc.tensor.transpose(bank[4 + k // 4][:, (k % 4) * TILE:(k % 4 + 1) * TILE],
                                               xn_cur[0:TILE, t, h * P:(h + 1) * P], ident[0:TILE, 0:TILE])
                last.then_inc(tk_T, 1)
                pe.wait_ge(tk_xT, 3 * c + 3)
                pe.wait_ge(tk_scaled, c)
                for t in range(CHUNK_TILES):
                    for h in range(HALVES):
                        last = nc.tensor.matmul(bank[7][0:TILE, t * EXPERTS:(t + 1) * EXPERTS], xnT[:, t, h], wr[:, h],
                                                start=(h == 0), stop=(h == 1))
                last.then_inc(tk_lg, 1)
            pe.wait_ge(cnt_ready, 1)
            cnt = rt[0:TILE, 2].rearrange("p t e -> p (t e)")
            nc.tensor.matmul(bank[0][0:TILE, 0:TILES * EXPERTS], below[0:TILE, 0:TILE], cnt, start=True, stop=True)
            nc.tensor.matmul(bank[0][0:P, 256:256 + TILES * EXPERTS], ones[0:TILE, :], cnt, start=True, stop=True
                             ).then_inc(rank_ps, 1)
            pe.wait_ge(list_zero, 1)
            zeros = eq[:].rearrange("p h c -> p (h c)")
            nc.tensor.matmul(bank[1][:, 0:3 * SLOTS], zeros[:, 0:P], zeros[:, 0:3 * SLOTS], start=True, stop=False,
                             skip_group_check=True)
            with pe.Fori(0, CHUNKS) as c:
                pe.wait_ge(oh_ready, 8 * c + 8)
                for s in range(2):
                    for t in range(CHUNK_TILES):
                        last = nc.tensor.matmul(bank[1][:, 0:3 * SLOTS], ob[0:TILE, s, t],
                                                oa[0:TILE, s * CHUNK_TILES + t].rearrange("p a b -> p (a b)"),
                                                start=False, stop=True, skip_group_check=True)
                last.then_inc(list_step, 1)

            pe.wait_ge(lists_ready, 1)

            def slot_transpose(j, u, r, fresh):
                pe.wait_ge(tok_in[u], 16 * (r + 1))
                if not fresh:
                    pe.wait_ge(xeT_half, 2 * j)
                for k in range(HALVES):
                    last = nc.tensor.transpose(bank[0][:, k * P:(k + 1) * P], tok[:, u, k * P:(k + 1) * P], ident[:])
                last.then_inc(tok_T, 1)

            def slot_up(j, u, e, fresh):
                pe.wait_ge(xeT_half, 2 * j + 2)
                pe.wait_ge(w_in[0], (e + 2) // 2 * (16 * W_DMAS))
                pe.wait_ge(w_in[1], (e + 1) // 2 * (16 * W_DMAS))
                par = e % 2
                for c in range(2):
                    if not fresh:
                        pe.wait_ge(hid_b, 2 * (j - 1) + c + 1)
                    for k in range(HALVES):
                        w = wts[:, bass.ds(par, 1), k * HIDDEN + c * 512:k * HIDDEN + (c + 1) * 512]
                        last = nc.tensor.matmul(bank[1 + c][:], xeT[:, u, k], w.rearrange("p a c -> p (a c)"),
                                                start=(k == 0), stop=(k == 1))
                    last.then_inc(hid_ps, 1)

            def slot_hidden_transpose(j, u, fresh):
                for c in range(2):
                    pe.wait_ge(hid_g, 2 * j + c + 1)
                    if not fresh:
                        pe.wait_ge((hidT_a, hidT_v)[c], j)
                    for k in range(4):
                        last = nc.tensor.transpose(bank[3 + c][:, k * P:(k + 1) * P],
                                                   hid[:, u, (4 * c + k) * P:(4 * c + k + 1) * P], ident[:])
                    last.then_inc(hidT_ps, 1)

            def slot_down(j, e, fresh):
                par = e % 2
                if not fresh:
                    pe.wait_ge(y_b, j)
                for k in range(HIDDEN // P):
                    if k % 4 == 0:
                        pe.wait_ge((hidT_a, hidT_v)[k // 4], j + 1)
                    w = wts[:, bass.ds(par, 1), 2048 + k * DIM:2048 + (k + 1) * DIM].rearrange("p a c -> p (a c)")
                    last = nc.tensor.matmul(bank[5][:, 0:DIM], hidT[:, k], w, start=(k == 0), stop=(k == HIDDEN // P - 1))
                last.then_inc(y_ps, 1)

            e0, e1 = experts_of(PE, 0, 2)
            slot_transpose(0, 0, 0, True)
            slot_up(0, 0, e0, True)
            slot_transpose(1, 1, 0, False)

            def slot_step(j, u, tok_u, r, e_here, e_next, fresh=False):
                slot_hidden_transpose(j, u, fresh)
                slot_up(j + 1, 1 - u, e_next, False)
                slot_transpose(j + 2, tok_u, r, False)
                slot_down(j, e_here, fresh)

            slot_step(0, 0, 2, 0, e0, e1, True)
            with pe.Fori(0, (SLOTS - 4) // 4) as i:
                e = experts_of(PE, 4 * i + 1, 5)
                for k in range(4):
                    slot_step(4 * i + 1 + k, (k + 1) % 2, (k + 3) % TOKS, i + (k + 3) // TOKS, e[k], e[k + 1])
            j = SLOTS - 3
            e0, e1, e2 = experts_of(PE, j, 3)
            slot_step(j, 1, TOKS - 1, SLOTS // TOKS - 1, e0, e1)
            slot_hidden_transpose(j + 1, 0, False)
            slot_up(j + 2, 1, e2, False)
            slot_down(j + 1, e1, False)
            slot_hidden_transpose(j + 2, 1, False)
            slot_down(j + 2, e2, False)

        @block.scalar
        def _(act):
            loads = [
                (w_natural[:, 0:2], a["L0_mix_Wq"].rearrange("(r p) c -> p r c", p=P)),
                (w_natural[:, 2:6], a["L0_mix_Wkv"].rearrange("(r p) c -> p r c", p=P)),
                (w_natural[:, 6:8], a["L0_mix_Wproj"].rearrange("(r p) c -> p r c", p=P)),
                (w_edge[:], a["L0_gnn_W_edge"]),
                (b_edge[:], a["L0_gnn_b_edge"].partition_broadcast(P)),
                (eps1[:], a["L0_gnn_eps"].partition_broadcast(P)),
                (w1[:], a["L0_gnn_W1"].rearrange("(k p) c -> p k c", p=P)),
                (w2[:], a["L0_gnn_W2"].rearrange("(k p) c -> p k c", p=P)),
                (wr[:], a["L0_ffn_Wr"].rearrange("(k p) e -> p k e", p=P)),
                (br[:], a["L0_ffn_br"].partition_broadcast(P)),
            ]
            for n, name in enumerate(("L0_gnn_b1", "L0_gnn_b2", "L0_gnn_gamma", "L0_gnn_beta", "L0_mix_bproj")):
                loads.append((cvec[:, n], a[name].rearrange("(h p) -> p h", p=P)))
            for t, name in ((ln_g, "L0_ffn_ln_g"), (ln_b, "L0_ffn_ln_b")):
                for h in range(HALVES):
                    loads.append((t[:, :, h], a[name][:, h * P:(h + 1) * P].rearrange("e p -> p e")))
            assert len(loads) == CONST_DMAS
            with nc.allow_non_contiguous_dma(reason="small columns of constants"):
                for s, d in loads:
                    act.dma_start(s, d).then_inc(consts_in, 16)
            act.wait_ge(var_ready, 1)
            nc.scalar.activation(ln[0:TILE, 3], ln[0:TILE, 2], ACT.Sqrt).then_inc(sd_ready, 1)
            act.wait_ge(tables_ready, 1)
            for g in range(2):
                nc.scalar.copy(idx_cur[:, g], srcT[:, g]).then_inc(idx_ready, 1)
            act.wait_ge(ln_ready, 1)
            with act.Fori(0, CHUNKS) as c:
                for k in range(CHUNK_TILES):
                    t = c * CHUNK_TILES + k
                    row = xs[0:TILE, bass.ds(t, 1)].rearrange("p a d -> p (a d)")
                    nc.scalar.activation(row, row, ACT.Identity, bias=ln[0:TILE, 5, bass.ds(t, 1)],
                                         scale=ln[0:TILE, 4, bass.ds(t, 1)]).then_inc(xn_ready, 1)
            act.wait_ge(wT_ready, 1)
            nc.scalar.copy(wqT[:], bank[0][:].rearrange("p (k c) -> p k c", k=2)).then_inc(wT_copied, 1)
            for k in range(2):
                nc.scalar.copy(wkvT[:, k], bank[1 + k][:]).then_inc(wT_copied, 1)
            nc.scalar.copy(wpT[:], bank[3][:].rearrange("p (k c) -> p k c", k=2)).then_inc(wT_copied, 1)
            act.wait_ge(xn_ready, TILES)
            nc.scalar.preload_act_table(ACT.Exp)

            def mix_in(t):
                act.wait_ge(mx_T, t)
                nc.scalar.copy(xn_t[0:TILE], xs[0:TILE, bass.ds(t, 1)].rearrange("p a d -> p (a d)")).then_inc(mx_in, 1)

            def mix_xT(t):
                act.wait_ge(mx_T, t + 1)
                act.wait_ge(mx_q, t)
                nc.scalar.copy(xT_t[:], bank[7][:, 0:HALVES * TILE].rearrange("p (h c) -> p h c", h=HALVES)
                               ).then_inc(mx_xT, 1)

            def mix_exp(t):
                act.wait_ge(mx_kv, t + 1)
                act.wait_ge(mx_k, t)
                act.wait_ge(mx_ctx, t)
                nc.scalar.activation(ek[0:TILE], bank[6][0:TILE, 0:DIM], ACT.Exp).then_inc(mx_ek, 1)
                nc.scalar.copy(v_t[0:TILE], bank[6][0:TILE, DIM:2 * DIM]).then_inc(mx_v, 1)
                act.wait_ge(mx_q, t + 1)
                act.wait_ge(mx_qT, t)
                nc.scalar.activation(eq[:], bank[7][:, 0:HALVES * TILE].rearrange("p (h c) -> p h c", h=HALVES),
                                     ACT.Exp).then_inc(mx_eq, 1)

            def attn_bias(c):
                for o in range(HALVES):
                    act.wait_ge(ao_ps, 2 * c + o + 1)
                    nc.scalar.activation(qT[:, o, bass.ds(c * COLS, COLS)], bank[6 + o][:, 0:COLS], ACT.Identity,
                                         bias=cvec[:, BPROJ, o:o + 1]).then_inc(ao_ready, 1)

            def edge_pass(n0, r0, phases, fresh):
                if not fresh:
                    for u in range(2):
                        for q in range(PAIRS):
                            act.wait_ge(xg_in[u][q], 32 * r0)
                        nc.scalar.copy(idx_cur[:, u], srcT[:, u]).then_inc(idx_ready, 1)
                copy_edges(act, n0, 0)
                copy_edges(act, n0 + 1, 1)
                relu_messages(act, 0, n0, r0, 0, True)

                def body(i, riders):
                    n = n0 + 2 * i
                    copy_edges(act, n + 2, 0)
                    if riders and riders[0]:
                        riders[0](i)
                    relu_messages(act, 2 * i + 1, n + 1, r0 + i, 1, True)
                    if riders and riders[1]:
                        riders[1](i)
                    copy_edges(act, n + 3, 1)
                    relu_messages(act, 2 * i + 2, n + 2, r0 + i + 1, 0, i_more)
                    if riders and riders[2]:
                        riders[2](i)

                for lo, hi, riders, between in phases:
                    i_more = True
                    if hi == BODIES:
                        with act.Fori(lo, hi - 1) as i:
                            body(i, riders)
                        i_more = False
                        body(hi - 1, riders)
                    else:
                        with act.Fori(lo, hi) as i:
                            body(i, riders)
                    if between:
                        between()
                relu_messages(act, GROUPS - 1, n0 + GROUPS - 1, r0 + BODIES, 1, False)

            def mix_middle(t):
                mix_xT(t)
                mix_exp(t)

            def copy_attn_w():
                act.wait_ge(aw_ps, 1)
                nc.scalar.copy(attn_w[:], bank[6][:].rearrange("p (h c) -> p h c", h=2)).then_inc(aw_ready, 1)

            edge_pass(0, 0, [(0, TILES, (mix_in, mix_middle, None), copy_attn_w),
                             (TILES, BODIES, (None, None, lambda i: attn_bias(i - TILES)), None)], True)
            again = act.value_load(miss_i[0:1, 0:1], min_val=0, max_val=1)
            with act.If(again > 0):
                with act.Fori(0, WINDOWS) as w:
                    edge_pass((w + 1) * GROUPS, (w + 1) * (GROUPS // 2), [(0, BODIES, None, None)], False)
            with act.Else():
                act.nop()

            def mlp1(c, u, fresh):
                for o in range(HALVES):
                    act.wait_ge(z1_ps, 2 * c + o + 1)
                    if not fresh:
                        act.wait_ge(z2_ps, 2 * (c - 1))
                    nc.scalar.activation(z1[:, u, o], bank[o][:, 0:COLS], ACT.Relu, bias=cvec[:, B1, o:o + 1]
                                         ).then_inc(z1_ready, 1)

            def mlp2(c, u):
                for o in range(HALVES):
                    act.wait_ge(z2_ps, 2 * c + o + 1)
                    nc.scalar.activation(hT[:, o, bass.ds(c * COLS, COLS)], bank[2 + o][:, 0:COLS], ACT.Identity,
                                         bias=cvec[:, B2, o:o + 1]).then_inc(z2_ready, 1)

            mlp1(0, 0, True)
            mlp1(1, 1, True)
            mlp2(0, 0)
            with act.Fori(0, (COL_CHUNKS - 3) // 2) as i:
                mlp1(2 * i + 2, 0, False)
                mlp2(2 * i + 1, 1)
                mlp1(2 * i + 3, 1, False)
                mlp2(2 * i + 2, 0)
            mlp1(COL_CHUNKS - 1, 0, False)
            mlp2(COL_CHUNKS - 2, 1)
            mlp2(COL_CHUNKS - 1, 0)
            act.wait_ge(bn_var, 1)
            nc.scalar.activation(bns[:, 1], bns[:, 0], ACT.Sqrt).then_inc(bn_sd, 1)
            act.wait_ge(bn_ready, 1)
            with act.Fori(0, CHUNKS) as c:
                act.wait_ge(y_T, c)
                for o in range(HALVES):
                    nc.scalar.activation(y_cur[:, o], hT[:, o, bass.ds(c * (CHUNK_TILES * TILE), CHUNK_TILES * TILE)],
                                         ACT.Relu, bias=bns[:, 3, o:o + 1], scale=bns[:, 2, o:o + 1]).then_inc(y_relu, 1)
            act.wait_ge(l2_var, 1)
            nc.scalar.activation(ln[0:TILE, 3], ln[0:TILE, 2], ACT.Sqrt).then_inc(l2_sd, 1)
            act.wait_ge(l2_var2, 1)
            nc.scalar.activation(ln[0:TILE, 7], ln[0:TILE, 6], ACT.Sqrt).then_inc(l2_sd2, 1)
            act.wait_ge(l2_ready, 1)
            with act.Fori(0, CHUNKS) as c:
                act.wait_ge(tk_stored, 32 * c)
                act.wait_ge(tk_T, c)
                for k in range(CHUNK_TILES):
                    t = c * CHUNK_TILES + k
                    last = nc.scalar.activation(xn_cur[0:TILE, k], xs[0:TILE, bass.ds(t, 1)].rearrange("p a d -> p (a d)"),
                                                ACT.Identity, bias=ln[0:TILE, 5, bass.ds(t, 1)],
                                                scale=ln[0:TILE, 4, bass.ds(t, 1)])
                last.then_inc(tk_ready, 1)
                act.wait_ge(tk_T, c + 1)
                act.wait_ge(tk_lg, c)
                flat = xnT.rearrange("p t h c -> p (t h) c")
                for b, m in enumerate((4, 4, 2)):
                    nc.scalar.copy(flat[:, 4 * b:4 * b + m], bank[4 + b][:, 0:m * TILE].rearrange("p (m c) -> p m c", m=m)
                                   ).then_inc(tk_xT, 1)
            act.wait_ge(gate_in, 1)
            nc.scalar.activation(rs[0:TILE, 3], rs[0:TILE, 2], ACT.Exp).then_inc(gate_exp, 1)

            act.wait_ge(lists_ready, 1)

            def slot_gelu(j, u):
                for c in range(2):
                    s = hid[:, u, c * 512:(c + 1) * 512]
                    act.wait_ge(hid_b, 2 * j + c + 1)
                    nc.scalar.activation(s, s, ACT.Gelu).then_inc(hid_g, 1)

            def slot_copy(j, fresh):
                act.wait_ge(hidT_ps, 2 * j + 1)
                if not fresh:
                    act.wait_ge(y_ps, j)
                nc.scalar.copy(hidT[:, 0:4], bank[3][:].rearrange("p (k c) -> p k c", k=4)).then_inc(hidT_a, 1)

            def slot_weigh(j, u, fresh):
                act.wait_ge(y_b, j + 1)
                nc.scalar.activation(ys[:, u], ys[:, u], ACT.Identity, scale=slot_f[:, 1, bass.ds(j, 1)]).then_inc(y_w, 1)

            def slot_step(j, u, fresh=False):
                slot_copy(j, fresh)
                slot_gelu(j + 1, 1 - u)
                slot_weigh(j, u, fresh)

            slot_gelu(0, 0)
            slot_step(0, 0, True)
            with act.Fori(0, (SLOTS - 2) // 2) as i:
                slot_step(2 * i + 1, 1)
                slot_step(2 * i + 2, 0)
            slot_copy(SLOTS - 1, False)
            slot_weigh(SLOTS - 1, 1, False)

        @block.vector
        def _(dve):
            step = Chain(dve, dve_chain)

            def moments_to_ln(chain):
                s = st[0:TILE].rearrange("p t s -> p s t")
                L = ln[0:TILE]
                chain(nc.vector.tensor_tensor(L[:, 0], s[:, 1], s[:, 4], ALU.subtract))
                chain(nc.vector.tensor_tensor(L[:, 1], s[:, 1], s[:, 4], ALU.add))
                chain(nc.vector.tensor_tensor(L[:, 0], L[:, 0], L[:, 0], ALU.mult))
                chain(nc.vector.tensor_tensor(L[:, 2], s[:, 2], s[:, 5], ALU.add))
                chain(nc.vector.scalar_tensor_tensor(out=L[:, 2], in0=L[:, 2], scalar=4.0 / DIM, in1=L[:, 0],
                                                     op0=ALU.mult, op1=ALU.add))
                chain(nc.vector.tensor_scalar(L[:, 2], L[:, 2], 0.25, LN_EPS, ALU.mult, ALU.add))

            nc.vector.memset(dst_i, FAR).then_inc(ids_memset, 1)
            nc.vector.memset(src_i, 0).then_inc(ids_memset, 1)
            dve.wait_ge(consts_made, 7)
            step(nc.vector.tensor_copy(iota_f[:], iota_i[:]))
            step(nc.vector.tensor_copy(part_f[:], part_i[:]))
            step(nc.vector.tensor_copy(tokid[:], tokid_i[:]))
            for c in range(CHUNKS):
                dve.wait_ge(x_in[c], 32)
                for t in range(c * CHUNK_TILES, (c + 1) * CHUNK_TILES):
                    last = nc.vector.bn_stats(st[0:TILE, t], xs[0:TILE, t])
            step(last)
            moments_to_ln(step)
            nc.vector.tensor_copy(ln[0:TILE, 6], ln[0:TILE, 2]).then_inc(var_ready, 1)

            dve.wait_ge(ids_in, 64)
            step(nc.vector.tensor_copy(dst_f, dst_i))
            step(nc.vector.tensor_reduce(gstat[:, 0:1], dst_f, AX.X, ALU.min))
            step(nc.vector.tensor_scalar(gstat[:, 0:1], gstat[:, 0:1], 0.0, float(NODES - 1), ALU.max, ALU.min))
            step(nc.vector.tensor_scalar(rel, dst_f, gstat[:, 0:1], None, ALU.subtract))
            step(nc.vector.scalar_tensor_tensor(out=src_f, in0=dst_f, scalar=float(FAR), in1=rel,
                                                op0=ALU.is_lt, op1=ALU.mult))
            step(nc.vector.tensor_reduce(gstat[:, 1:2], src_f, AX.X, ALU.max))
            step(nc.vector.tensor_copy(src_f, src_i))
            nc.vector.memset(gstat[:, 2:3], 0.0).then_inc(rel_ready, 1)

            dve.wait_ge(sd_ready, 1)
            step(nc.vector.reciprocal(ln[0:TILE, 4], ln[0:TILE, 3]))
            nc.vector.scalar_tensor_tensor(out=ln[0:TILE, 5], in0=ln[0:TILE, 1], scalar=-0.5, in1=ln[0:TILE, 4],
                                           op0=ALU.mult, op1=ALU.mult).then_inc(ln_ready, 1)
            dve.wait_ge(ids_T, 1)
            nc.vector.tensor_copy(srcT[:], bank[5][:, 0:GT * GROUPS].rearrange("p (j g) -> p g j", j=GT)
                                  ).then_inc(tables_ready, 1)
            step(nc.vector.tensor_copy(relT[:], bank[4][:, 0:GT * GROUPS].rearrange("p (j g) -> p g j", j=GT)))
            step(nc.vector.tensor_copy(base_row[:, 0:GROUPS], bank[6][0:1, 0:GROUPS]))
            step(nc.vector.tensor_reduce(gstat[0:1, 3:4], bank[6][0:1, P:P + GROUPS], AX.X, ALU.max))
            nc.vector.tensor_scalar(miss_i[:], gstat[0:1, 3:4], float(WINDOW), None, ALU.is_ge).then_inc(tables_ready, 1)
            nc.vector.memset(gstat[:, 2:3], 0.0).then_inc(tables_ready, 1)
            dve.wait_ge(tables_ready, 3)
            dve.wait_ge(consts_in, CONST_DMAS * 16)
            step(nc.vector.tensor_scalar(eps1[:], eps1[:], 1.0, None, ALU.add))
            for c in range(CHUNKS):
                dve.wait_ge(xn_ready, CHUNK_TILES * (c + 1))
                if c >= 2:
                    dve.wait_ge(rows_stored[c % 2], 32 * (c // 2))
                nc.vector.tensor_tensor(table_stage[0:TILE, c % 2], xs[0:TILE, c * CHUNK_TILES:(c + 1) * CHUNK_TILES],
                                        b_edge[0:TILE].unsqueeze(1).to_broadcast([TILE, CHUNK_TILES, DIM]), ALU.add
                                        ).then_inc(rows_ready, 1)
            dve.wait_ge(wT_ready, 1)

            def mix_h(t, h_count):
                dve.wait_ge(mx_xT, t + 1)
                dve.wait_ge(h_updates, h_count)
                w = hT[:, :, bass.ds(t * TILE, TILE)]
                nc.vector.scalar_tensor_tensor(out=w, in0=bank[7][:, 0:HALVES * TILE].rearrange("p (h c) -> p h c", h=HALVES),
                                               scalar=eps1[:], in1=w, op0=ALU.mult, op1=ALU.add).then_inc(h_updates, 1)

            def mix_elu(t):
                dve.wait_ge(mx_v, t + 1)
                dve.wait_ge(mx_ctx, t)
                dve.wait_ge(mx_kacc, t + 1)
                nc.vector.tensor_scalar(k_t[0:TILE], bank[6][0:TILE, 0:DIM], 0.0, None, ALU.max).then_inc(mx_rk, 1)
                dve.wait_ge(mx_rk, t + 1)
                nc.vector.scalar_tensor_tensor(out=k_t[0:TILE], in0=ek[0:TILE], scalar=1.0, in1=k_t[0:TILE],
                                               op0=ALU.min, op1=ALU.add).then_inc(mx_k, 1)
                dve.wait_ge(mx_kacc, t + 1)
                dve.wait_ge(mx_k, t + 1)
                nc.vector.tensor_tensor(k_acc[0:TILE], k_acc[0:TILE], k_t[0:TILE], ALU.add).then_inc(mx_kacc, 1)
                dve.wait_ge(mx_eq, t + 1)
                dve.wait_ge(mx_qT, t)
                nc.vector.tensor_scalar(rq[:], bank[7][:, 0:HALVES * TILE].rearrange("p (h c) -> p h c", h=HALVES),
                                        0.0, None, ALU.max).then_inc(mx_rq, 1)
                dve.wait_ge(mx_rq, t + 1)
                nc.vector.scalar_tensor_tensor(out=qT[:, :, bass.ds(t * TILE, TILE)], in0=eq[:], scalar=1.0, in1=rq[:],
                                               op0=ALU.min, op1=ALU.add).then_inc(mx_qT, 1)

            def mix_context(t):
                dve.wait_ge(mx_ctx, t + 1)
                dve.wait_ge(mx_acc, t + 1)
                nc.vector.tensor_tensor(ctx_acc[:], ctx_acc[:], bank[7][:, 0:2 * P], ALU.add).then_inc(mx_acc, 1)

            def mask_context():
                dve.wait_ge(mx_acc, TILES + 1)
                dve.wait_ge(ksum_ps, 1)
                for h in range(HALVES):
                    nc.vector.tensor_tensor(ctx_m[:, h], ctx_acc[:, h * P:(h + 1) * P], blocks[:], ALU.mult
                                            ).then_inc(ctx_masked, 1)
                    nc.vector.tensor_scalar(ksum_m[:, h], blocks[:], bank[7][:, h:h + 1], None, ALU.mult
                                            ).then_inc(ctx_masked, 1)

            def attn_norm(c):
                dve.wait_ge(den_ps, c + 1)
                for h in range(HALVES):
                    nc.vector.tensor_scalar(dinv[:, h], bank[6 + h][:, 0:COLS], 1e-6, None, ALU.max).then_inc(den_max, 1)
                dve.wait_ge(den_max, 2 * c + 2)
                nc.vector.reciprocal(dinv[:], dinv[:]).then_inc(den_inv, 1)
                dve.wait_ge(den_inv, c + 1)
                dve.wait_ge(ao_ps, 2 * c)
                nc.vector.tensor_tensor(qn, dinv, qT[:, :, bass.ds(c * COLS, COLS)], ALU.mult).then_inc(qn_ready, 1)

            def edge_pass(n0, r0, start_of, h_of, phases):
                mark_window(dve, 0, 0)
                add_nodes(dve, n0, r0, 0)

                def body(i, riders, per_body, h0, lo):
                    n = n0 + 2 * i
                    h = h0 + (i - lo) * per_body
                    add_nodes(dve, n + 1, r0 + i, 1)
                    mark_window(dve, 2 * i + 1, 1)
                    s0 = start_of(2 * i)
                    add_window(dve, n, 0, s0, h)
                    dve.wait_ge(h_updates, h + 1)
                    dve.sem_inc(agg_read, 1)
                    h = h + 1
                    if riders:
                        if riders[0]:
                            riders[0](i, h)
                            h = h + 1
                    add_nodes(dve, n + 2, r0 + i + 1, 0)
                    if riders:
                        riders[1](i)
                    mark_window(dve, 2 * i + 2, 0)
                    s1 = start_of(2 * i + 1)
                    add_window(dve, n + 1, 1, s1, h)
                    dve.wait_ge(h_updates, h + 1)
                    dve.sem_inc(agg_read, 1)
                    if riders and riders[2]:
                        riders[2](i)

                h0 = h_of
                for lo, hi, riders, between in phases:
                    per_body = 3 if riders and riders[0] else 2
                    with dve.Fori(lo, hi) as i:
                        body(i, riders, per_body, h0, lo)
                    h0 = h0 + (hi - lo) * per_body
                    if between:
                        between()
                n = n0 + GROUPS
                mark_window(dve, GROUPS - 1, 1)
                add_nodes(dve, n - 1, r0 + BODIES, 1)
                for k in range(2):
                    add_window(dve, n - 2 + k, k, start_of(GROUPS - 2 + k), h0 + k)
                    dve.wait_ge(h_updates, h0 + k + 1)
                    dve.sem_inc(agg_read, 1)
                return h0 + 2

            def own_window(g):
                return dve.value_load(base_row[0:1, bass.ds(g, 1)], min_val=0, max_val=NODES - 1)

            dve.sem_inc(agg_read, 1)
            dve.wait_ge(h_updates, 1)
            h_end = edge_pass(0, 0, own_window, 1, [
                (0, TILES, (mix_h, mix_elu, mix_context), mask_context),
                (TILES, BODIES, (None, lambda i: attn_norm(i - TILES), None), None)])
            again = dve.value_load(miss_i[0:1, 0:1], min_val=0, max_val=1)
            with dve.If(again > 0):
                nc.vector.tensor_scalar(rel, rel, float(WINDOW), None, ALU.is_ge).then_inc(pass_tables, 1)
                dve.wait_ge(pass_tables, 1)
                nc.vector.scalar_tensor_tensor(out=rel, in0=dst_f, scalar=float(4 * FAR), in1=rel,
                                               op0=ALU.add, op1=ALU.mult).then_inc(pass_tables, 1)
                dve.wait_ge(pass_tables, 2)
                nc.vector.tensor_scalar(rel, rel, float(4 * FAR), None, ALU.subtract).then_inc(pass_tables, 1)
                dve.wait_ge(pass_tables, 3)
                dve.wait_ge(pass_T, 1)
                nc.vector.tensor_copy(relT[:], bank[4][:, 0:GT * GROUPS].rearrange("p (j g) -> p g j", j=GT)
                                      ).then_inc(pass_done, 1)
                with dve.Fori(0, WINDOWS) as w:
                    dve.wait_ge(pass_done, w + 1)
                    h1 = h_end + w * GROUPS
                    edge_pass((w + 1) * GROUPS, (w + 1) * (GROUPS // 2), lambda g: w * WINDOW, h1, [(0, BODIES, None, None)])
                    nc.vector.tensor_scalar(relT[:], relT[:], float(WINDOW), None, ALU.subtract).then_inc(pass_done, 1)
            with dve.Else():
                dve.nop()
            nc.vector.memset(eq[:], 0.0).then_inc(edges_done, 1)
            nc.vector.memset(ek[:], 0.0).then_inc(edges_done, 1)

            for c in range(COL_CHUNKS):
                dve.wait_ge(z2_ready, 2 * c + 2)
                for o in range(HALVES):
                    last = nc.vector.bn_stats(bn[:, o, c], hT[:, o, c * COLS:min((c + 1) * COLS, NODES)])
            step(last)
            for o in range(HALVES):
                last = nc.vector.bn_aggr(mv[:, o], bn[:, o])
            step(last)
            nc.vector.tensor_scalar(bns[:, 0], mv[:, :, 1], LN_EPS, None, ALU.add).then_inc(bn_var, 1)
            dve.wait_ge(bn_sd, 1)
            step(nc.vector.reciprocal(bns[:, 1], bns[:, 1]))
            step(nc.vector.tensor_tensor(bns[:, 2], bns[:, 1], cvec[:, GAMMA], ALU.mult))
            step(nc.vector.tensor_tensor(bns[:, 0], bns[:, 2], mv[:, :, 0], ALU.mult))
            nc.vector.tensor_tensor(bns[:, 3], cvec[:, BETA], bns[:, 0], ALU.subtract).then_inc(bn_ready, 1)
            dve.wait_ge(x_again, 32 * CHUNKS)
            with dve.Fori(0, CHUNKS) as c:
                dve.wait_ge(y_relu, 2 * c + 2)
                nc.vector.tensor_tensor(y_cur, y_cur, qT[:, :, bass.ds(c * (CHUNK_TILES * TILE), CHUNK_TILES * TILE)],
                                        ALU.add).then_inc(y_sum, 1)
                dve.wait_ge(y_T, c + 1)
                for b, m in enumerate((2, 2, 1)):
                    rows = xs[0:TILE, bass.ds(c * CHUNK_TILES + 2 * b, m)]
                    nc.vector.tensor_tensor(rows, bank[b][0:TILE, 0:m * DIM].rearrange("p (m d) -> p m d", m=m), rows,
                                            ALU.add).then_inc(x1_ready, 1)
                dve.wait_ge(x1_ready, 3 * c + 3)
                for k in range(CHUNK_TILES):
                    t = c * CHUNK_TILES + k
                    last = nc.vector.bn_stats(st[0:TILE, bass.ds(t, 1)].rearrange("p a s -> p (a s)"),
                                              xs[0:TILE, bass.ds(t, 1)].rearrange("p a d -> p (a d)"))
                last.then_inc(x1_stats, 1)
            dve.wait_ge(x1_stats, CHUNKS)
            L = ln[0:TILE]
            moments_to_ln(step)
            nc.vector.tensor_copy(L[:, 6], L[:, 2]).then_inc(l2_var, 1)
            dve.wait_ge(l2_sd, 1)
            step(nc.vector.reciprocal(L[:, 4], L[:, 3]))
            step(nc.vector.scalar_tensor_tensor(out=L[:, 6], in0=L[:, 2], scalar=LN_EPS, in1=L[:, 4],
                                                op0=ALU.subtract, op1=ALU.mult))
            step(nc.vector.tensor_tensor(L[:, 6], L[:, 6], L[:, 4], ALU.mult))
            nc.vector.tensor_scalar(L[:, 6], L[:, 6], LN_EPS, None, ALU.add).then_inc(l2_var2, 1)
            dve.wait_ge(l2_sd2, 1)
            step(nc.vector.reciprocal(L[:, 0], L[:, 7]))
            step(nc.vector.tensor_tensor(L[:, 4], L[:, 4], L[:, 0], ALU.mult))
            nc.vector.scalar_tensor_tensor(out=L[:, 5], in0=L[:, 1], scalar=-0.5, in1=L[:, 4],
                                           op0=ALU.mult, op1=ALU.mult).then_inc(l2_ready, 1)
            with dve.Fori(0, CHUNKS) as c:
                dve.wait_ge(tk_lg, c + 1)
                back = L[:, 7, bass.ds(c * CHUNK_TILES, CHUNK_TILES)].unsqueeze(2).to_broadcast([TILE, CHUNK_TILES, EXPERTS])
                nc.vector.tensor_tensor(logits[0:TILE, bass.ds(c * CHUNK_TILES, CHUNK_TILES)],
                                        bank[7][0:TILE, 0:CHUNK_TILES * EXPERTS].rearrange("p (t e) -> p t e", e=EXPERTS),
                                        back, ALU.mult).then_inc(tk_scaled, 1)
            dve.wait_ge(tk_scaled, CHUNKS)

            shape = [TILE, TILES, EXPERTS]
            R, S, lg = rt[0:TILE], rs[0:TILE], logits[0:TILE]
            by_t = lambda v: v.unsqueeze(2).to_broadcast(shape)
            by_e = lambda v: v.unsqueeze(1).to_broadcast(shape)
            step(nc.vector.tensor_tensor(lg, lg, by_e(br[0:TILE]), ALU.add))
            step(nc.vector.tensor_scalar(ex[:, 0], iota_f[:, 0:EXPERTS], -1.0, float(EXPERTS), ALU.mult, ALU.add))
            for s, src in ((0, lg), (1, R[:, 3])):
                if s == 1:
                    step(nc.vector.scalar_tensor_tensor(out=R[:, 3], in0=R[:, 0], scalar=-1e30, in1=lg,
                                                        op0=ALU.mult, op1=ALU.add))
                step(nc.vector.tensor_reduce(S[:, s], src, AX.X, ALU.max))
                step(nc.vector.tensor_tensor(R[:, 4], src, by_t(S[:, s]), ALU.is_equal))
                step(nc.vector.tensor_tensor(R[:, 4], R[:, 4], by_e(ex[0:TILE, 0]), ALU.mult))
                step(nc.vector.tensor_reduce(S[:, 6], R[:, 4], AX.X, ALU.max))
                step(nc.vector.tensor_tensor(R[:, s], R[:, 4], by_t(S[:, 6]), ALU.is_equal))
            nc.vector.tensor_tensor(R[:, 2], R[:, 0], R[:, 1], ALU.add).then_inc(cnt_ready, 1)
            nc.vector.tensor_tensor(S[:, 2], S[:, 1], S[:, 0], ALU.subtract).then_inc(gate_in, 1)
            dve.wait_ge(gate_exp, 1)
            step(nc.vector.tensor_scalar(S[:, 4], S[:, 3], 1.0, None, ALU.add))
            step(nc.vector.reciprocal(S[:, 4], S[:, 4]))
            step(nc.vector.tensor_tensor(S[:, 5], S[:, 3], S[:, 4], ALU.mult))
            dve.wait_ge(rank_ps, 1)
            total = bank[0][0:TILE, 256:256 + TILES * EXPERTS].rearrange("p (t e) -> p t e", e=EXPERTS)
            rank = bank[0][0:TILE, 0:TILES * EXPERTS].rearrange("p (t e) -> p t e", e=EXPERTS)
            for e in range(EXPERTS):
                last = nc.vector.tensor_tensor_scan(R[:, 5, :, e], ones[0:TILE, 0:TILES], total[:, :, e], 0.0,
                                                    ALU.mult, ALU.add)
            step(last)
            X = ex[0:TILE]
            step(nc.vector.tensor_scalar(X[:, 2], R[:, 5, TILES - 1], float(P - 1), None, ALU.add))
            step(nc.vector.tensor_copy(exi[0:TILE], X[:, 2]))
            step(nc.vector.tensor_scalar(exi[0:TILE], exi[0:TILE], 7, None, ALU.logical_shift_right))
            step(nc.vector.tensor_copy(X[:, 3], exi[0:TILE]))
            step(nc.vector.tensor_tensor_scan(X[:, 4], ones[0:TILE, 0:EXPERTS], X[:, 3], 0.0, ALU.mult, ALU.add))
            step(nc.vector.tensor_tensor(X[:, 5], X[:, 4], X[:, 3], ALU.subtract))
            step(nc.vector.tensor_scalar(X[:, 2], X[:, 5], float(P), None, ALU.mult))
            step(nc.vector.tensor_tensor(R[:, 5], R[:, 5], total, ALU.subtract))
            step(nc.vector.tensor_tensor(R[:, 5], R[:, 5], rank, ALU.add))
            step(nc.vector.tensor_tensor(R[:, 5], R[:, 5], by_e(X[:, 2]), ALU.add))
            for s in range(2):
                step(nc.vector.tensor_tensor(R[:, 4], R[:, s], R[:, 5], ALU.mult))
                step(nc.vector.tensor_reduce(S[:, 6], R[:, 4], AX.X, ALU.add))
                step(nc.vector.tensor_copy(rsi[0:TILE, 0], S[:, 6]))
                step(nc.vector.tensor_scalar(rsi[0:TILE, 1], rsi[0:TILE, 0], 7, None, ALU.logical_shift_right))
                step(nc.vector.tensor_copy(S[:, 8 if s == 0 else 1], rsi[0:TILE, 1]))
                step(nc.vector.tensor_scalar(rsi[0:TILE, 1], rsi[0:TILE, 0], P - 1, None, ALU.bitwise_and))
                step(nc.vector.tensor_copy(S[:, 9 if s == 0 else 2], rsi[0:TILE, 1]))
            nc.vector.memset(ej[:], 0.0).then_inc(list_zero, 1)
            with dve.Fori(0, CHUNKS) as c:
                dve.wait_ge(list_step, c)
                ts_ = bass.ds(c * CHUNK_TILES, CHUNK_TILES)
                for s, (hi, lo, wt) in enumerate(((8, 9, 4), (1, 2, 5))):
                    o = oa[0:TILE, s * CHUNK_TILES:(s + 1) * CHUNK_TILES]
                    narrow = [TILE, CHUNK_TILES, SLOTS]
                    nc.vector.tensor_tensor(ob[0:TILE, s], iota_f[0:TILE].unsqueeze(1).to_broadcast([TILE, CHUNK_TILES, P]),
                                            S[:, lo, ts_].unsqueeze(2).to_broadcast([TILE, CHUNK_TILES, P]), ALU.is_equal
                                            ).then_inc(oh_ready, 1)
                    nc.vector.tensor_tensor(o[:, :, 2], iota_f[0:TILE, 0:SLOTS].unsqueeze(1).to_broadcast(narrow),
                                            S[:, hi, ts_].unsqueeze(2).to_broadcast(narrow), ALU.is_equal).then_inc(oh_ready, 1)
                    dve.wait_ge(oh_ready, 8 * c + 4 * s + 2)
                    nc.vector.tensor_tensor(o[:, :, 0], o[:, :, 2], tokid[0:TILE, ts_].unsqueeze(2).to_broadcast(narrow),
                                            ALU.mult).then_inc(oh_ready, 1)
                    nc.vector.tensor_tensor(o[:, :, 1], o[:, :, 2], S[:, wt, ts_].unsqueeze(2).to_broadcast(narrow),
                                            ALU.mult).then_inc(oh_ready, 1)
            for e in range(1, EXPERTS):
                step(nc.vector.scalar_tensor_tensor(out=ej[0:1, 0], in0=iota_f[0:1, 0:SLOTS], scalar=ex[0:1, 5, e:e + 1],
                                                    in1=ej[0:1, 0], op0=ALU.is_ge, op1=ALU.add))
            step(nc.vector.tensor_copy(ej_i[:, 3:3 + SLOTS], ej[0:1, 0]))
            step(nc.vector.tensor_copy(first_i[:], ex[0:1, 5]))
            dve.wait_ge(list_step, CHUNKS)
            step(nc.vector.tensor_copy(slot_f[:], bank[1][:, 0:3 * SLOTS].rearrange("p (a s) -> p a s", a=3)))
            step(nc.vector.tensor_copy(tok_i[:], slot_f[:, 0]))
            step(nc.vector.tensor_scalar(slot_f[:, 2], slot_f[:, 2], -1.0, 1.0, ALU.mult, ALU.add))
            step(nc.vector.tensor_scalar(part_f[:], part_f[:], float(NODES), None, ALU.add))
            step(nc.vector.scalar_tensor_tensor(out=slot_f[:, 2], in0=slot_f[:, 2], scalar=part_f[:], in1=slot_f[:, 0],
                                                op0=ALU.mult, op1=ALU.add))
            nc.vector.tensor_copy(row_i[:], slot_f[:, 2]).then_inc(lists_ready, 1)

            def slot_scale(j, u, e, fresh):
                dve.wait_ge(tok_T, j + 1)
                if not fresh:
                    dve.wait_ge(hid_ps, 2 * (j - 1))
                for k in range(HALVES):
                    g = ln_g[:, bass.ds(e, 1), k]
                    b = ln_b[:, bass.ds(e, 1), k]
                    nc.vector.tensor_scalar(xeT[:, u, k], bank[0][:, k * P:(k + 1) * P], g, b, ALU.mult, ALU.add
                                            ).then_inc(xeT_half, 1)

            def slot_bias(j, u, e, fresh):
                for c in range(2):
                    dve.wait_ge(hid_ps, 2 * j + c + 1)
                    if not fresh:
                        dve.wait_ge(hidT_ps, 2 * (j - 1))
                    b1 = wts[:, bass.ds(e % 2, 1), 4096 + c * 512:4096 + (c + 1) * 512].rearrange("p a c -> p (a c)")
                    nc.vector.tensor_tensor(hid[:, u, c * 512:(c + 1) * 512], bank[1 + c][:], b1, ALU.add).then_inc(hid_b, 1)

            def slot_copy(j, fresh):
                dve.wait_ge(hidT_ps, 2 * j + 2)
                if not fresh:
                    dve.wait_ge(y_ps, j)
                nc.vector.tensor_copy(hidT[:, 4:8], bank[4][:].rearrange("p (k c) -> p k c", k=4)).then_inc(hidT_v, 1)

            def slot_out(j, u, e, fresh):
                dve.wait_ge(y_ps, j + 1)
                if not fresh:
                    dve.wait_ge(acc_in, 16 * (j - 1))
                b2 = wts[:, bass.ds(e % 2, 1), 5120:5120 + DIM].rearrange("p a c -> p (a c)")
                nc.vector.tensor_tensor(ys[:, u], bank[5][:, 0:DIM], b2, ALU.add).then_inc(y_b, 1)

            def slot_step(j, u, e0, e1, e2, fresh=False):
                slot_copy(j, fresh)
                slot_bias(j + 1, 1 - u, e1, False)
                slot_scale(j + 2, u, e2, False)
                slot_out(j, u, e0, fresh)

            dve.wait_ge(lists_ready, 1)
            e0, e1, e2 = experts_of(DVE, 0, 3)
            slot_scale(0, 0, e0, True)
            slot_bias(0, 0, e0, True)
            slot_scale(1, 1, e1, True)
            slot_step(0, 0, e0, e1, e2, True)
            with dve.Fori(0, (SLOTS - 4) // 4) as i:
                e = experts_of(DVE, 4 * i + 1, 6)
                for k in range(4):
                    slot_step(4 * i + 1 + k, (k + 1) % 2, e[k], e[k + 1], e[k + 2])
            j = SLOTS - 3
            e0, e1, e2 = experts_of(DVE, j, 3)
            slot_step(j, 1, e0, e1, e2)
            slot_copy(j + 1, False)
            slot_bias(j + 2, 1, e2, False)
            slot_out(j + 1, 0, e1, False)
            slot_copy(j + 2, False)
            slot_out(j + 2, 1, e2, False)


_INS = ['x', 'src', 'dst', 'edge_attr_128', 'L0_gnn_W_edge', 'L0_gnn_b_edge', 'L0_gnn_W1', 'L0_gnn_b1', 'L0_gnn_W2',
        'L0_gnn_b2', 'L0_gnn_eps', 'L0_gnn_gamma', 'L0_gnn_beta', 'L0_mix_Wq', 'L0_mix_Wkv', 'L0_mix_Wproj',
        'L0_mix_bproj', 'L0_ffn_Wr', 'L0_ffn_br', 'L0_ffn_ln_g', 'L0_ffn_ln_b', 'L0_ffn_W1', 'L0_ffn_b1', 'L0_ffn_W2',
        'L0_ffn_b2']


def kernel(**inputs):
    import numpy as _np
    import concourse.bacc as _bacc
    from concourse import mybir as _mybir
    from concourse.bass_utils import run_bass_kernel_spmd as _run

    nc = _bacc.Bacc("TRN2", target_bir_lowering=False, num_devices=1)
    arrays, args = {}, {}
    for name in _INS:
        a = _np.ascontiguousarray(inputs[name])
        arrays[f"in_{name}"] = a
        args[name] = nc.dram_tensor(f"in_{name}", a.shape, _mybir.dt.from_np(a.dtype), kind="ExternalInput").ap()
    out = nc.dram_tensor("out_0", (NODES, DIM), F32, kind="ExternalOutput").ap()
    build(nc, args, out)
    r = _run(nc, [arrays], core_ids=[0])
    return r.results[0]["out_0"]
```

```python
import concourse.bass as bass
from concourse import mybir
from contextlib import ExitStack

F32 = mybir.dt.float32
I32 = mybir.dt.int32
ALU = mybir.AluOpType
ACT = mybir.ActivationFunctionType
AX = mybir.AxisListType
PE = mybir.EngineType.PE
DVE = mybir.EngineType.DVE

P = 128
NODES, DIM = 3125, 256
EDGES, EDGE_DIM = 50000, 128
EXPERTS, HIDDEN = 8, 1024
HEAD_DIM = 32
HALVES = DIM // P
TILE = 125
TILES = NODES // TILE
CHUNK_TILES = 5
CHUNKS = TILES // CHUNK_TILES
GT = 6
GROUP = GT * P
GROUPS = -(-EDGES // GROUP)
TAIL = EDGES - (GROUPS - 1) * GROUP
PAIRS = GT // 2
PIECES = 4
BODIES = (GROUPS - 2) // 2
WINDOW = P
WINDOWS = -(-NODES // WINDOW)
COLS = 448
COL_CHUNKS = -(-NODES // COLS)
NODES_PAD = COLS * COL_CHUNKS
H_COLS = NODES_PAD + WINDOW
SLOTS = (2 * NODES + EXPERTS * (P - 1)) // P
LIST = P // 2
MAIN = SLOTS - 4
TOKS = 4
W_DMAS = 4
CONST_DMAS = 18
L2_STEPS = 10
FAR = 8192
LN_EPS = 1e-5
DMA_ROWS = 112
assert GROUPS % 2 == 0 and SLOTS <= LIST and MAIN % TOKS == 0 and CHUNKS % 2 == 1 and TILES + COL_CHUNKS == BODIES


class Chain:

    def __init__(self, eng, sem, base=0):
        self.eng, self.sem, self.base, self.n = eng, sem, base, 0

    def __call__(self, ins):
        self.n += 1
        ins.then_inc(self.sem, 1)
        self.eng.wait_ge(self.sem, self.base + self.n)


def build(nc, a, out):
    with ExitStack() as ctx:
        def sb(name, shape, dt=F32):
            return ctx.enter_context(nc.sbuf_tensor(name, shape, dt))

        def sem(name):
            return ctx.enter_context(nc.semaphore(name))

        node_table = nc.dram_tensor("node_table", [NODES, DIM], F32).ap()
        token_table = nc.dram_tensor("token_table", [NODES, DIM], F32).ap()
        acc_table = nc.dram_tensor("acc_table", [NODES + P, DIM], F32).ap()

        hT = sb("hT", [P, HALVES, H_COLS])
        qT = sb("qT", [P, HALVES, NODES_PAD])
        xs = sb("xs", [P, TILES, DIM])
        work = sb("work", [P, 10752])
        wts = sb("wts", [P, 2, 5376])

        def view(t, lo, *dims):
            n = 1
            for d in dims:
                n *= d
            v = t[:, lo:lo + n]
            if len(dims) == 2:
                v = v.rearrange("p (a b) -> p a b", b=dims[1])
            if len(dims) == 3:
                v = v.rearrange("p (a b c) -> p a b c", b=dims[1], c=dims[2])
            return v

        ea = view(work, 0, 2, GT, EDGE_DIM)
        xg = view(work, 1536, 2, GT, DIM)
        eaT = view(work, 4608, 2, GT, P)
        msg = view(work, 6144, 2, GT, DIM)
        onehot = view(work, 9216, 2, GT, P)
        table_stage = view(work, 1536, 2, CHUNK_TILES, DIM)
        w_natural = view(work, 6144, 8, DIM)
        z1 = view(work, 0, 2, HALVES, COLS)
        y_cur = view(work, 0, 2, HALVES, CHUNK_TILES * TILE)
        xn_cur = view(work, 2560, 2, CHUNK_TILES, DIM)
        xnT = view(work, 5120, 4 * CHUNK_TILES, TILE).rearrange("p (u t h) c -> p u t h c", u=2, h=HALVES)
        ob = view(work, 6400, 2, 2 * CHUNK_TILES, P)
        oa = view(work, 0, 2, 2 * CHUNK_TILES, P)
        oh = work[:, 8960:8960 + 4 * CHUNK_TILES * LIST].rearrange("p (u s t c) -> p u s t c", u=2, s=2, t=CHUNK_TILES)
        tok = view(work, 0, TOKS, DIM)
        xeT = view(work, 1024, 2, HALVES, P)
        hid = view(work, 1536, 2, HIDDEN)
        hidT = view(work, 3584, HIDDEN // P, P)
        ys = view(work, 4608, 2, DIM)
        early = wts[:, 1, :]
        dst_i = early[0:GROUPS, 0:GROUP].bitcast(I32)
        dst_f = early[0:GROUPS, 768:768 + GROUP]
        rel = early[0:GROUPS, 1536:1536 + GROUP]
        src_i = early[0:GROUPS, 2304:2304 + GROUP].bitcast(I32)
        src_f = early[0:GROUPS, 3072:3072 + GROUP]
        qn = view(early, 2304, HALVES, COLS)
        dinv = view(early, 3200, HALVES, COLS)

        relT = sb("relT", [P, GROUPS, GT])
        srcT = sb("srcT", [P, GROUPS, GT], I32)
        idx_cur = sb("idx_cur", [P, 2, GT], I32)
        base_row = sb("base_row", [1, P], I32)
        miss_i = sb("miss_i", [1, 1], I32)
        gstat = sb("gstat", [GROUPS, 4])
        w_edge = sb("w_edge", [P, DIM])
        w1 = sb("w1", [P, HALVES, DIM])
        w2 = sb("w2", [P, HALVES, DIM])
        wqT = sb("wqT", [P, HALVES, DIM])
        wkvT = sb("wkvT", [P, HALVES, 2 * DIM])
        wpT = sb("wpT", [P, HALVES, DIM])
        wr = sb("wr", [P, HALVES, EXPERTS])
        br = sb("br", [P, EXPERTS])
        b_edge = sb("b_edge", [P, DIM])
        cvec = sb("cvec", [P, 5, HALVES])
        B1, B2, GAMMA, BETA, BPROJ = range(5)
        eps1 = sb("eps1", [P, 1])
        ln_g = sb("ln_g", [P, EXPERTS, HALVES])
        ln_b = sb("ln_b", [P, EXPERTS, HALVES])
        iota_i = sb("iota_i", [P, P], I32)
        iota_f = sb("iota_f", [P, P])
        part_i = sb("part_i", [P, 1], I32)
        part_f = sb("part_f", [P, 1])
        ident = sb("ident", [P, P])
        below = sb("below", [P, P])
        ones = sb("ones", [P, P])
        blocks = sb("blocks", [P, P])
        st = sb("st", [P, TILES, 6])
        ln = sb("ln", [P, 8, TILES])
        xn_t = sb("xn_t", [P, DIM])
        xT_t = sb("xT_t", [P, HALVES, P])
        ek = sb("ek", [P, DIM])
        k_t = sb("k_t", [P, DIM])
        v_t = sb("v_t", [P, DIM])
        eq = sb("eq", [P, HALVES, TILE])
        rq = sb("rq", [P, HALVES, TILE])
        ctx_acc = sb("ctx_acc", [P, 2 * P])
        k_acc = sb("k_acc", [P, DIM])
        ctx_m = sb("ctx_m", [P, HALVES, P])
        ksum_m = sb("ksum_m", [P, HALVES, P])
        attn_w = sb("attn_w", [P, HALVES, DIM])
        bn = sb("bn", [P, HALVES, COL_CHUNKS, 6])
        mv = sb("mv", [P, HALVES, 2])
        bns = sb("bns", [P, 4, HALVES])
        logits = sb("logits", [P, TILES, EXPERTS])
        rt = sb("rt", [P, 6, TILES, EXPERTS])
        rs = sb("rs", [P, 10, TILES])
        rsi = sb("rsi", [P, 2, TILES], I32)
        ex = sb("ex", [P, 6, EXPERTS])
        exi = sb("exi", [P, EXPERTS], I32)
        tokid = sb("tokid", [P, TILES])
        tokid_i = sb("tokid_i", [P, TILES], I32)
        slot_f = sb("slot_f", [P, 3, LIST])
        tok_i = sb("tok_i", [P, LIST], I32)
        row_i = sb("row_i", [P, LIST], I32)
        ej = sb("ej", [P, 2, SLOTS])
        ej_i = sb("ej_i", [1, SLOTS + 8], I32)
        first_i = sb("first_i", [1, EXPERTS], I32)
        more_i = sb("more_i", [1, 1], I32)
        tokc = sb("tokc", [P, TOKS], I32)
        rowc = sb("rowc", [P, 2], I32)

        bank = [ctx.enter_context(nc.psum_tensor(f"bank{i}", [P, 512], F32)) for i in range(8)]

        x_in = [sem(f"x_in{c}") for c in range(CHUNKS)]
        consts_in = sem("consts_in")
        b_edge_in = sem("b_edge_in")
        ids_in = sem("ids_in")
        pool_chain = sem("pool_chain")
        pool_passed = sem("pool_passed")
        consts_made = sem("consts_made")
        dve_chain = sem("dve_chain")
        act_chain = sem("act_chain")
        var_ready = sem("var_ready")
        sd_ready = sem("sd_ready")
        ln_ready = sem("ln_ready")
        xn_ready = sem("xn_ready")
        rows_ready = sem("rows_ready")
        rows_stored = [sem(f"rows_stored{i}") for i in range(2)]
        ids_memset = sem("ids_memset")
        rel_ready = sem("rel_ready")
        base_T = sem("base_T")
        ids_T = sem("ids_T")
        ids_used = sem("ids_used")
        tables_ready = sem("tables_ready")
        wT_ready = sem("wT_ready")
        wT_copied = sem("wT_copied")

        ea_in = [sem(f"ea_in{u}") for u in range(2)]
        ea_tail = sem("ea_tail")
        idx_ready = sem("idx_ready")
        xg_in = [[sem(f"xg_in{u}_{q}") for q in range(PAIRS)] for u in range(2)]
        eaT_ps = sem("eaT_ps")
        eaT_ready = sem("eaT_ready")
        e_ready = sem("e_ready")
        sums_done = sem("sums_done")
        msg_ready = sem("msg_ready")
        onehot_ready = sem("onehot_ready")
        agg_ready = sem("agg_ready")
        h_updates = sem("h_updates")
        agg_read = sem("agg_read")

        mx_in = sem("mx_in")
        mx_T = sem("mx_T")
        mx_xT = sem("mx_xT")
        mx_kv = sem("mx_kv")
        mx_q = sem("mx_q")
        mx_ek = sem("mx_ek")
        mx_v = sem("mx_v")
        mx_eq = sem("mx_eq")
        mx_rk = sem("mx_rk")
        mx_k = sem("mx_k")
        mx_rq = sem("mx_rq")
        mx_qT = sem("mx_qT")
        mx_ctx = sem("mx_ctx")
        mx_acc = sem("mx_acc")
        mx_kacc = sem("mx_kacc")
        ksum_ps = sem("ksum_ps")
        ctx_masked = sem("ctx_masked")
        aw_ps = sem("aw_ps")
        aw_ready = sem("aw_ready")
        den_ps = sem("den_ps")
        den_max = sem("den_max")
        den_inv = sem("den_inv")
        qn_ready = sem("qn_ready")
        ao_ps = sem("ao_ps")
        ao_ready = sem("ao_ready")

        pass_done = sem("pass_done")
        pass_tables = sem("pass_tables")
        pass_T = sem("pass_T")
        edges_done = sem("edges_done")
        x_again = sem("x_again")

        z1_ps = sem("z1_ps")
        z1_ready = sem("z1_ready")
        z2_ps = sem("z2_ps")
        z2_ready = sem("z2_ready")
        bn_var = sem("bn_var")
        bn_sd = sem("bn_sd")
        bn_ready = sem("bn_ready")
        y_relu = sem("y_relu")
        y_sum = sem("y_sum")
        y_T = sem("y_T")
        x1_ready = sem("x1_ready")
        x1_stats = sem("x1_stats")
        x1_stored = sem("x1_stored")
        trash_stored = sem("trash_stored")
        l2_var = sem("l2_var")
        l2_sd = sem("l2_sd")
        l2_chain = sem("l2_chain")
        l2_ready = sem("l2_ready")
        tk_ready = sem("tk_ready")
        tk_stored = [sem(f"tk_stored{i}") for i in range(2)]
        tk_T = sem("tk_T")
        tk_xT = sem("tk_xT")
        tk_lg = sem("tk_lg")
        tk_scaled = sem("tk_scaled")
        lg_ready = sem("lg_ready")
        gate_in = sem("gate_in")
        gate_exp = sem("gate_exp")
        cnt_ready = sem("cnt_ready")
        rank_ps = sem("rank_ps")
        ob_ready = sem("ob_ready")
        oh_made = sem("oh_made")
        oa_ready = sem("oa_ready")
        list_step = sem("list_step")
        list_zero = sem("list_zero")
        tok_ready = sem("tok_ready")
        lists_ready = sem("lists_ready")

        w_in = [sem(f"w_in{i}") for i in range(2)]
        w_ready = sem("w_ready")
        cur_ready = sem("cur_ready")
        tok_in = [sem(f"tok_in{i}") for i in range(TOKS)]
        tok_T = sem("tok_T")
        xeT_half = sem("xeT_half")
        hid_ps = sem("hid_ps")
        hid_b = sem("hid_b")
        hid_g = sem("hid_g")
        hidT_ps = sem("hidT_ps")
        hidT_a = sem("hidT_a")
        hidT_v = sem("hidT_v")
        y_ps = sem("y_ps")
        y_b = sem("y_b")
        y_w = sem("y_w")
        row_ready = sem("row_ready")
        acc_in = sem("acc_in")
        out_in = sem("out_in")

        block = ctx.enter_context(nc.Block())

        def by_half(b):
            return b[:, 0:HALVES * P].rearrange("p (h c) -> p h c", h=HALVES)[:, :, 0:TILE]

        def experts_of(engine, j, n):
            return nc.values_load_multi_w_load_instructions(ej_i[0:1, bass.ds(j + 3, n)], engines=(engine,), min_val=0,
                                                            max_val=EXPERTS - 1)[1]

        def node_rows(dram, sbuf, c):
            d = dram[bass.ds(c * CHUNK_TILES * TILE, CHUNK_TILES * TILE), :].rearrange("(t p) d -> p t d", p=TILE)
            return [(d[0:DMA_ROWS], sbuf[0:DMA_ROWS]), (d[DMA_ROWS:TILE], sbuf[DMA_ROWS:TILE])]


        def load_edges(sp, g, n, r, u, fresh):
            if not fresh:
                sp.wait_ge(eaT_ps, 2 * (n - 1))
            rows = a["edge_attr_128"][bass.ds(g * GROUP, GROUP), :].rearrange("(p j) d -> p (j d)", j=GT)
            sp.dma_start(ea[:, u].rearrange("p j d -> p (j d)"), rows).then_inc(ea_in[u], 16)

        def load_tail(sp, n, passes):
            full, rest = TAIL // GT, TAIL % GT
            sp.wait_ge(eaT_ps, 2 * (n - 1))
            start = (GROUPS - 1) * GROUP
            last = a["edge_attr_128"][start + full * GT:start + TAIL, :].rearrange("(p j) d -> p (j d)", j=rest)
            sp.dma_start(ea[full:full + 1, 1, 0:rest, :].rearrange("p j d -> p (j d)"), last).then_inc(ea_tail, 16)
            sp.wait_ge(ea_tail, 16 * (passes + 1))
            rows = a["edge_attr_128"][start:start + full * GT, :].rearrange("(p j) d -> p (j d)", j=GT)
            sp.dma_start(ea[0:full, 1].rearrange("p j d -> p (j d)"), rows).then_inc(ea_in[1], 16)

        def gather_nodes(pool, n, u, fresh):
            pool.wait_ge(idx_ready, n + 1)
            if not fresh:
                pool.wait_ge(sums_done, PAIRS * (n - 1))
            pool.sem_inc(pool_passed, 1)
            for j in range(GT):
                pool.indirect_dma_start(out=xg[:, u, j], out_offset=None, in_=node_table,
                                        in_offset=bass.IndirectOffsetOnAxis(ap=idx_cur[:, u, j:j + 1], axis=0)
                                        ).then_inc(xg_in[u][j // 2], 16)

        def transpose_edges(pe, n, r, u, fresh):
            pe.wait_ge(ea_in[u], 16 * (r + 1))
            for hh in range(2):
                if not fresh:
                    pe.wait_ge(eaT_ready, 2 * (n - 1) + hh + 1)
                for k in range(3):
                    last = nc.tensor.transpose(bank[hh][:, k * P:(k + 1) * P], ea[:, u, 3 * hh + k], ident[:])
                last.then_inc(eaT_ps, 1)

        def embed_edges(pe, n, r, u, fresh):
            for q in range(PAIRS):
                pe.wait_ge(eaT_ready, 2 * n + (1 if q == 0 else 2))
                if not fresh:
                    pe.wait_ge(sums_done, PAIRS * (n - 1) + q + 1)
                b = bank[2 + q]
                for k in range(2):
                    last = nc.tensor.matmul(b[:, k * DIM:(k + 1) * DIM], eaT[:, u, 2 * q + k], w_edge[:],
                                            start=True, stop=True)
                last.then_inc(e_ready, 1)

        def aggregate(pe, n, u):
            b = bank[5]
            pe.wait_ge(agg_read, n + 1)
            pe.wait_ge(onehot_ready, n + 1)
            for j in range(GT):
                if j % 2 == 0:
                    pe.wait_ge(msg_ready, PAIRS * n + j // 2 + 1)
                for h in range(HALVES):
                    last = nc.tensor.matmul(b[:, h * P:(h + 1) * P], msg[:, u, j, h * P:(h + 1) * P], onehot[:, u, j],
                                            start=(j == 0 and h == 0), stop=(j == GT - 1), skip_group_check=True)
            last.then_inc(agg_ready, 1)

        def copy_edges(act, n, u):
            for hh in range(2):
                act.wait_ge(eaT_ps, 2 * n + hh + 1)
                nc.scalar.copy(eaT[:, u, 3 * hh:3 * hh + 3], bank[hh][:, 0:3 * P].rearrange("p (k c) -> p k c", k=3)
                               ).then_inc(eaT_ready, 1)

        def relu_messages(act, g, n, r, u, more):
            if more:
                for q in range(PAIRS):
                    act.wait_ge(xg_in[u][q], 32 * (r + 1))
                nc.scalar.copy(idx_cur[:, u], srcT[:, bass.ds(g + 2, 1)].rearrange("p a j -> p (a j)")
                               ).then_inc(idx_ready, 1)
            for q in range(PAIRS):
                act.wait_ge(sums_done, PAIRS * n + q + 1)
                nc.scalar.activation(msg[:, u, 2 * q:2 * q + 2], msg[:, u, 2 * q:2 * q + 2], ACT.Relu
                                     ).then_inc(msg_ready, 1)

        def mark_window(dve, g, u):
            nc.vector.tensor_tensor(onehot[:, u], iota_f[:].unsqueeze(1).to_broadcast([P, GT, P]),
                                    relT[:, bass.ds(g, 1)].rearrange("p a j -> p (a j)").unsqueeze(2).to_broadcast([P, GT, P]),
                                    ALU.is_equal).then_inc(onehot_ready, 1)

        def add_nodes(dve, n, r, u):
            for q in range(PAIRS):
                dve.wait_ge(e_ready, PAIRS * n + q + 1)
                dve.wait_ge(xg_in[u][q], 32 * (r + 1))
                nc.vector.tensor_tensor(msg[:, u, 2 * q:2 * q + 2],
                                        bank[2 + q][:].rearrange("p (k c) -> p k c", k=2),
                                        xg[:, u, 2 * q:2 * q + 2], ALU.add).then_inc(sums_done, 1)

        def add_window(dve, n, u, start, h_count):
            dve.wait_ge(agg_ready, n + 1)
            dve.wait_ge(h_updates, h_count)
            w = hT[:, :, bass.ds(start, WINDOW)]
            nc.vector.tensor_tensor(w, bank[5][:, 0:HALVES * P].rearrange("p (h c) -> p h c", h=HALVES),
                                    w, ALU.add).then_inc(h_updates, 1)

        def load_expert(sp, e):
            s = wts[:, e % 2]
            sp.dma_start(view(s, 0, HALVES, HIDDEN), a["L0_ffn_W1"][e].rearrange("(k p) h -> p k h", p=P)
                         ).then_inc(w_in[e % 2], 16)
            sp.dma_start(view(s, 2048, HIDDEN // P, DIM), a["L0_ffn_W2"][e].rearrange("(c p) d -> p c d", p=P)
                         ).then_inc(w_in[e % 2], 16)
            sp.dma_start(s[:, 4096:4096 + HIDDEN], a["L0_ffn_b1"][e].partition_broadcast(P)).then_inc(w_in[e % 2], 16)
            sp.dma_start(s[:, 5120:5120 + DIM], a["L0_ffn_b2"][e].partition_broadcast(P)).then_inc(w_in[e % 2], 16)

        @block.sync
        def _(sp):
            def load_x(c):
                for d, s in node_rows(a["x"], xs[:, c * CHUNK_TILES:(c + 1) * CHUNK_TILES], c):
                    sp.dma_start(s, d).then_inc(x_in[c], 16)

            load_x(0)
            sp.wait_ge(ids_memset, 2)
            for name, t in (("dst", dst_i), ("src", src_i)):
                v = a[name]
                full = (GROUPS - 1) * GROUP
                sp.dma_start(t[0:GROUPS - 1], v[0:full].rearrange("(g e) -> g e", e=GROUP)).then_inc(ids_in, 16)
                sp.dma_start(t[GROUPS - 1:GROUPS, 0:TAIL], v[full:EDGES].unsqueeze(0)).then_inc(ids_in, 16)
            for c in range(1, CHUNKS):
                load_x(c)
            load_edges(sp, 0, 0, 0, 0, True)
            load_edges(sp, 1, 1, 0, 1, True)
            loads = [
                (eps1[:], a["L0_gnn_eps"].partition_broadcast(P)),
                (wr[:], a["L0_ffn_Wr"].rearrange("(k p) e -> p k e", p=P)),
                (br[:], a["L0_ffn_br"].partition_broadcast(P)),
            ]
            for n, name in enumerate(("L0_gnn_b1", "L0_gnn_b2", "L0_gnn_gamma", "L0_gnn_beta", "L0_mix_bproj")):
                loads.append((cvec[:, n], a[name].rearrange("(h p) -> p h", p=P)))
            for t, name in ((ln_g, "L0_ffn_ln_g"), (ln_b, "L0_ffn_ln_b")):
                for h in range(HALVES):
                    loads.append((t[:, :, h], a[name][:, h * P:(h + 1) * P].rearrange("e p -> p e")))
            assert len(loads) + 6 == CONST_DMAS
            with nc.allow_non_contiguous_dma(reason="small columns of constants"):
                for s, d in loads:
                    sp.dma_start(s, d).then_inc(consts_in, 16)
            for c in range(CHUNKS):
                sp.wait_ge(rows_ready, c + 1)
                for d, s in node_rows(node_table, table_stage[:, c % 2], c):
                    sp.dma_start(d, s).then_inc(rows_stored[c % 2], 16)
            load_expert(sp, 0)

            with sp.Fori(0, BODIES - 1) as i:
                load_edges(sp, 2 * i + 2, 2 * i + 2, i + 1, 0, False)
                load_edges(sp, 2 * i + 3, 2 * i + 3, i + 1, 1, False)
            load_edges(sp, GROUPS - 2, GROUPS - 2, BODIES, 0, False)
            load_tail(sp, GROUPS - 1, 0)
            sp.wait_ge(mx_in, TILES)
            for c in range(CHUNKS):
                for d, s in node_rows(a["x"], xs[:, c * CHUNK_TILES:(c + 1) * CHUNK_TILES], c):
                    sp.dma_start(s, d).then_inc(x_again, 16)

            sp.wait_ge(tables_ready, 3)
            again = sp.value_load(miss_i[0:1, 0:1], min_val=0, max_val=1)
            with sp.If(again > 0):
                with sp.Fori(0, WINDOWS) as w:
                    n0 = (w + 1) * GROUPS
                    r0 = (w + 1) * (GROUPS // 2)
                    load_edges(sp, 0, n0, r0, 0, False)
                    load_edges(sp, 1, n0 + 1, r0, 1, False)
                    with sp.Fori(0, BODIES - 1) as i:
                        load_edges(sp, 2 * i + 2, n0 + 2 * i + 2, r0 + i + 1, 0, False)
                        load_edges(sp, 2 * i + 3, n0 + 2 * i + 3, r0 + i + 1, 1, False)
                    load_edges(sp, GROUPS - 2, n0 + GROUPS - 2, r0 + BODIES, 0, False)
                    load_tail(sp, n0 + GROUPS - 1, w + 1)
            with sp.Else():
                sp.nop()
            sp.wait_ge(edges_done, 2)
            sp.wait_ge(ao_ps, 2 * COL_CHUNKS)
            load_expert(sp, 1)
            sp.dma_start(acc_table[NODES:NODES + P, :], ek[:]).then_inc(trash_stored, 16)
            def store_rows(c, u):
                sp.wait_ge(x1_ready, 3 * c + 3)
                for d, s in node_rows(acc_table, xs[:, bass.ds(c * CHUNK_TILES, CHUNK_TILES)], c):
                    sp.dma_start(d, s).then_inc(x1_stored, 16)
                sp.wait_ge(tk_ready, c + 1)
                for d, s in node_rows(token_table, xn_cur[:, u], c):
                    sp.dma_start(d, s).then_inc(tk_stored[u], 16)

            for c in range(CHUNKS):
                store_rows(c, c % 2)
            for e in range(EXPERTS):
                if e == 2:
                    sp.wait_ge(lists_ready, 1)
                if e >= 2:
                    done = sp.value_load(first_i[0:1, e - 1:e], min_val=1, max_val=SLOTS)
                    sp.wait_ge(y_b, done)
                    load_expert(sp, e)
                sp.wait_ge(w_in[e % 2], 16 * W_DMAS * (e // 2 + 1))
                sp.sem_inc(w_ready, 1)
            sp.wait_ge(acc_in, 16 * MAIN)
            second = sp.value_load(more_i[0:1, 0:1], min_val=0, max_val=1)
            with sp.If(second > 0):
                sp.wait_ge(acc_in, 16 * SLOTS)
            with sp.Else():
                sp.nop()
            sp.dma_start(out.rearrange("n d -> (n d)").rearrange("(r c) -> r c", r=80),
                         acc_table[0:NODES, :].rearrange("n d -> (n d)").rearrange("(r c) -> r c", r=80)
                         ).then_inc(out_in, 16)
            sp.wait_ge(out_in, 16)

        @block.gpsimd
        def _(pool):
            step = Chain(pool, pool_chain)
            nc.gpsimd.iota(iota_i[:], pattern=[[1, P]], base=0, channel_multiplier=0).then_inc(consts_made, 1)
            nc.gpsimd.iota(part_i[:], pattern=[[1, 1]], base=0, channel_multiplier=1).then_inc(consts_made, 1)
            nc.gpsimd.iota(tokid_i[:], pattern=[[TILE, TILES]], base=0, channel_multiplier=1).then_inc(consts_made, 1)
            step(nc.gpsimd.memset(ident[:], 0.0))
            nc.gpsimd.affine_select(out=ident[:], in_=ident[:], compare_op=ALU.not_equal, fill=1.0, base=0,
                                    pattern=[[-1, P]], channel_multiplier=1).then_inc(consts_made, 1)
            nc.gpsimd.memset(ones[:], 1.0).then_inc(consts_made, 1)
            step(nc.gpsimd.memset(below[:], 1.0))
            nc.gpsimd.affine_select(out=below[:], in_=below[:], compare_op=ALU.is_gt, fill=0.0, base=0,
                                    pattern=[[1, P]], channel_multiplier=-1).then_inc(consts_made, 1)
            step(nc.gpsimd.memset(blocks[:], 0.0))
            for b in range(P // HEAD_DIM):
                s = slice(b * HEAD_DIM, (b + 1) * HEAD_DIM)
                step(nc.gpsimd.memset(blocks[s, s], 1.0))
            nc.gpsimd.memset(xT_t[:], 0.0).then_inc(consts_made, 1)
            nc.gpsimd.memset(qT[:, :, NODES:NODES_PAD], 0.0).then_inc(consts_made, 1)
            nc.gpsimd.memset(hT[:], 0.0).then_inc(h_updates, 1)
            nc.gpsimd.memset(ctx_acc[:], 0.0).then_inc(mx_acc, 1)
            nc.gpsimd.memset(k_acc[:], 0.0).then_inc(mx_kacc, 1)

            pool.wait_ge(b_edge_in, 16)
            for c in range(CHUNKS - 1):
                pool.wait_ge(xn_ready, CHUNK_TILES * (c + 1))
                if c >= 2:
                    pool.wait_ge(rows_stored[c % 2], 32 * (c // 2))
                nc.gpsimd.tensor_tensor(table_stage[0:TILE, c % 2], xs[0:TILE, c * CHUNK_TILES:(c + 1) * CHUNK_TILES],
                                        b_edge[0:TILE].unsqueeze(1).to_broadcast([TILE, CHUNK_TILES, DIM]), ALU.add
                                        ).then_inc(rows_ready, 1)
            for c in range(2):
                pool.wait_ge(rows_stored[c], 32 * ((CHUNKS + 1 - c) // 2))
            gather_nodes(pool, 0, 0, True)
            gather_nodes(pool, 1, 1, True)
            with pool.Fori(0, BODIES) as i:
                gather_nodes(pool, 2 * i + 2, 0, False)
                gather_nodes(pool, 2 * i + 3, 1, False)
            pool.wait_ge(tables_ready, 3)
            again = pool.value_load(miss_i[0:1, 0:1], min_val=0, max_val=1)
            with pool.If(again > 0):
                with pool.Fori(0, WINDOWS) as w:
                    n0 = (w + 1) * GROUPS
                    gather_nodes(pool, n0, 0, False)
                    gather_nodes(pool, n0 + 1, 1, False)
                    with pool.Fori(0, BODIES) as i:
                        gather_nodes(pool, n0 + 2 * i + 2, 0, False)
                        gather_nodes(pool, n0 + 2 * i + 3, 1, False)
            with pool.Else():
                pool.nop()

            def add_attention(c, u):
                pool.wait_ge(y_relu, 2 * c + 2)
                nc.gpsimd.tensor_tensor(y_cur[:, u], y_cur[:, u], qT[:, :, bass.ds(c * (CHUNK_TILES * TILE), CHUNK_TILES * TILE)],
                                        ALU.add).then_inc(y_sum, 1)

            for c in range(CHUNKS):
                add_attention(c, c % 2)

            def weigh_slots(c, u, fresh):
                if not fresh:
                    pool.wait_ge(list_step, c - 1)
                ts_ = bass.ds(c * CHUNK_TILES, CHUNK_TILES)
                for s in range(2):
                    o = oa[0:TILE, u, s * CHUNK_TILES:(s + 1) * CHUNK_TILES]
                    pool.wait_ge(oh_made, 2 * c + s + 1)
                    for k, v in enumerate((tokid[0:TILE, ts_], rs[0:TILE, (4, 5)[s], ts_])):
                        nc.gpsimd.tensor_tensor(o[:, :, k * LIST:(k + 1) * LIST], oh[0:TILE, u, s],
                                                v.unsqueeze(2).to_broadcast([TILE, CHUNK_TILES, LIST]), ALU.mult
                                                ).then_inc(oa_ready, 1)

            for c in range(CHUNKS):
                weigh_slots(c, c % 2, c < 2)

            for u in range(2):
                pool.wait_ge(tk_stored[u], 32 * ((CHUNKS + 1 - u) // 2))
            pool.wait_ge(x1_stored, 32 * CHUNKS)
            pool.wait_ge(trash_stored, 16)
            pool.wait_ge(tok_ready, 1)

            def fetch(j, r, u, fresh):
                pool.wait_ge(tok_in[u], 16 * r)
                nc.gpsimd.tensor_copy(tokc[:, u:u + 1], tok_i[:, bass.ds(j, 1)]).then_inc(cur_ready, 1)
                pool.wait_ge(cur_ready, j + 1)
                if not fresh:
                    pool.wait_ge(tok_T, j - TOKS + 1)
                pool.sem_inc(pool_passed, 1)
                pool.indirect_dma_start(out=tok[:, u], out_offset=None, in_=token_table,
                                        in_offset=bass.IndirectOffsetOnAxis(ap=tokc[:, u:u + 1], axis=0)
                                        ).then_inc(tok_in[u], 16)

            def put(j, u, fresh=False):
                if not fresh:
                    pool.wait_ge(acc_in, 16 * j)
                nc.gpsimd.tensor_copy(rowc[:, u:u + 1], row_i[:, bass.ds(j, 1)]).then_inc(row_ready, 1)
                pool.wait_ge(row_ready, j + 1)
                pool.wait_ge(y_w, j + 1)
                pool.sem_inc(pool_passed, 1)
                pool.indirect_dma_start(out=acc_table, out_offset=bass.IndirectOffsetOnAxis(ap=rowc[:, u:u + 1], axis=0),
                                        in_=ys[:, u], in_offset=None, compute_op=ALU.add).then_inc(acc_in, 16)

            for k in range(TOKS):
                fetch(k, 0, k, True)
            pool.wait_ge(lists_ready, 1)
            for k in range(TOKS):
                fetch(TOKS + k, 1, k, False)
                put(k, k % 2, k == 0)
            with pool.Fori(1, MAIN // TOKS - 1) as i:
                for k in range(TOKS):
                    fetch(TOKS * (i + 1) + k, i + 1, k, False)
                    put(TOKS * i + k, k % 2)
            for k in range(TOKS):
                put(MAIN - TOKS + k, k % 2)
            second = pool.value_load(more_i[0:1, 0:1], min_val=0, max_val=1)
            with pool.If(second > 0):
                for k in range(TOKS):
                    fetch(MAIN + k, MAIN // TOKS, k, False)
                for k in range(TOKS):
                    put(MAIN + k, k % 2)
            with pool.Else():
                pool.nop()

        @block.tensor
        def _(pe):
            pe.wait_ge(consts_made, 8)
            pe.wait_ge(rel_ready, 1)
            nc.tensor.transpose(bank[6][0:1, 0:GROUPS], gstat[:, 0:1], ident[0:GROUPS, 0:GROUPS])
            nc.tensor.transpose(bank[6][0:1, P:P + GROUPS], gstat[:, 1:2], ident[0:GROUPS, 0:GROUPS]).then_inc(base_T, 1)
            for j in range(GT):
                nc.tensor.transpose(bank[4][:, j * GROUPS:(j + 1) * GROUPS], rel[:, j:GROUP:GT], ident[0:GROUPS, 0:GROUPS])
            for j in range(GT):
                last = nc.tensor.transpose(bank[5][:, j * GROUPS:(j + 1) * GROUPS], src_f[:, j:GROUP:GT], ident[0:GROUPS, 0:GROUPS])
            last.then_inc(ids_T, 1)
            pe.wait_ge(consts_in, CONST_DMAS * 16)
            for rb in range(8):
                for k in range(HALVES):
                    if rb < 2:
                        o = bank[0][:, k * 256 + rb * P:k * 256 + (rb + 1) * P]
                    elif rb < 6:
                        o = bank[1 + k][:, (rb - 2) * P:(rb - 1) * P]
                    else:
                        o = bank[3][:, k * 256 + (rb - 6) * P:k * 256 + (rb - 5) * P]
                    last = nc.tensor.transpose(o, w_natural[:, rb, k * P:(k + 1) * P], ident[:])
            last.then_inc(wT_ready, 1)
            pe.wait_ge(wT_copied, 4)
            pe.wait_ge(tables_ready, 3)

            def mix_transpose(t):
                pe.wait_ge(mx_in, t + 1)
                pe.wait_ge(mx_acc, t + 1)
                for k in range(HALVES):
                    last = nc.tensor.transpose(bank[7][:, k * P:k * P + TILE], xn_t[0:TILE, k * P:(k + 1) * P],
                                               ident[0:TILE, 0:TILE])
                last.then_inc(mx_T, 1)

            def mix_qkv(t):
                pe.wait_ge(mx_xT, t + 1)
                pe.wait_ge(mx_rk, t + 1)
                pe.wait_ge(mx_ek, t + 1)
                pe.wait_ge(mx_v, t + 1)
                for k in range(HALVES):
                    last = nc.tensor.matmul(bank[6][0:TILE, :], xT_t[:, k, 0:TILE], wkvT[:, k], start=(k == 0), stop=(k == 1))
                last.then_inc(mx_kv, 1)
                pe.wait_ge(h_updates, 3 * t + 3)
                for o in range(HALVES):
                    for k in range(HALVES):
                        last = nc.tensor.matmul(bank[7][:, o * P:(o + 1) * P], wqT[:, k, o * P:(o + 1) * P],
                                                xT_t[:, k], start=(k == 0), stop=(k == 1))
                last.then_inc(mx_q, 1)

            def mix_context(t):
                pe.wait_ge(mx_k, t + 2)
                pe.wait_ge(mx_v, t + 2)
                pe.wait_ge(mx_rq, t + 1)
                for h in range(HALVES):
                    s = slice(h * P, (h + 1) * P)
                    last = nc.tensor.matmul(bank[7][:, h * P:(h + 1) * P], v_t[0:TILE, s], k_t[0:TILE, s],
                                            start=True, stop=True)
                last.then_inc(mx_ctx, 1)

            def attn_den(c, more):
                if more:
                    pe.wait_ge(ao_ready, 2 * c - 2)
                for h in range(HALVES):
                    last = nc.tensor.matmul(bank[6 + h][:, 0:COLS], ksum_m[:, h], qT[:, h, bass.ds(c * COLS, COLS)],
                                            start=True, stop=True)
                last.then_inc(den_ps, 1)

            def attn_out(c, more):
                pe.wait_ge(qn_ready, c + 1)
                if more:
                    pe.wait_ge(den_max, 2 * (c + 2))
                for o in range(HALVES):
                    for h in range(HALVES):
                        last = nc.tensor.matmul(bank[6 + o][:, 0:COLS], attn_w[:, h, o * P:(o + 1) * P], qn[:, h],
                                                start=(h == 0), stop=(h == 1))
                    last.then_inc(ao_ps, 1)

            def edge_pass(n0, r0, fresh, phases):
                transpose_edges(pe, n0, r0, 0, fresh)
                transpose_edges(pe, n0 + 1, r0, 1, False)
                embed_edges(pe, n0, r0, 0, fresh)

                def body(i, riders):
                    n = n0 + 2 * i
                    transpose_edges(pe, n + 2, r0 + i + 1, 0, False)
                    embed_edges(pe, n + 1, r0 + i, 1, False)
                    if riders and riders[0]:
                        riders[0](i)
                    aggregate(pe, n, 0)
                    if riders and riders[1]:
                        riders[1](i)
                    transpose_edges(pe, n + 3, r0 + i + 1, 1, False)
                    embed_edges(pe, n + 2, r0 + i + 1, 0, False)
                    aggregate(pe, n + 1, 1)
                    if riders and riders[2]:
                        riders[2](i)

                for lo, hi, riders, between in phases:
                    with pe.Fori(lo, hi) as i:
                        body(i, riders)
                    if between:
                        between()
                n = n0 + GROUPS
                embed_edges(pe, n - 1, r0 + BODIES, 1, False)
                aggregate(pe, n - 2, 0)
                aggregate(pe, n - 1, 1)

            def attn_weights():
                pe.wait_ge(mx_kacc, TILES + 1)
                pe.wait_ge(mx_acc, TILES + 1)
                for h in range(HALVES):
                    last = nc.tensor.matmul(bank[7][:, h:h + 1], k_acc[0:TILE, h * P:(h + 1) * P], ones[0:TILE, 0:1],
                                            start=True, stop=True)
                last.then_inc(ksum_ps, 1)
                pe.wait_ge(ctx_masked, 4)
                pe.wait_ge(mx_rk, TILES + 1)
                pe.wait_ge(mx_ek, TILES + 1)
                pe.wait_ge(mx_v, TILES + 1)
                for h in range(HALVES):
                    last = nc.tensor.matmul(bank[6][:, h * DIM:(h + 1) * DIM], ctx_m[:, h], wpT[:, h], start=True, stop=True)
                last.then_inc(aw_ps, 1)
                pe.wait_ge(aw_ready, 1)
                attn_den(0, False)

            edge_pass(0, 0, True, [
                (0, TILES, (mix_transpose, mix_qkv, mix_context), attn_weights),
                (TILES, TILES + 1, (None, None, lambda i: attn_den(1, False)), None),
                (TILES + 1, BODIES - 1, (None, lambda i: attn_out(i - TILES - 1, True),
                                         lambda i: attn_den(i - TILES + 1, True)), None),
                (BODIES - 1, BODIES, (None, lambda i: attn_out(COL_CHUNKS - 2, True), None), None)])
            attn_out(COL_CHUNKS - 1, False)
            again = pe.value_load(miss_i[0:1, 0:1], min_val=0, max_val=1)
            with pe.If(again > 0):
                pe.wait_ge(pass_tables, 3)
                for j in range(GT):
                    last = nc.tensor.transpose(bank[4][:, j * GROUPS:(j + 1) * GROUPS], rel[:, j:GROUP:GT], ident[0:GROUPS, 0:GROUPS])
                last.then_inc(pass_T, 1)
                pe.wait_ge(pass_done, 1)
                with pe.Fori(0, WINDOWS) as w:
                    edge_pass((w + 1) * GROUPS, (w + 1) * (GROUPS // 2), False, [(0, BODIES, None, None)])
            with pe.Else():
                pe.nop()

            pe.wait_ge(edges_done, 2)

            def mlp1(c, u, fresh):
                for o in range(HALVES):
                    if not fresh:
                        pe.wait_ge(z1_ready, 2 * (c - 1) + o + 1)
                    for k in range(HALVES):
                        last = nc.tensor.matmul(bank[o][:, 0:COLS], w1[:, k, o * P:(o + 1) * P],
                                                hT[:, k, bass.ds(c * COLS, COLS)], start=(k == 0), stop=(k == 1))
                    last.then_inc(z1_ps, 1)

            def mlp2(c, u, fresh):
                pe.wait_ge(z1_ready, 2 * c + 2)
                for o in range(HALVES):
                    if not fresh:
                        pe.wait_ge(z2_ready, 2 * (c - 1) + o + 1)
                    for k in range(HALVES):
                        last = nc.tensor.matmul(bank[2 + o][:, 0:COLS], w2[:, k, o * P:(o + 1) * P], z1[:, u, k],
                                                start=(k == 0), stop=(k == 1))
                    last.then_inc(z2_ps, 1)

            mlp1(0, 0, True)
            mlp1(1, 1, False)
            mlp2(0, 0, True)
            with pe.Fori(0, (COL_CHUNKS - 3) // 2) as i:
                mlp1(2 * i + 2, 0, False)
                mlp2(2 * i + 1, 1, False)
                mlp1(2 * i + 3, 1, False)
                mlp2(2 * i + 2, 0, False)
            mlp1(COL_CHUNKS - 1, 0, False)
            mlp2(COL_CHUNKS - 2, 1, False)
            mlp2(COL_CHUNKS - 1, 0, False)

            def y_transpose(c, u, fresh):
                pe.wait_ge(y_sum, c + 1)
                if not fresh:
                    pe.wait_ge(x1_ready, 3 * c)
                for k in range(CHUNK_TILES):
                    for h in range(HALVES):
                        last = nc.tensor.transpose(bank[k // 2][0:TILE, (k % 2) * DIM + h * P:(k % 2) * DIM + (h + 1) * P],
                                                   y_cur[:, u, h, k * TILE:(k + 1) * TILE], ident[:])
                last.then_inc(y_T, 1)

            def row_transpose(c, u, fresh):
                pe.wait_ge(tk_ready, c + 1)
                if not fresh:
                    pe.wait_ge(tk_xT, 3 * c)
                for k in range(2 * CHUNK_TILES):
                    t, h = k // 2, k % 2
                    last = nc.tensor.transpose(bank[4 + k // 4][:, (k % 4) * TILE:(k % 4 + 1) * TILE],
                                               xn_cur[0:TILE, u, t, h * P:(h + 1) * P], ident[0:TILE, 0:TILE])
                last.then_inc(tk_T, 1)

            def route(c, u, fresh):
                pe.wait_ge(tk_xT, 3 * c + 3)
                if not fresh:
                    pe.wait_ge(tk_scaled, c - 1)
                for t in range(CHUNK_TILES):
                    for h in range(HALVES):
                        last = nc.tensor.matmul(bank[(7, 3)[u]][0:TILE, t * EXPERTS:(t + 1) * EXPERTS], xnT[:, u, t, h], wr[:, h],
                                                start=(h == 0), stop=(h == 1))
                last.then_inc(tk_lg, 1)

            for c in range(CHUNKS):
                if c == 0:
                    for k in range(3):
                        y_transpose(k, k % 2, k == 0)
                    row_transpose(0, 0, True)
                if c + 3 < CHUNKS:
                    y_transpose(c + 3, (c + 3) % 2, False)
                if c + 1 < CHUNKS:
                    row_transpose(c + 1, (c + 1) % 2, False)
                route(c, c % 2, c < 2)
            pe.wait_ge(cnt_ready, 1)
            cnt = rt[0:TILE, 2].rearrange("p t e -> p (t e)")
            nc.tensor.matmul(bank[0][0:TILE, 0:TILES * EXPERTS], below[0:TILE, 0:TILE], cnt, start=True, stop=True)
            nc.tensor.matmul(bank[0][0:P, 256:256 + TILES * EXPERTS], ones[0:TILE, :], cnt, start=True, stop=True
                             ).then_inc(rank_ps, 1)
            pe.wait_ge(list_zero, 1)
            zeros = eq[:].rearrange("p h c -> p (h c)")
            nc.tensor.matmul(bank[1][:, 0:2 * LIST], zeros[:, 0:P], zeros[:, 0:2 * LIST], start=True, stop=False,
                             skip_group_check=True)

            def collect(c, u):
                pe.wait_ge(ob_ready, 2 * c + 2)
                pe.wait_ge(oa_ready, 4 * c + 4)
                for t in range(2 * CHUNK_TILES):
                    last = nc.tensor.matmul(bank[1][:, 0:2 * LIST], ob[0:TILE, u, t], oa[0:TILE, u, t],
                                            start=False, stop=True, skip_group_check=True)
                last.then_inc(list_step, 1)

            for c in range(CHUNKS):
                collect(c, c % 2)

            pe.wait_ge(lists_ready, 1)

            def slot_transpose(j, u, r, fresh):
                pe.wait_ge(tok_in[u], 16 * (r + 1))
                if not fresh:
                    pe.wait_ge(xeT_half, 2 * j)
                for k in range(HALVES):
                    last = nc.tensor.transpose(bank[0][:, k * P:(k + 1) * P], tok[:, u, k * P:(k + 1) * P], ident[:])
                last.then_inc(tok_T, 1)

            def slot_up(j, u, e, fresh):
                pe.wait_ge(xeT_half, 2 * j + 2)
                pe.wait_ge(w_ready, e + 1)
                par = e % 2
                for c in range(2):
                    if not fresh:
                        pe.wait_ge(hid_b, 2 * (j - 1) + c + 1)
                    for k in range(HALVES):
                        w = wts[:, bass.ds(par, 1), k * HIDDEN + c * 512:k * HIDDEN + (c + 1) * 512]
                        last = nc.tensor.matmul(bank[1 + c][:], xeT[:, u, k], w.rearrange("p a c -> p (a c)"),
                                                start=(k == 0), stop=(k == 1))
                    last.then_inc(hid_ps, 1)

            def slot_hidden_transpose(j, u, fresh):
                for c in range(2):
                    pe.wait_ge(hid_g, 2 * j + c + 1)
                    if not fresh:
                        pe.wait_ge((hidT_a, hidT_v)[c], j)
                    for k in range(4):
                        last = nc.tensor.transpose(bank[3 + c][:, k * P:(k + 1) * P],
                                                   hid[:, u, (4 * c + k) * P:(4 * c + k + 1) * P], ident[:])
                    last.then_inc(hidT_ps, 1)

            def slot_down(j, e, fresh):
                par = e % 2
                if not fresh:
                    pe.wait_ge(y_b, j)
                for k in range(HIDDEN // P):
                    if k % 4 == 0:
                        pe.wait_ge((hidT_a, hidT_v)[k // 4], j + 1)
                    w = wts[:, bass.ds(par, 1), 2048 + k * DIM:2048 + (k + 1) * DIM].rearrange("p a c -> p (a c)")
                    last = nc.tensor.matmul(bank[5][:, 0:DIM], hidT[:, k], w, start=(k == 0), stop=(k == HIDDEN // P - 1))
                last.then_inc(y_ps, 1)

            def slot_step(j, u, tok_u, r, e_here, e_next, fresh=False):
                slot_hidden_transpose(j, u, fresh)
                slot_up(j + 1, 1 - u, e_next, False)
                slot_transpose(j + 2, tok_u, r, False)
                slot_down(j, e_here, fresh)

            def slots(j0, n):
                fresh = j0 == 0
                e0, e1 = experts_of(PE, j0, 2)
                slot_transpose(j0, 0, j0 // TOKS, fresh)
                slot_up(j0, 0, e0, fresh)
                slot_transpose(j0 + 1, 1, j0 // TOKS, False)
                slot_step(j0, 0, 2, j0 // TOKS, e0, e1, fresh)
                if n > 4:
                    with pe.Fori(0, (n - 4) // 4) as i:
                        e = experts_of(PE, j0 + 4 * i + 1, 5)
                        for k in range(4):
                            slot_step(j0 + 4 * i + 1 + k, (k + 1) % 2, (k + 3) % TOKS, j0 // TOKS + i + (k + 3) // TOKS,
                                      e[k], e[k + 1])
                j = j0 + n - 3
                e0, e1, e2 = experts_of(PE, j, 3)
                slot_step(j, 1, TOKS - 1, (j0 + n) // TOKS - 1, e0, e1)
                slot_hidden_transpose(j + 1, 0, False)
                slot_up(j + 2, 1, e2, False)
                slot_down(j + 1, e1, False)
                slot_hidden_transpose(j + 2, 1, False)
                slot_down(j + 2, e2, False)

            slots(0, MAIN)
            second = pe.value_load(more_i[0:1, 0:1], min_val=0, max_val=1)
            with pe.If(second > 0):
                slots(MAIN, SLOTS - MAIN)
            with pe.Else():
                pe.nop()

        @block.scalar
        def _(act):
            loads = [
                (w_natural[:, 0:2], a["L0_mix_Wq"].rearrange("(r p) c -> p r c", p=P)),
                (w_natural[:, 2:6], a["L0_mix_Wkv"].rearrange("(r p) c -> p r c", p=P)),
                (w_natural[:, 6:8], a["L0_mix_Wproj"].rearrange("(r p) c -> p r c", p=P)),
                (w_edge[:], a["L0_gnn_W_edge"]),
                (w1[:], a["L0_gnn_W1"].rearrange("(k p) c -> p k c", p=P)),
                (w2[:], a["L0_gnn_W2"].rearrange("(k p) c -> p k c", p=P)),
            ]
            act.dma_start(b_edge[:], a["L0_gnn_b_edge"].partition_broadcast(P)).then_inc(b_edge_in, 16)
            for s, d in loads:
                act.dma_start(s, d).then_inc(consts_in, 16)
            for c in range(CHUNKS):
                ts_ = slice(c * CHUNK_TILES, (c + 1) * CHUNK_TILES)
                act.wait_ge(var_ready, c + 1)
                nc.scalar.activation(ln[0:TILE, 3, ts_], ln[0:TILE, 2, ts_], ACT.Sqrt).then_inc(sd_ready, 1)
                act.wait_ge(ln_ready, c + 1)
                for t in range(c * CHUNK_TILES, (c + 1) * CHUNK_TILES):
                    nc.scalar.activation(xs[0:TILE, t], xs[0:TILE, t], ACT.Identity, bias=ln[0:TILE, 5, t:t + 1],
                                         scale=ln[0:TILE, 4, t:t + 1]).then_inc(xn_ready, 1)
            act.wait_ge(tables_ready, 1)
            for g in range(2):
                nc.scalar.copy(idx_cur[:, g], srcT[:, g]).then_inc(idx_ready, 1)
            act.wait_ge(wT_ready, 1)
            nc.scalar.copy(wqT[:], bank[0][:].rearrange("p (k c) -> p k c", k=2)).then_inc(wT_copied, 1)
            for k in range(2):
                nc.scalar.copy(wkvT[:, k], bank[1 + k][:]).then_inc(wT_copied, 1)
            nc.scalar.copy(wpT[:], bank[3][:].rearrange("p (k c) -> p k c", k=2)).then_inc(wT_copied, 1)
            act.wait_ge(xn_ready, TILES)
            nc.scalar.preload_act_table(ACT.Exp)

            def mix_in(t):
                act.wait_ge(mx_T, t + 1)
                nc.scalar.copy(xn_t[0:TILE], xs[0:TILE, bass.ds(t, 1)].rearrange("p a d -> p (a d)")).then_inc(mx_in, 1)

            def mix_xT(t):
                act.wait_ge(mx_T, t + 2)
                act.wait_ge(mx_q, t + 1)
                nc.scalar.copy(xT_t[:, :, 0:TILE], by_half(bank[7])
                               ).then_inc(mx_xT, 1)

            def mix_exp(t):
                act.wait_ge(mx_kv, t + 1)
                act.wait_ge(mx_k, t + 1)
                act.wait_ge(mx_ctx, t + 1)
                nc.scalar.activation(ek[0:TILE], bank[6][0:TILE, 0:DIM], ACT.Exp).then_inc(mx_ek, 1)
                nc.scalar.copy(v_t[0:TILE], bank[6][0:TILE, DIM:2 * DIM]).then_inc(mx_v, 1)
                act.wait_ge(mx_q, t + 2)
                act.wait_ge(mx_qT, t + 1)
                nc.scalar.activation(eq[:], by_half(bank[7]),
                                     ACT.Exp).then_inc(mx_eq, 1)

            def attn_bias(c):
                for o in range(HALVES):
                    act.wait_ge(ao_ps, 2 * c + o + 1)
                    nc.scalar.activation(qT[:, o, bass.ds(c * COLS, COLS)], bank[6 + o][:, 0:COLS], ACT.Identity,
                                         bias=cvec[:, BPROJ, o:o + 1]).then_inc(ao_ready, 1)

            def edge_pass(n0, r0, phases, fresh):
                if not fresh:
                    for u in range(2):
                        for q in range(PAIRS):
                            act.wait_ge(xg_in[u][q], 32 * r0)
                        nc.scalar.copy(idx_cur[:, u], srcT[:, u]).then_inc(idx_ready, 1)
                copy_edges(act, n0, 0)
                copy_edges(act, n0 + 1, 1)
                relu_messages(act, 0, n0, r0, 0, True)

                def body(i, riders):
                    n = n0 + 2 * i
                    copy_edges(act, n + 2, 0)
                    if riders and riders[0]:
                        riders[0](i)
                    relu_messages(act, 2 * i + 1, n + 1, r0 + i, 1, True)
                    if riders and riders[1]:
                        riders[1](i)
                    copy_edges(act, n + 3, 1)
                    relu_messages(act, 2 * i + 2, n + 2, r0 + i + 1, 0, i_more)
                    if riders and riders[2]:
                        riders[2](i)

                for lo, hi, riders, between in phases:
                    i_more = True
                    if hi == BODIES:
                        with act.Fori(lo, hi - 1) as i:
                            body(i, riders)
                        i_more = False
                        body(hi - 1, riders)
                    else:
                        with act.Fori(lo, hi) as i:
                            body(i, riders)
                    if between:
                        between()
                relu_messages(act, GROUPS - 1, n0 + GROUPS - 1, r0 + BODIES, 1, False)

            def mix_middle(t):
                mix_xT(t)
                mix_exp(t)

            def copy_attn_w():
                act.wait_ge(aw_ps, 1)
                nc.scalar.copy(attn_w[:], bank[6][:].rearrange("p (h c) -> p h c", h=2)).then_inc(aw_ready, 1)

            edge_pass(0, 0, [(0, TILES, (mix_in, mix_middle, None), copy_attn_w),
                             (TILES, TILES + 1, None, None),
                             (TILES + 1, BODIES, (None, lambda i: attn_bias(i - TILES - 1), None), None)], True)
            attn_bias(COL_CHUNKS - 1)
            again = act.value_load(miss_i[0:1, 0:1], min_val=0, max_val=1)
            with act.If(again > 0):
                with act.Fori(0, WINDOWS) as w:
                    edge_pass((w + 1) * GROUPS, (w + 1) * (GROUPS // 2), [(0, BODIES, None, None)], False)
            with act.Else():
                act.nop()

            def mlp1(c, u, fresh):
                for o in range(HALVES):
                    act.wait_ge(z1_ps, 2 * c + o + 1)
                    if not fresh:
                        act.wait_ge(z2_ps, 2 * (c - 1))
                    nc.scalar.activation(z1[:, u, o], bank[o][:, 0:COLS], ACT.Relu, bias=cvec[:, B1, o:o + 1]
                                         ).then_inc(z1_ready, 1)

            def mlp2(c, u):
                for o in range(HALVES):
                    act.wait_ge(z2_ps, 2 * c + o + 1)
                    nc.scalar.activation(hT[:, o, bass.ds(c * COLS, COLS)], bank[2 + o][:, 0:COLS], ACT.Identity,
                                         bias=cvec[:, B2, o:o + 1]).then_inc(z2_ready, 1)

            mlp1(0, 0, True)
            mlp1(1, 1, True)
            mlp2(0, 0)
            with act.Fori(0, (COL_CHUNKS - 3) // 2) as i:
                mlp1(2 * i + 2, 0, False)
                mlp2(2 * i + 1, 1)
                mlp1(2 * i + 3, 1, False)
                mlp2(2 * i + 2, 0)
            mlp1(COL_CHUNKS - 1, 0, False)
            mlp2(COL_CHUNKS - 2, 1)
            mlp2(COL_CHUNKS - 1, 0)
            act.wait_ge(bn_var, 1)
            nc.scalar.activation(bns[:, 1], bns[:, 0], ACT.Sqrt).then_inc(bn_sd, 1)
            act.wait_ge(bn_ready, 1)

            def y_activate(c, u, fresh):
                if not fresh:
                    act.wait_ge(y_T, c - 1)
                for o in range(HALVES):
                    nc.scalar.activation(y_cur[:, u, o], hT[:, o, bass.ds(c * (CHUNK_TILES * TILE), CHUNK_TILES * TILE)],
                                         ACT.Relu, bias=bns[:, 3, o:o + 1], scale=bns[:, 2, o:o + 1]).then_inc(y_relu, 1)

            def normalise(c, r, u, fresh):
                ts_ = bass.ds(c * CHUNK_TILES, CHUNK_TILES)
                act.wait_ge(l2_var, c + 1)
                nc.scalar.activation(ln[0:TILE, 6:8, ts_], ln[0:TILE, 2:4, ts_], ACT.Sqrt).then_inc(l2_sd, 1)
                act.wait_ge(l2_ready, c + 1)
                if not fresh:
                    act.wait_ge(tk_stored[u], 32 * r)
                    act.wait_ge(tk_T, c - 1)
                for k in range(CHUNK_TILES):
                    t = c * CHUNK_TILES + k
                    last = nc.scalar.activation(xn_cur[0:TILE, u, k], xs[0:TILE, bass.ds(t, 1)].rearrange("p a d -> p (a d)"),
                                                ACT.Identity, bias=ln[0:TILE, 5, bass.ds(t, 1)],
                                                scale=ln[0:TILE, 4, bass.ds(t, 1)])
                last.then_inc(tk_ready, 1)

            def copy_rows(c, u, fresh):
                act.wait_ge(tk_T, c + 1)
                if not fresh:
                    act.wait_ge(tk_lg, c - 1)
                flat = xnT[:, u].rearrange("p t h c -> p (t h) c")
                for b, m in enumerate((4, 4, 2)):
                    nc.scalar.copy(flat[:, 4 * b:4 * b + m], bank[4 + b][:, 0:m * TILE].rearrange("p (m c) -> p m c", m=m)
                                   ).then_inc(tk_xT, 1)

            for c in range(2):
                y_activate(c, c, True)
            for c in range(CHUNKS):
                if c + 2 < CHUNKS:
                    y_activate(c + 2, c % 2, False)
                normalise(c, c // 2, c % 2, c < 2)
                if c >= 1:
                    copy_rows(c - 1, (c - 1) % 2, c < 3)
            copy_rows(CHUNKS - 1, (CHUNKS - 1) % 2, False)
            act.wait_ge(gate_in, 1)
            nc.scalar.activation(rs[0:TILE, 3], rs[0:TILE, 2], ACT.Exp).then_inc(gate_exp, 1)
            nc.scalar.preload_act_table(ACT.Gelu)

            act.wait_ge(lists_ready, 1)

            def slot_gelu(j, u):
                for c in range(2):
                    s = hid[:, u, c * 512:(c + 1) * 512]
                    act.wait_ge(hid_b, 2 * j + c + 1)
                    nc.scalar.activation(s, s, ACT.Gelu).then_inc(hid_g, 1)

            def slot_copy(j, fresh):
                act.wait_ge(hidT_ps, 2 * j + 1)
                if not fresh:
                    act.wait_ge(y_ps, j)
                nc.scalar.copy(hidT[:, 0:4], bank[3][:].rearrange("p (k c) -> p k c", k=4)).then_inc(hidT_a, 1)

            def slot_weigh(j, u, fresh):
                act.wait_ge(y_b, j + 1)
                nc.scalar.activation(ys[:, u], ys[:, u], ACT.Identity, scale=slot_f[:, 1, bass.ds(j, 1)]).then_inc(y_w, 1)

            def slot_step(j, u, fresh=False):
                slot_copy(j, fresh)
                slot_gelu(j + 1, 1 - u)
                slot_weigh(j, u, fresh)

            def slots(j0, n):
                slot_gelu(j0, 0)
                slot_step(j0, 0, j0 == 0)
                if n > 4:
                    with act.Fori(0, (n - 4) // 2) as i:
                        slot_step(j0 + 2 * i + 1, 1)
                        slot_step(j0 + 2 * i + 2, 0)
                slot_step(j0 + n - 3, 1)
                slot_step(j0 + n - 2, 0)
                slot_copy(j0 + n - 1, False)
                slot_weigh(j0 + n - 1, 1, False)

            slots(0, MAIN)
            second = act.value_load(more_i[0:1, 0:1], min_val=0, max_val=1)
            with act.If(second > 0):
                slots(MAIN, SLOTS - MAIN)
            with act.Else():
                act.nop()

        @block.vector
        def _(dve):
            step = Chain(dve, dve_chain)
            for s in (mx_rk, mx_ek, mx_v, mx_T, mx_q, mx_k, mx_ctx, mx_qT):
                dve.sem_inc(s, 1)

            def moments_to_ln(chain, t, n):
                s = st[0:TILE, bass.ds(t, n)].rearrange("p t s -> p s t")
                L = ln[0:TILE, :, bass.ds(t, n)]
                chain(nc.vector.tensor_tensor(L[:, 0], s[:, 1], s[:, 4], ALU.subtract))
                chain(nc.vector.tensor_tensor(L[:, 1], s[:, 1], s[:, 4], ALU.add))
                chain(nc.vector.tensor_tensor(L[:, 0], L[:, 0], L[:, 0], ALU.mult))
                chain(nc.vector.tensor_tensor(L[:, 2], s[:, 2], s[:, 5], ALU.add))
                chain(nc.vector.scalar_tensor_tensor(out=L[:, 2], in0=L[:, 2], scalar=4.0 / DIM, in1=L[:, 0],
                                                     op0=ALU.mult, op1=ALU.add))
                chain(nc.vector.tensor_scalar(L[:, 2], L[:, 2], 0.25, LN_EPS, ALU.mult, ALU.add))

            nc.vector.memset(dst_i, FAR).then_inc(ids_memset, 1)
            nc.vector.memset(src_i, 0).then_inc(ids_memset, 1)
            def norm_of_x(c):
                dve.wait_ge(x_in[c], 32)
                ts_ = slice(c * CHUNK_TILES, (c + 1) * CHUNK_TILES)
                for t in range(c * CHUNK_TILES, (c + 1) * CHUNK_TILES):
                    last = nc.vector.bn_stats(st[0:TILE, t], xs[0:TILE, t])
                step(last)
                moments_to_ln(step, c * CHUNK_TILES, CHUNK_TILES)
                dve.sem_inc(var_ready, 1)
                dve.wait_ge(sd_ready, c + 1)
                step(nc.vector.reciprocal(ln[0:TILE, 4, ts_], ln[0:TILE, 3, ts_]))
                nc.vector.scalar_tensor_tensor(out=ln[0:TILE, 5, ts_], in0=ln[0:TILE, 1, ts_], scalar=-0.5,
                                               in1=ln[0:TILE, 4, ts_], op0=ALU.mult, op1=ALU.mult).then_inc(ln_ready, 1)

            norm_of_x(0)
            dve.wait_ge(ids_in, 64)
            step(nc.vector.tensor_copy(dst_f, dst_i))
            step(nc.vector.tensor_reduce(gstat[:, 0:1], dst_f, AX.X, ALU.min))
            step(nc.vector.tensor_scalar(gstat[:, 0:1], gstat[:, 0:1], 0.0, float(NODES - 1), ALU.max, ALU.min))
            step(nc.vector.tensor_scalar(rel, dst_f, gstat[:, 0:1], None, ALU.subtract))
            step(nc.vector.scalar_tensor_tensor(out=src_f, in0=dst_f, scalar=float(FAR), in1=rel,
                                                op0=ALU.is_lt, op1=ALU.mult))
            step(nc.vector.tensor_reduce(gstat[:, 1:2], src_f, AX.X, ALU.max))
            step(nc.vector.tensor_copy(src_f, src_i))
            nc.vector.memset(gstat[:, 2:3], 0.0).then_inc(rel_ready, 1)

            norm_of_x(1)
            dve.wait_ge(consts_made, 8)
            step(nc.vector.tensor_copy(iota_f[:], iota_i[:]))
            step(nc.vector.tensor_copy(part_f[:], part_i[:]))
            step(nc.vector.tensor_copy(tokid[:], tokid_i[:]))
            dve.wait_ge(ids_T, 1)
            nc.vector.tensor_copy(srcT[:], bank[5][:, 0:GT * GROUPS].rearrange("p (j g) -> p g j", j=GT)
                                  ).then_inc(tables_ready, 1)
            step(nc.vector.tensor_copy(relT[:], bank[4][:, 0:GT * GROUPS].rearrange("p (j g) -> p g j", j=GT)))
            step(nc.vector.tensor_copy(base_row[:, 0:GROUPS], bank[6][0:1, 0:GROUPS]))
            step(nc.vector.tensor_reduce(gstat[0:1, 3:4], bank[6][0:1, P:P + GROUPS], AX.X, ALU.max))
            nc.vector.tensor_scalar(miss_i[:], gstat[0:1, 3:4], float(WINDOW), None, ALU.is_ge).then_inc(tables_ready, 1)
            nc.vector.memset(gstat[:, 2:3], 0.0).then_inc(tables_ready, 1)
            dve.wait_ge(tables_ready, 3)
            for c in range(2, CHUNKS):
                norm_of_x(c)
            dve.wait_ge(b_edge_in, 16)
            dve.wait_ge(xn_ready, TILES)
            dve.wait_ge(rows_stored[0], 64)
            dve.wait_ge(rows_ready, CHUNKS - 1)
            nc.vector.tensor_tensor(table_stage[0:TILE, 0], xs[0:TILE, TILES - CHUNK_TILES:TILES],
                                    b_edge[0:TILE].unsqueeze(1).to_broadcast([TILE, CHUNK_TILES, DIM]), ALU.add
                                    ).then_inc(rows_ready, 1)
            dve.wait_ge(consts_in, CONST_DMAS * 16)
            step(nc.vector.tensor_scalar(eps1[:], eps1[:], 1.0, None, ALU.add))
            dve.wait_ge(wT_ready, 1)

            def mix_h(t, h_count):
                dve.wait_ge(mx_xT, t + 1)
                dve.wait_ge(h_updates, h_count)
                w = hT[:, :, bass.ds(t * TILE, TILE)]
                nc.vector.scalar_tensor_tensor(out=w, in0=by_half(bank[7]),
                                               scalar=eps1[:], in1=w, op0=ALU.mult, op1=ALU.add).then_inc(h_updates, 1)

            def mix_elu(t):
                dve.wait_ge(mx_v, t + 2)
                dve.wait_ge(mx_ctx, t + 1)
                dve.wait_ge(mx_kacc, t + 1)
                nc.vector.tensor_scalar(k_t[0:TILE], bank[6][0:TILE, 0:DIM], 0.0, None, ALU.max).then_inc(mx_rk, 1)
                dve.wait_ge(mx_rk, t + 2)
                nc.vector.scalar_tensor_tensor(out=k_t[0:TILE], in0=ek[0:TILE], scalar=1.0, in1=k_t[0:TILE],
                                               op0=ALU.min, op1=ALU.add).then_inc(mx_k, 1)
                dve.wait_ge(mx_kacc, t + 1)
                dve.wait_ge(mx_k, t + 2)
                nc.vector.tensor_tensor(k_acc[0:TILE], k_acc[0:TILE], k_t[0:TILE], ALU.add).then_inc(mx_kacc, 1)
                dve.wait_ge(mx_eq, t + 1)
                dve.wait_ge(mx_qT, t + 1)
                nc.vector.tensor_scalar(rq[:], by_half(bank[7]),
                                        0.0, None, ALU.max).then_inc(mx_rq, 1)
                dve.wait_ge(mx_rq, t + 1)
                nc.vector.scalar_tensor_tensor(out=qT[:, :, bass.ds(t * TILE, TILE)], in0=eq[:], scalar=1.0, in1=rq[:],
                                               op0=ALU.min, op1=ALU.add).then_inc(mx_qT, 1)

            def mix_context(t):
                dve.wait_ge(mx_ctx, t + 2)
                dve.wait_ge(mx_acc, t + 1)
                nc.vector.tensor_tensor(ctx_acc[:], ctx_acc[:], bank[7][:, 0:2 * P], ALU.add).then_inc(mx_acc, 1)

            def mask_context():
                dve.wait_ge(mx_acc, TILES + 1)
                dve.wait_ge(ksum_ps, 1)
                for h in range(HALVES):
                    nc.vector.tensor_tensor(ctx_m[:, h], ctx_acc[:, h * P:(h + 1) * P], blocks[:], ALU.mult
                                            ).then_inc(ctx_masked, 1)
                    nc.vector.tensor_scalar(ksum_m[:, h], blocks[:], bank[7][:, h:h + 1], None, ALU.mult
                                            ).then_inc(ctx_masked, 1)

            def attn_max(c, more):
                dve.wait_ge(den_ps, c + 1)
                if more:
                    dve.wait_ge(qn_ready, c)
                for h in range(HALVES):
                    nc.vector.tensor_scalar(dinv[:, h], bank[6 + h][:, 0:COLS], 1e-6, None, ALU.max).then_inc(den_max, 1)

            def attn_inverse(c, k):
                n = COLS // 2
                d = dinv[:, k // 2, k % 2 * n:(k % 2 + 1) * n]
                dve.wait_ge(den_max, 2 * c + 2)
                nc.vector.reciprocal(d, d).then_inc(den_inv, 1)

            def attn_norm(c, more):
                dve.wait_ge(den_inv, PIECES * (c + 1))
                if more:
                    dve.wait_ge(ao_ps, 2 * c)
                nc.vector.tensor_tensor(qn, dinv, qT[:, :, bass.ds(c * COLS, COLS)], ALU.mult).then_inc(qn_ready, 1)

            def attn_riders(more):
                def first(i):
                    attn_max(i - TILES, more)
                    attn_inverse(i - TILES, 0)
                piece = lambda k: lambda i: attn_inverse(i - TILES, k)
                return (None, first, piece(1), piece(2), piece(3), lambda i: attn_norm(i - TILES, more))

            def edge_pass(n0, r0, start_of, h_of, phases):
                mark_window(dve, 0, 0)
                add_nodes(dve, n0, r0, 0)

                def body(i, riders, per_body, h0, lo):
                    n = n0 + 2 * i
                    h = h0 + (i - lo) * per_body
                    add_nodes(dve, n + 1, r0 + i, 1)
                    mark_window(dve, 2 * i + 1, 1)
                    if riders and riders[1]:
                        riders[1](i)
                    s0 = start_of(2 * i)
                    add_window(dve, n, 0, s0, h)
                    dve.wait_ge(h_updates, h + 1)
                    dve.sem_inc(agg_read, 1)
                    h = h + 1
                    if riders:
                        if riders[0]:
                            riders[0](i, h)
                            h = h + 1
                        if riders[2]:
                            riders[2](i)
                    add_nodes(dve, n + 2, r0 + i + 1, 0)
                    if riders:
                        riders[3](i)
                    mark_window(dve, 2 * i + 2, 0)
                    if riders and riders[4]:
                        riders[4](i)
                    s1 = start_of(2 * i + 1)
                    add_window(dve, n + 1, 1, s1, h)
                    dve.wait_ge(h_updates, h + 1)
                    dve.sem_inc(agg_read, 1)
                    if riders and riders[5]:
                        riders[5](i)

                h0 = h_of
                for lo, hi, riders, between in phases:
                    per_body = 3 if riders and riders[0] else 2
                    with dve.Fori(lo, hi) as i:
                        body(i, riders, per_body, h0, lo)
                    h0 = h0 + (hi - lo) * per_body
                    if between:
                        between()
                n = n0 + GROUPS
                mark_window(dve, GROUPS - 1, 1)
                add_nodes(dve, n - 1, r0 + BODIES, 1)
                for k in range(2):
                    add_window(dve, n - 2 + k, k, start_of(GROUPS - 2 + k), h0 + k)
                    dve.wait_ge(h_updates, h0 + k + 1)
                    dve.sem_inc(agg_read, 1)
                return h0 + 2

            def own_window(g):
                return dve.value_load(base_row[0:1, bass.ds(g, 1)], min_val=0, max_val=NODES - 1)

            dve.sem_inc(agg_read, 1)
            dve.wait_ge(h_updates, 1)
            h_end = edge_pass(0, 0, own_window, 1, [
                (0, TILES, (mix_h, None, None, mix_elu, None, mix_context), mask_context),
                (TILES, TILES + 1, attn_riders(False), None),
                (TILES + 1, BODIES, attn_riders(True), None)])
            again = dve.value_load(miss_i[0:1, 0:1], min_val=0, max_val=1)
            with dve.If(again > 0):
                nc.vector.tensor_scalar(rel, rel, float(WINDOW), None, ALU.is_ge).then_inc(pass_tables, 1)
                dve.wait_ge(pass_tables, 1)
                nc.vector.scalar_tensor_tensor(out=rel, in0=dst_f, scalar=float(4 * FAR), in1=rel,
                                               op0=ALU.add, op1=ALU.mult).then_inc(pass_tables, 1)
                dve.wait_ge(pass_tables, 2)
                nc.vector.tensor_scalar(rel, rel, float(4 * FAR), None, ALU.subtract).then_inc(pass_tables, 1)
                dve.wait_ge(pass_tables, 3)
                dve.wait_ge(pass_T, 1)
                nc.vector.tensor_copy(relT[:], bank[4][:, 0:GT * GROUPS].rearrange("p (j g) -> p g j", j=GT)
                                      ).then_inc(pass_done, 1)
                with dve.Fori(0, WINDOWS) as w:
                    dve.wait_ge(pass_done, w + 1)
                    h1 = h_end + w * GROUPS
                    edge_pass((w + 1) * GROUPS, (w + 1) * (GROUPS // 2), lambda g: w * WINDOW, h1, [(0, BODIES, None, None)])
                    nc.vector.tensor_scalar(relT[:], relT[:], float(WINDOW), None, ALU.subtract).then_inc(pass_done, 1)
            with dve.Else():
                dve.nop()
            nc.vector.memset(eq[:], 0.0).then_inc(edges_done, 1)
            nc.vector.memset(ek[:], 0.0).then_inc(edges_done, 1)

            for c in range(COL_CHUNKS):
                dve.wait_ge(z2_ready, 2 * c + 2)
                for o in range(HALVES):
                    last = nc.vector.bn_stats(bn[:, o, c], hT[:, o, c * COLS:min((c + 1) * COLS, NODES)])
            step(last)
            for o in range(HALVES):
                last = nc.vector.bn_aggr(mv[:, o], bn[:, o])
            step(last)
            nc.vector.tensor_scalar(bns[:, 0], mv[:, :, 1], LN_EPS, None, ALU.add).then_inc(bn_var, 1)
            dve.wait_ge(bn_sd, 1)
            step(nc.vector.reciprocal(bns[:, 1], bns[:, 1]))
            step(nc.vector.tensor_tensor(bns[:, 2], bns[:, 1], cvec[:, GAMMA], ALU.mult))
            step(nc.vector.tensor_tensor(bns[:, 0], bns[:, 2], mv[:, :, 0], ALU.mult))
            nc.vector.tensor_tensor(bns[:, 3], cvec[:, BETA], bns[:, 0], ALU.subtract).then_inc(bn_ready, 1)
            dve.wait_ge(x_again, 32 * CHUNKS)
            def residual(c):
                dve.wait_ge(y_T, c + 1)
                for b, m in enumerate((2, 2, 1)):
                    rows = xs[0:TILE, bass.ds(c * CHUNK_TILES + 2 * b, m)]
                    nc.vector.tensor_tensor(rows, bank[b][0:TILE, 0:m * DIM].rearrange("p (m d) -> p m d", m=m), rows,
                                            ALU.add).then_inc(x1_ready, 1)
                dve.wait_ge(x1_ready, 3 * c + 3)
                for k in range(CHUNK_TILES):
                    t = c * CHUNK_TILES + k
                    last = nc.vector.bn_stats(st[0:TILE, bass.ds(t, 1)].rearrange("p a s -> p (a s)"),
                                              xs[0:TILE, bass.ds(t, 1)].rearrange("p a d -> p (a d)"))
                last.then_inc(x1_stats, 1)
                dve.wait_ge(x1_stats, c + 1)

            def norm_of_rows(c):
                chain = Chain(dve, l2_chain, c * L2_STEPS)
                ts_ = bass.ds(c * CHUNK_TILES, CHUNK_TILES)
                L = [ln[0:TILE, k, ts_] for k in range(8)]
                moments_to_ln(chain, c * CHUNK_TILES, CHUNK_TILES)
                chain(nc.vector.reciprocal(L[3], L[2]))
                chain(nc.vector.scalar_tensor_tensor(out=L[3], in0=L[2], scalar=LN_EPS, in1=L[3],
                                                     op0=ALU.subtract, op1=ALU.mult))
                nc.vector.tensor_scalar(L[3], L[3], LN_EPS, None, ALU.add).then_inc(l2_var, 1)
                dve.wait_ge(l2_sd, c + 1)
                chain(nc.vector.tensor_tensor(L[0], L[6], L[7], ALU.mult))
                chain(nc.vector.reciprocal(L[4], L[0]))
                nc.vector.scalar_tensor_tensor(out=L[5], in0=L[1], scalar=-0.5, in1=L[4],
                                               op0=ALU.mult, op1=ALU.mult).then_inc(l2_ready, 1)
                assert chain.n == L2_STEPS

            def scale_logits(c):
                dve.wait_ge(tk_lg, c + 1)
                back = ln[0:TILE, 7, bass.ds(c * CHUNK_TILES, CHUNK_TILES)].unsqueeze(2).to_broadcast([TILE, CHUNK_TILES, EXPERTS])
                nc.vector.tensor_tensor(logits[0:TILE, bass.ds(c * CHUNK_TILES, CHUNK_TILES)],
                                        bank[(7, 3)[c % 2]][0:TILE, 0:CHUNK_TILES * EXPERTS].rearrange("p (t e) -> p t e", e=EXPERTS),
                                        back, ALU.mult).then_inc(tk_scaled, 1)

            for c in range(CHUNKS):
                residual(c)
                norm_of_rows(c)
                if c >= 3:
                    scale_logits(c - 3)
            for c in range(CHUNKS - 3, CHUNKS - 1):
                scale_logits(c)
            step(nc.vector.tensor_scalar(part_f[:], part_f[:], float(NODES), None, ALU.add))
            step(nc.vector.tensor_scalar(tokid[:], tokid[:], 1.0, None, ALU.add))
            step(nc.vector.tensor_scalar(ex[:, 0], iota_f[:, 0:EXPERTS], -1.0, float(EXPERTS), ALU.mult, ALU.add))
            nc.vector.memset(ej[:], 0.0).then_inc(list_zero, 1)
            scale_logits(CHUNKS - 1)
            dve.wait_ge(tk_scaled, CHUNKS)

            shape = [TILE, TILES, EXPERTS]
            R, S, lg = rt[0:TILE], rs[0:TILE], logits[0:TILE]
            by_t = lambda v: v.unsqueeze(2).to_broadcast(shape)
            by_e = lambda v: v.unsqueeze(1).to_broadcast(shape)
            step(nc.vector.tensor_tensor(lg, lg, by_e(br[0:TILE]), ALU.add))
            for s, src in ((0, lg), (1, R[:, 3])):
                if s == 1:
                    step(nc.vector.scalar_tensor_tensor(out=R[:, 3], in0=R[:, 0], scalar=-1e30, in1=lg,
                                                        op0=ALU.mult, op1=ALU.add))
                step(nc.vector.tensor_reduce(S[:, s], src, AX.X, ALU.max))
                step(nc.vector.tensor_tensor(R[:, 4], src, by_t(S[:, s]), ALU.is_equal))
                step(nc.vector.tensor_tensor(R[:, 4], R[:, 4], by_e(ex[0:TILE, 0]), ALU.mult))
                step(nc.vector.tensor_reduce(S[:, 6], R[:, 4], AX.X, ALU.max))
                step(nc.vector.tensor_tensor(R[:, s], R[:, 4], by_t(S[:, 6]), ALU.is_equal))
            nc.vector.tensor_tensor(R[:, 2], R[:, 0], R[:, 1], ALU.add).then_inc(cnt_ready, 1)
            nc.vector.tensor_tensor(S[:, 2], S[:, 1], S[:, 0], ALU.subtract).then_inc(gate_in, 1)
            dve.wait_ge(gate_exp, 1)
            step(nc.vector.tensor_scalar(S[:, 4], S[:, 3], 1.0, None, ALU.add))
            step(nc.vector.reciprocal(S[:, 4], S[:, 4]))
            step(nc.vector.tensor_tensor(S[:, 5], S[:, 3], S[:, 4], ALU.mult))
            dve.wait_ge(rank_ps, 1)
            total = bank[0][0:TILE, 256:256 + TILES * EXPERTS].rearrange("p (t e) -> p t e", e=EXPERTS)
            rank = bank[0][0:TILE, 0:TILES * EXPERTS].rearrange("p (t e) -> p t e", e=EXPERTS)
            for e in range(EXPERTS):
                last = nc.vector.tensor_tensor_scan(R[:, 5, :, e], ones[0:TILE, 0:TILES], total[:, :, e], 0.0,
                                                    ALU.mult, ALU.add)
            step(last)
            X = ex[0:TILE]
            step(nc.vector.tensor_scalar(X[:, 2], R[:, 5, TILES - 1], float(P - 1), float(P), ALU.add, ALU.max))
            step(nc.vector.tensor_copy(exi[0:TILE], X[:, 2]))
            step(nc.vector.tensor_scalar(exi[0:TILE], exi[0:TILE], 7, None, ALU.logical_shift_right))
            step(nc.vector.tensor_copy(X[:, 3], exi[0:TILE]))
            step(nc.vector.tensor_tensor_scan(X[:, 4], ones[0:TILE, 0:EXPERTS], X[:, 3], 0.0, ALU.mult, ALU.add))
            step(nc.vector.tensor_tensor(X[:, 5], X[:, 4], X[:, 3], ALU.subtract))
            step(nc.vector.tensor_scalar(X[:, 2], X[:, 5], float(P), None, ALU.mult))
            step(nc.vector.tensor_tensor(R[:, 5], R[:, 5], total, ALU.subtract))
            step(nc.vector.tensor_tensor(R[:, 5], R[:, 5], rank, ALU.add))
            step(nc.vector.tensor_tensor(R[:, 5], R[:, 5], by_e(X[:, 2]), ALU.add))
            for s in range(2):
                step(nc.vector.tensor_tensor(R[:, 4], R[:, s], R[:, 5], ALU.mult))
                step(nc.vector.tensor_reduce(S[:, 6], R[:, 4], AX.X, ALU.add))
                step(nc.vector.tensor_copy(rsi[0:TILE, 0], S[:, 6]))
                step(nc.vector.tensor_scalar(rsi[0:TILE, 1], rsi[0:TILE, 0], 7, None, ALU.logical_shift_right))
                step(nc.vector.tensor_copy(S[:, 8 if s == 0 else 1], rsi[0:TILE, 1]))
                step(nc.vector.tensor_scalar(rsi[0:TILE, 1], rsi[0:TILE, 0], P - 1, None, ALU.bitwise_and))
                step(nc.vector.tensor_copy(S[:, 9 if s == 0 else 2], rsi[0:TILE, 1]))
            def mark_slots(c, u, fresh):
                if not fresh:
                    dve.wait_ge(oa_ready, 4 * c - 4)
                    dve.wait_ge(list_step, c - 1)
                ts_ = bass.ds(c * CHUNK_TILES, CHUNK_TILES)
                for s in range(2):
                    narrow = [TILE, CHUNK_TILES, LIST]
                    nc.vector.tensor_tensor(oh[0:TILE, u, s], iota_f[0:TILE, 0:LIST].unsqueeze(1).to_broadcast(narrow),
                                            S[:, (8, 1)[s], ts_].unsqueeze(2).to_broadcast(narrow), ALU.is_equal
                                            ).then_inc(oh_made, 1)
                for s in range(2):
                    wide = [TILE, CHUNK_TILES, P]
                    nc.vector.tensor_tensor(ob[0:TILE, u, s * CHUNK_TILES:(s + 1) * CHUNK_TILES],
                                            iota_f[0:TILE].unsqueeze(1).to_broadcast(wide),
                                            S[:, (9, 2)[s], ts_].unsqueeze(2).to_broadcast(wide), ALU.is_equal
                                            ).then_inc(ob_ready, 1)

            for c in range(CHUNKS):
                mark_slots(c, c % 2, c < 2)
            for e in range(1, EXPERTS):
                step(nc.vector.scalar_tensor_tensor(out=ej[0:1, 0], in0=iota_f[0:1, 0:SLOTS], scalar=ex[0:1, 5, e:e + 1],
                                                    in1=ej[0:1, 0], op0=ALU.is_ge, op1=ALU.add))
            step(nc.vector.tensor_copy(ej_i[:, 3:3 + SLOTS], ej[0:1, 0]))
            step(nc.vector.tensor_copy(first_i[:], ex[0:1, 5]))
            step(nc.vector.tensor_scalar(more_i[:], ex[0:1, 4, EXPERTS - 1:EXPERTS], float(MAIN), None, ALU.is_gt))
            dve.wait_ge(list_step, CHUNKS)
            step(nc.vector.tensor_copy(slot_f[:, 0:2], bank[1][:, 0:2 * LIST].rearrange("p (a s) -> p a s", a=2)))
            step(nc.vector.tensor_scalar(slot_f[:, 2], slot_f[:, 0], 1.0, 0.0, ALU.subtract, ALU.max))
            nc.vector.tensor_copy(tok_i[:], slot_f[:, 2]).then_inc(tok_ready, 1)
            step(nc.vector.tensor_scalar(slot_f[:, 0], slot_f[:, 0], 0.0, part_f[:], ALU.is_equal, ALU.mult))
            step(nc.vector.tensor_tensor(slot_f[:, 0], slot_f[:, 0], slot_f[:, 2], ALU.add))
            nc.vector.tensor_copy(row_i[:], slot_f[:, 0]).then_inc(lists_ready, 1)

            def slot_scale(j, u, e, fresh):
                dve.wait_ge(tok_T, j + 1)
                if not fresh:
                    dve.wait_ge(hid_ps, 2 * (j - 1))
                for k in range(HALVES):
                    g = ln_g[:, bass.ds(e, 1), k]
                    b = ln_b[:, bass.ds(e, 1), k]
                    nc.vector.tensor_scalar(xeT[:, u, k], bank[0][:, k * P:(k + 1) * P], g, b, ALU.mult, ALU.add
                                            ).then_inc(xeT_half, 1)

            def slot_bias(j, u, e, fresh):
                for c in range(2):
                    dve.wait_ge(hid_ps, 2 * j + c + 1)
                    if not fresh:
                        dve.wait_ge(hidT_ps, 2 * (j - 1))
                    b1 = wts[:, bass.ds(e % 2, 1), 4096 + c * 512:4096 + (c + 1) * 512].rearrange("p a c -> p (a c)")
                    nc.vector.tensor_tensor(hid[:, u, c * 512:(c + 1) * 512], bank[1 + c][:], b1, ALU.add).then_inc(hid_b, 1)

            def slot_copy(j, fresh):
                dve.wait_ge(hidT_ps, 2 * j + 2)
                if not fresh:
                    dve.wait_ge(y_ps, j)
                nc.vector.tensor_copy(hidT[:, 4:8], bank[4][:].rearrange("p (k c) -> p k c", k=4)).then_inc(hidT_v, 1)

            def slot_out(j, u, e, fresh):
                dve.wait_ge(y_ps, j + 1)
                if not fresh:
                    dve.wait_ge(row_ready, j)
                b2 = wts[:, bass.ds(e % 2, 1), 5120:5120 + DIM].rearrange("p a c -> p (a c)")
                nc.vector.tensor_tensor(ys[:, u], bank[5][:, 0:DIM], b2, ALU.add).then_inc(y_b, 1)

            def slot_step(j, u, e0, e1, e2, fresh=False):
                slot_copy(j, fresh)
                slot_bias(j + 1, 1 - u, e1, False)
                slot_scale(j + 2, u, e2, False)
                slot_out(j, u, e0, fresh)

            dve.wait_ge(lists_ready, 1)

            def slots(j0, n):
                fresh = j0 == 0
                e0, e1, e2 = experts_of(DVE, j0, 3)
                slot_scale(j0, 0, e0, fresh)
                slot_bias(j0, 0, e0, fresh)
                slot_scale(j0 + 1, 1, e1, fresh)
                slot_step(j0, 0, e0, e1, e2, fresh)
                if n > 4:
                    with dve.Fori(0, (n - 4) // 4) as i:
                        e = experts_of(DVE, j0 + 4 * i + 1, 6)
                        for k in range(4):
                            slot_step(j0 + 4 * i + 1 + k, (k + 1) % 2, e[k], e[k + 1], e[k + 2])
                j = j0 + n - 3
                e0, e1, e2 = experts_of(DVE, j, 3)
                slot_step(j, 1, e0, e1, e2)
                slot_copy(j + 1, False)
                slot_bias(j + 2, 1, e2, False)
                slot_out(j + 1, 0, e1, False)
                slot_copy(j + 2, False)
                slot_out(j + 2, 1, e2, False)

            slots(0, MAIN)
            second = dve.value_load(more_i[0:1, 0:1], min_val=0, max_val=1)
            with dve.If(second > 0):
                slots(MAIN, SLOTS - MAIN)
            with dve.Else():
                dve.nop()


_INS = ['x', 'src', 'dst', 'edge_attr_128', 'L0_gnn_W_edge', 'L0_gnn_b_edge', 'L0_gnn_W1', 'L0_gnn_b1', 'L0_gnn_W2',
        'L0_gnn_b2', 'L0_gnn_eps', 'L0_gnn_gamma', 'L0_gnn_beta', 'L0_mix_Wq', 'L0_mix_Wkv', 'L0_mix_Wproj',
        'L0_mix_bproj', 'L0_ffn_Wr', 'L0_ffn_br', 'L0_ffn_ln_g', 'L0_ffn_ln_b', 'L0_ffn_W1', 'L0_ffn_b1', 'L0_ffn_W2',
        'L0_ffn_b2']


def kernel(**inputs):
    import numpy as _np
    import concourse.bacc as _bacc
    from concourse import mybir as _mybir
    from concourse.bass_utils import run_bass_kernel_spmd as _run

    nc = _bacc.Bacc("TRN2", target_bir_lowering=False, num_devices=1)
    arrays, args = {}, {}
    for name in _INS:
        a = _np.ascontiguousarray(inputs[name])
        arrays[f"in_{name}"] = a
        args[name] = nc.dram_tensor(f"in_{name}", a.shape, _mybir.dt.from_np(a.dtype), kind="ExternalInput").ap()
    out = nc.dram_tensor("out_0", (NODES, DIM), F32, kind="ExternalOutput").ap()
    build(nc, args, out)
    r = _run(nc, [arrays], core_ids=[0])
    return r.results[0]["out_0"]
```

```python
import concourse.bass as bass
from concourse import mybir
from contextlib import ExitStack

F32 = mybir.dt.float32
F32R = mybir.dt.float32r
I32 = mybir.dt.int32
ALU = mybir.AluOpType
ACT = mybir.ActivationFunctionType
AX = mybir.AxisListType
PE = mybir.EngineType.PE
DVE = mybir.EngineType.DVE
ACT_ENGINE = mybir.EngineType.Activation
POOL = mybir.EngineType.Pool

P = 128
NODES, DIM = 3125, 256
EDGES, EDGE_DIM = 50000, 128
EXPERTS, HIDDEN = 8, 1024
HEAD_DIM = 32
HALVES = DIM // P
TILE = 125
TILES = NODES // TILE
CHUNK_TILES = 5
CHUNKS = TILES // CHUNK_TILES
GT = 6
GROUP = GT * P
GROUPS = -(-EDGES // GROUP)
TAIL = EDGES - (GROUPS - 1) * GROUP
PAIRS = GT // 2
PIECES = 4
BODIES = (GROUPS - 2) // 2
WINDOW = P
WINDOWS = -(-NODES // WINDOW)
COLS = 448
COL_CHUNKS = -(-NODES // COLS)
NODES_PAD = COLS * COL_CHUNKS
H_COLS = NODES_PAD + WINDOW
SLOTS = (2 * NODES + EXPERTS * (P - 1)) // P
LIST = P // 2
MAIN = SLOTS - 4
TOKS = 4
W_COLS = HALVES * HIDDEN + HIDDEN // P * DIM
W_PIECE = 1024
W_PIECES = W_COLS // W_PIECE
W_HALF = W_PIECES // 2
CONST_DMAS = 18
L2_STEPS = 10
FAR = 8192
LN_EPS = 1e-5
DMA_ROWS = 112
assert GROUPS % 2 == 0 and SLOTS <= LIST and MAIN % TOKS == 0 and CHUNKS % 2 == 1 and TILES + COL_CHUNKS == BODIES


class Chain:

    def __init__(self, eng, sem, base=0):
        self.eng, self.sem, self.base, self.n = eng, sem, base, 0

    def __call__(self, ins):
        self.n += 1
        ins.then_inc(self.sem, 1)
        self.eng.wait_ge(self.sem, self.base + self.n)


def build(nc, a, out):
    with ExitStack() as ctx:
        def sb(name, shape, dt=F32):
            return ctx.enter_context(nc.sbuf_tensor(name, shape, dt))

        def sem(name):
            return ctx.enter_context(nc.semaphore(name))

        node_table = nc.dram_tensor("node_table", [NODES, DIM], F32).ap()
        token_table = nc.dram_tensor("token_table", [NODES, DIM], F32).ap()
        acc_table = nc.dram_tensor("acc_table", [NODES + P, DIM], F32).ap()

        def next_offset():
            return -(-nc.sbuf_base // 32) * 32

        hT_offset = next_offset()
        hT = sb("hT", [P, HALVES, H_COLS])
        qT = sb("qT", [P, HALVES, NODES_PAD])
        xs = sb("xs", [P, TILES, DIM])
        work_offset = next_offset()
        work = sb("work", [P, 9216])
        wts = sb("wts", [P, 10752])

        def view(t, lo, *dims):
            n = 1
            for d in dims:
                n *= d
            v = t[:, lo:lo + n]
            if len(dims) == 2:
                v = v.rearrange("p (a b) -> p a b", b=dims[1])
            if len(dims) == 3:
                v = v.rearrange("p (a b c) -> p a b c", b=dims[1], c=dims[2])
            return v

        ea = view(work, 0, 2, GT, EDGE_DIM)
        xg = view(work, 1536, 2, GT, DIM)
        msg = view(work, 4608, 2, GT, DIM)
        onehot = view(work, 7680, 2, GT, P)
        table_stage = view(work, 1536, 2, CHUNK_TILES, DIM)
        w_natural = view(work, 6144, 8, DIM)
        z1 = view(work, 0, 2, HALVES, COLS)
        y_cur = view(work, 0, 2, HALVES, CHUNK_TILES * TILE)
        xn_cur = view(work, 2560, 2, CHUNK_TILES, DIM)
        xnT = view(work, 5120, 4 * CHUNK_TILES, TILE).rearrange("p (u t h) c -> p u t h c", u=2, h=HALVES)
        ob = view(work, 6400, 2, 2 * CHUNK_TILES, P)
        oa = view(work, 0, 2, 2 * CHUNK_TILES, P)
        rt = view(work, 0, 6, TILES, EXPERTS)
        oh = work[:, 5120:5120 + 4 * CHUNK_TILES * LIST].rearrange("p (u s t c) -> p u s t c", u=2, s=2, t=CHUNK_TILES)
        tok = view(work, 0, TOKS, DIM)
        xeT = view(work, 1024, 2, HALVES, P)
        hid = view(work, 1536, 2, HIDDEN)
        ys = view(work, 4608, 2, DIM)
        raw = wts[:, 0:W_COLS]
        bias = view(wts, W_COLS, 2, HIDDEN + DIM)
        wsplit = nc.alloc_sbuf_tensor_at("wsplit", [P, 2, 2 * W_COLS], F32R, offset=hT_offset)
        xeT_hi = nc.alloc_sbuf_tensor_at("xeT_hi", [P, 2, HALVES, P], F32R, offset=work_offset + 4 * 5120)
        xeT_lo = nc.alloc_sbuf_tensor_at("xeT_lo", [P, 2, HALVES, P], F32R, offset=work_offset + 4 * 5632)
        hidT_hi = nc.alloc_sbuf_tensor_at("hidT_hi", [P, HIDDEN // P, P], F32R, offset=work_offset + 4 * 6144)
        hidT_lo = nc.alloc_sbuf_tensor_at("hidT_lo", [P, HIDDEN // P, P], F32R, offset=work_offset + 4 * 7168)
        early = wts[:, 5376:]
        dst_i = early[0:GROUPS, 0:GROUP].bitcast(I32)
        dst_f = early[0:GROUPS, 768:768 + GROUP]
        rel = early[0:GROUPS, 1536:1536 + GROUP]
        src_i = early[0:GROUPS, 2304:2304 + GROUP].bitcast(I32)
        src_f = early[0:GROUPS, 3072:3072 + GROUP]
        qn = view(early, 2304, HALVES, COLS)
        dinv = view(early, 3200, 2, HALVES, COLS)

        relT = sb("relT", [P, GROUPS, GT])
        srcT = sb("srcT", [P, GROUPS, GT], I32)
        idx_cur = sb("idx_cur", [P, 2, GT], I32)
        base_row = sb("base_row", [1, P], I32)
        miss_i = sb("miss_i", [1, 1], I32)
        gstat = sb("gstat", [GROUPS, 4])
        w_edge = sb("w_edge", [P, DIM])
        w_hi = sb("w_hi", [P, DIM], F32R)
        w_lo = sb("w_lo", [P, DIM], F32R)
        eaT_hi = sb("eaT_hi", [P, 2, GT, P], F32R)
        eaT_lo = sb("eaT_lo", [P, 2, GT, P], F32R)
        w1 = sb("w1", [P, HALVES, DIM])
        w2 = sb("w2", [P, HALVES, DIM])
        wqT = sb("wqT", [P, HALVES, DIM])
        wkvT = sb("wkvT", [P, HALVES, 2 * DIM])
        wpT = sb("wpT", [P, HALVES, DIM])
        wr = sb("wr", [P, HALVES, EXPERTS])
        br = sb("br", [P, EXPERTS])
        b_edge = sb("b_edge", [P, DIM])
        cvec = sb("cvec", [P, 5, HALVES])
        B1, B2, GAMMA, BETA, BPROJ = range(5)
        eps1 = sb("eps1", [P, 1])
        tiny = sb("tiny", [P, 1])
        ln_g = sb("ln_g", [P, EXPERTS, HALVES])
        ln_b = sb("ln_b", [P, EXPERTS, HALVES])
        iota_i = sb("iota_i", [P, P], I32)
        iota_f = sb("iota_f", [P, P])
        part_i = sb("part_i", [P, 1], I32)
        part_f = sb("part_f", [P, 1])
        ident = sb("ident", [P, P])
        below = sb("below", [P, P])
        ones = sb("ones", [P, P])
        blocks = sb("blocks", [P, P])
        st = sb("st", [P, TILES, 6])
        ln = sb("ln", [P, 8, TILES])
        xn_t = sb("xn_t", [P, DIM])
        xT_t = sb("xT_t", [P, HALVES, P])
        ek = sb("ek", [P, DIM])
        k_t = sb("k_t", [P, DIM])
        v_t = sb("v_t", [P, DIM])
        eq = sb("eq", [P, HALVES, TILE])
        rq = sb("rq", [P, HALVES, TILE])
        ctx_acc = sb("ctx_acc", [P, 2 * P])
        k_acc = sb("k_acc", [P, DIM])
        ctx_m = sb("ctx_m", [P, HALVES, P])
        ksum_m = sb("ksum_m", [P, HALVES, P])
        attn_w = sb("attn_w", [P, HALVES, DIM])
        bn = sb("bn", [P, HALVES, COL_CHUNKS, 6])
        mv = sb("mv", [P, HALVES, 2])
        bns = sb("bns", [P, 4, HALVES])
        logits = sb("logits", [P, TILES, EXPERTS])
        rs = sb("rs", [P, 10, TILES])
        rsi = sb("rsi", [P, 2, TILES], I32)
        ex = sb("ex", [P, 6, EXPERTS])
        exi = sb("exi", [P, EXPERTS], I32)
        tokid = sb("tokid", [P, TILES])
        tokid_i = sb("tokid_i", [P, TILES], I32)
        slot_f = sb("slot_f", [P, 3, LIST])
        tok_i = sb("tok_i", [P, LIST], I32)
        row_i = sb("row_i", [P, LIST], I32)
        ej = sb("ej", [P, 2, SLOTS])
        ej_i = sb("ej_i", [1, SLOTS + 8], I32)
        first_i = sb("first_i", [1, EXPERTS], I32)
        more_i = sb("more_i", [1, 1], I32)
        tokc = sb("tokc", [P, TOKS], I32)
        rowc = sb("rowc", [P, 2], I32)

        bank = [ctx.enter_context(nc.psum_tensor(f"bank{i}", [P, 512], F32)) for i in range(8)]

        x_in = [sem(f"x_in{c}") for c in range(CHUNKS)]
        consts_in = sem("consts_in")
        b_edge_in = sem("b_edge_in")
        ids_in = sem("ids_in")
        pool_chain = sem("pool_chain")
        pool_passed = sem("pool_passed")
        consts_made = sem("consts_made")
        tiny_made = sem("tiny_made")
        dve_chain = sem("dve_chain")
        var_ready = sem("var_ready")
        sd_ready = sem("sd_ready")
        ln_ready = sem("ln_ready")
        xn_ready = sem("xn_ready")
        rows_ready = sem("rows_ready")
        rows_stored = [sem(f"rows_stored{i}") for i in range(2)]
        ids_memset = sem("ids_memset")
        rel_ready = sem("rel_ready")
        base_T = sem("base_T")
        ids_T = sem("ids_T")
        tables_ready = sem("tables_ready")
        wT_ready = sem("wT_ready")
        wT_copied = sem("wT_copied")

        ea_in = [sem(f"ea_in{u}") for u in range(2)]
        ea_tail = sem("ea_tail")
        idx_ready = sem("idx_ready")
        xg_in = [[sem(f"xg_in{u}_{q}") for q in range(PAIRS)] for u in range(2)]
        eaT_ps = sem("eaT_ps")
        w_split = sem("w_split")
        hi_ready = sem("hi_ready")
        eaT_ready = sem("eaT_ready")
        e_ready = sem("e_ready")
        sums_done = sem("sums_done")
        msg_ready = sem("msg_ready")
        onehot_ready = sem("onehot_ready")
        agg_ready = sem("agg_ready")
        h_updates = sem("h_updates")
        agg_read = sem("agg_read")

        mx_in = sem("mx_in")
        mx_T = sem("mx_T")
        mx_xT = sem("mx_xT")
        mx_kv = sem("mx_kv")
        mx_q = sem("mx_q")
        mx_ek = sem("mx_ek")
        mx_v = sem("mx_v")
        mx_eq = sem("mx_eq")
        mx_rk = sem("mx_rk")
        mx_k = sem("mx_k")
        mx_rq = sem("mx_rq")
        mx_qT = sem("mx_qT")
        mx_ctx = sem("mx_ctx")
        mx_acc = sem("mx_acc")
        mx_kacc = sem("mx_kacc")
        ksum_ps = sem("ksum_ps")
        ctx_masked = sem("ctx_masked")
        aw_ps = sem("aw_ps")
        aw_ready = sem("aw_ready")
        den_ps = sem("den_ps")
        den_out = sem("den_out")
        den_inv = sem("den_inv")
        qn_ready = sem("qn_ready")
        ao_ps = sem("ao_ps")
        ao_ready = sem("ao_ready")

        pass_done = sem("pass_done")
        pass_tables = sem("pass_tables")
        pass_T = sem("pass_T")
        edges_done = sem("edges_done")
        x_again = sem("x_again")

        z1_ps = sem("z1_ps")
        z1_ready = sem("z1_ready")
        z2_ps = sem("z2_ps")
        z2_ready = sem("z2_ready")
        bn_var = sem("bn_var")
        bn_sd = sem("bn_sd")
        bn_ready = sem("bn_ready")
        y_relu = sem("y_relu")
        y_sum = sem("y_sum")
        y_T = sem("y_T")
        x1_ready = sem("x1_ready")
        x1_stats = sem("x1_stats")
        x1_stored = sem("x1_stored")
        trash_stored = sem("trash_stored")
        l2_var = sem("l2_var")
        l2_sd = sem("l2_sd")
        l2_chain = sem("l2_chain")
        l2_ready = sem("l2_ready")
        tk_ready = sem("tk_ready")
        tk_stored = [sem(f"tk_stored{i}") for i in range(2)]
        tk_T = sem("tk_T")
        tk_xT = sem("tk_xT")
        tk_lg = sem("tk_lg")
        tk_scaled = sem("tk_scaled")
        gate_in = sem("gate_in")
        gate_exp = sem("gate_exp")
        cnt_ready = sem("cnt_ready")
        rank_ps = sem("rank_ps")
        ob_ready = sem("ob_ready")
        oh_made = sem("oh_made")
        oa_ready = sem("oa_ready")
        list_step = sem("list_step")
        list_zero = sem("list_zero")
        tok_ready = sem("tok_ready")
        lists_ready = sem("lists_ready")

        raw_in = sem("raw_in")
        bias_in = sem("bias_in")
        raw_ready = sem("raw_ready")
        whi_ready = sem("whi_ready")
        wlo_ready = sem("wlo_ready")
        wpool_ready = sem("wpool_ready")
        xe_hi = sem("xe_hi")
        w_ready = sem("w_ready")
        cur_ready = sem("cur_ready")
        tok_in = [sem(f"tok_in{i}") for i in range(TOKS)]
        tok_T = sem("tok_T")
        xeT_half = sem("xeT_half")
        xeT_low = sem("xeT_low")
        hidT_low = sem("hidT_low")
        hidT_high = sem("hidT_high")
        hid_ps = sem("hid_ps")
        hid_b = sem("hid_b")
        hid_g = sem("hid_g")
        hidT_ps = sem("hidT_ps")
        y_ps = sem("y_ps")
        y_b = sem("y_b")
        y_w = sem("y_w")
        row_ready = sem("row_ready")
        acc_in = sem("acc_in")
        out_in = sem("out_in")

        block = ctx.enter_context(nc.Block())

        def by_half(b):
            return b[:, 0:HALVES * P].rearrange("p (h c) -> p h c", h=HALVES)[:, :, 0:TILE]

        def experts_of(engine, j, n):
            return nc.values_load_multi_w_load_instructions(ej_i[0:1, bass.ds(j + 3, n)], engines=(engine,), min_val=0,
                                                            max_val=EXPERTS - 1)[1]

        def node_rows(dram, sbuf, c):
            d = dram[bass.ds(c * CHUNK_TILES * TILE, CHUNK_TILES * TILE), :].rearrange("(t p) d -> p t d", p=TILE)
            return [(d[0:DMA_ROWS], sbuf[0:DMA_ROWS]), (d[DMA_ROWS:TILE], sbuf[DMA_ROWS:TILE])]


        def load_edges(sp, g, n, r, u, fresh):
            if not fresh:
                sp.wait_ge(eaT_ps, 2 * (n - 1))
            rows = a["edge_attr_128"][bass.ds(g * GROUP, GROUP), :].rearrange("(p j) d -> p (j d)", j=GT)
            sp.dma_start(ea[:, u].rearrange("p j d -> p (j d)"), rows).then_inc(ea_in[u], 16)

        def load_tail(sp, n, passes):
            full, rest = TAIL // GT, TAIL % GT
            sp.wait_ge(eaT_ps, 2 * (n - 1))
            start = (GROUPS - 1) * GROUP
            last = a["edge_attr_128"][start + full * GT:start + TAIL, :].rearrange("(p j) d -> p (j d)", j=rest)
            sp.dma_start(ea[full:full + 1, 1, 0:rest, :].rearrange("p j d -> p (j d)"), last).then_inc(ea_tail, 16)
            sp.wait_ge(ea_tail, 16 * (passes + 1))
            rows = a["edge_attr_128"][start:start + full * GT, :].rearrange("(p j) d -> p (j d)", j=GT)
            sp.dma_start(ea[0:full, 1].rearrange("p j d -> p (j d)"), rows).then_inc(ea_in[1], 16)

        def gather_nodes(pool, n, u, fresh):
            pool.wait_ge(idx_ready, n + 1)
            if not fresh:
                pool.wait_ge(sums_done, PAIRS * (n - 1))
            pool.sem_inc(pool_passed, 1)
            for j in range(GT):
                pool.indirect_dma_start(out=xg[:, u, j], out_offset=None, in_=node_table,
                                        in_offset=bass.IndirectOffsetOnAxis(ap=idx_cur[:, u, j:j + 1], axis=0)
                                        ).then_inc(xg_in[u][j // 2], 16)

        def transpose_edges(pe, n, r, u, fresh):
            pe.wait_ge(ea_in[u], 16 * (r + 1))
            for hh in range(2):
                if not fresh:
                    pe.wait_ge(eaT_ready, 2 * (n - 1) + hh + 1)
                for k in range(3):
                    last = nc.tensor.transpose(bank[hh][:, k * P:(k + 1) * P], ea[:, u, 3 * hh + k], ident[:])
                last.then_inc(eaT_ps, 1)

        def embed_edges(pe, n, r, u, fresh):
            for q in range(PAIRS):
                pe.wait_ge(eaT_ready, 2 * n + (1 if q == 0 else 2))
                if not fresh:
                    pe.wait_ge(sums_done, PAIRS * (n - 1) + q + 1)
                b = bank[2 + q]
                for k in range(2):
                    for m, (x, w) in enumerate(((eaT_hi, w_hi), (eaT_hi, w_lo), (eaT_lo, w_hi))):
                        last = nc.tensor.matmul(b[:, k * DIM:(k + 1) * DIM], x[:, u, 2 * q + k], w[:],
                                                start=(m == 0), stop=(m == 2))
                last.then_inc(e_ready, 1)

        def aggregate(pe, n, u):
            b = bank[5]
            pe.wait_ge(agg_read, n + 1)
            pe.wait_ge(onehot_ready, n + 1)
            for j in range(GT):
                if j % 2 == 0:
                    pe.wait_ge(msg_ready, PAIRS * n + j // 2 + 1)
                for h in range(HALVES):
                    last = nc.tensor.matmul(b[:, h * P:(h + 1) * P], msg[:, u, j, h * P:(h + 1) * P], onehot[:, u, j],
                                            start=(j == 0 and h == 0), stop=(j == GT - 1), skip_group_check=True)
            last.then_inc(agg_ready, 1)

        def copy_edges(act, n, u):
            for hh in range(2):
                act.wait_ge(eaT_ps, 2 * n + hh + 1)
                nc.scalar.copy(eaT_hi[:, u, 3 * hh:3 * hh + 3], bank[hh][:, 0:3 * P].rearrange("p (k c) -> p k c", k=3)
                               ).then_inc(hi_ready, 1)

        def split_edges(dve, n, u):
            for hh in range(2):
                dve.wait_ge(hi_ready, 2 * n + hh + 1)
                nc.vector.tensor_tensor(eaT_lo[:, u, 3 * hh:3 * hh + 3], bank[hh][:, 0:3 * P].rearrange("p (k c) -> p k c", k=3),
                                        eaT_hi[:, u, 3 * hh:3 * hh + 3].bitcast(F32), ALU.subtract).then_inc(eaT_ready, 1)

        def relu_messages(act, g, n, r, u, more):
            if more:
                for q in range(PAIRS):
                    act.wait_ge(xg_in[u][q], 32 * (r + 1))
                nc.scalar.copy(idx_cur[:, u], srcT[:, bass.ds(g + 2, 1)].rearrange("p a j -> p (a j)")
                               ).then_inc(idx_ready, 1)
            for q in range(PAIRS):
                act.wait_ge(sums_done, PAIRS * n + q + 1)
                nc.scalar.activation(msg[:, u, 2 * q:2 * q + 2], msg[:, u, 2 * q:2 * q + 2], ACT.Relu
                                     ).then_inc(msg_ready, 1)

        def mark_window(dve, g, u):
            nc.vector.tensor_tensor(onehot[:, u], iota_f[:].unsqueeze(1).to_broadcast([P, GT, P]),
                                    relT[:, bass.ds(g, 1)].rearrange("p a j -> p (a j)").unsqueeze(2).to_broadcast([P, GT, P]),
                                    ALU.is_equal).then_inc(onehot_ready, 1)

        def add_nodes(dve, n, r, u):
            for q in range(PAIRS):
                dve.wait_ge(e_ready, PAIRS * n + q + 1)
                dve.wait_ge(xg_in[u][q], 32 * (r + 1))
                nc.vector.tensor_tensor(msg[:, u, 2 * q:2 * q + 2],
                                        bank[2 + q][:].rearrange("p (k c) -> p k c", k=2),
                                        xg[:, u, 2 * q:2 * q + 2], ALU.add).then_inc(sums_done, 1)

        def add_window(dve, n, u, start, h_count):
            dve.wait_ge(agg_ready, n + 1)
            dve.wait_ge(h_updates, h_count)
            w = hT[:, :, bass.ds(start, WINDOW)]
            nc.vector.tensor_tensor(w, bank[5][:, 0:HALVES * P].rearrange("p (h c) -> p h c", h=HALVES),
                                    w, ALU.add).then_inc(h_updates, 1)

        def load_weights(sp, e):
            sp.dma_start(view(raw, 0, HALVES, HIDDEN), a["L0_ffn_W1"][e].rearrange("(k p) h -> p k h", p=P)
                         ).then_inc(raw_in, 16)
            sp.dma_start(view(raw, 2048, HIDDEN // P, DIM), a["L0_ffn_W2"][e].rearrange("(c p) d -> p c d", p=P)
                         ).then_inc(raw_in, 16)

        def load_biases(sp, e):
            sp.dma_start(bias[:, e % 2, 0:HIDDEN], a["L0_ffn_b1"][e].partition_broadcast(P)).then_inc(bias_in, 16)
            sp.dma_start(bias[:, e % 2, HIDDEN:HIDDEN + DIM], a["L0_ffn_b2"][e].partition_broadcast(P)).then_inc(bias_in, 16)

        def piece(q):
            return slice(q * W_PIECE, (q + 1) * W_PIECE)

        def split_piece(e, q, low):
            lo = (W_COLS if low else 0) + piece(q).start
            return wsplit[:, bass.ds(e % 2, 1), lo:lo + W_PIECE].rearrange("p a c -> p (a c)")

        @block.sync
        def _(sp):
            def load_x(c):
                for d, s in node_rows(a["x"], xs[:, c * CHUNK_TILES:(c + 1) * CHUNK_TILES], c):
                    sp.dma_start(s, d).then_inc(x_in[c], 16)

            load_x(0)
            sp.wait_ge(ids_memset, 2)
            for name, t in (("dst", dst_i), ("src", src_i)):
                v = a[name]
                full = (GROUPS - 1) * GROUP
                sp.dma_start(t[0:GROUPS - 1], v[0:full].rearrange("(g e) -> g e", e=GROUP)).then_inc(ids_in, 16)
                sp.dma_start(t[GROUPS - 1:GROUPS, 0:TAIL], v[full:EDGES].unsqueeze(0)).then_inc(ids_in, 16)
            for c in range(1, CHUNKS):
                load_x(c)
            load_edges(sp, 0, 0, 0, 0, True)
            load_edges(sp, 1, 1, 0, 1, True)
            loads = [
                (eps1[:], a["L0_gnn_eps"].partition_broadcast(P)),
                (wr[:], a["L0_ffn_Wr"].rearrange("(k p) e -> p k e", p=P)),
                (br[:], a["L0_ffn_br"].partition_broadcast(P)),
            ]
            for n, name in enumerate(("L0_gnn_b1", "L0_gnn_b2", "L0_gnn_gamma", "L0_gnn_beta", "L0_mix_bproj")):
                loads.append((cvec[:, n], a[name].rearrange("(h p) -> p h", p=P)))
            for t, name in ((ln_g, "L0_ffn_ln_g"), (ln_b, "L0_ffn_ln_b")):
                for h in range(HALVES):
                    loads.append((t[:, :, h], a[name][:, h * P:(h + 1) * P].rearrange("e p -> p e")))
            assert len(loads) + 6 == CONST_DMAS
            with nc.allow_non_contiguous_dma(reason="small columns of constants"):
                for s, d in loads:
                    sp.dma_start(s, d).then_inc(consts_in, 16)
            for c in range(CHUNKS):
                sp.wait_ge(rows_ready, c + 1)
                for d, s in node_rows(node_table, table_stage[:, c % 2], c):
                    sp.dma_start(d, s).then_inc(rows_stored[c % 2], 16)
            load_weights(sp, 0)
            load_biases(sp, 0)

            with sp.Fori(0, BODIES - 1) as i:
                load_edges(sp, 2 * i + 2, 2 * i + 2, i + 1, 0, False)
                load_edges(sp, 2 * i + 3, 2 * i + 3, i + 1, 1, False)
            load_edges(sp, GROUPS - 2, GROUPS - 2, BODIES, 0, False)
            load_tail(sp, GROUPS - 1, 0)
            sp.wait_ge(mx_in, TILES)
            for c in range(CHUNKS):
                for d, s in node_rows(a["x"], xs[:, c * CHUNK_TILES:(c + 1) * CHUNK_TILES], c):
                    sp.dma_start(s, d).then_inc(x_again, 16)

            sp.wait_ge(tables_ready, 3)
            again = sp.value_load(miss_i[0:1, 0:1], min_val=0, max_val=1)
            with sp.If(again > 0):
                with sp.Fori(0, WINDOWS) as w:
                    n0 = (w + 1) * GROUPS
                    r0 = (w + 1) * (GROUPS // 2)
                    load_edges(sp, 0, n0, r0, 0, False)
                    load_edges(sp, 1, n0 + 1, r0, 1, False)
                    with sp.Fori(0, BODIES - 1) as i:
                        load_edges(sp, 2 * i + 2, n0 + 2 * i + 2, r0 + i + 1, 0, False)
                        load_edges(sp, 2 * i + 3, n0 + 2 * i + 3, r0 + i + 1, 1, False)
                    load_edges(sp, GROUPS - 2, n0 + GROUPS - 2, r0 + BODIES, 0, False)
                    load_tail(sp, n0 + GROUPS - 1, w + 1)
            with sp.Else():
                sp.nop()
            sp.wait_ge(edges_done, 2)
            load_biases(sp, 1)
            sp.dma_start(acc_table[NODES:NODES + P, :], ek[:]).then_inc(trash_stored, 16)
            def store_rows(c, u):
                sp.wait_ge(x1_ready, 3 * c + 3)
                for d, s in node_rows(acc_table, xs[:, bass.ds(c * CHUNK_TILES, CHUNK_TILES)], c):
                    sp.dma_start(d, s).then_inc(x1_stored, 16)
                sp.wait_ge(tk_ready, c + 1)
                for d, s in node_rows(token_table, xn_cur[:, u], c):
                    sp.dma_start(d, s).then_inc(tk_stored[u], 16)

            for c in range(CHUNKS):
                store_rows(c, c % 2)
            for e in range(EXPERTS):
                if e >= 1:
                    sp.wait_ge(wlo_ready, W_HALF * e)
                    sp.wait_ge(wpool_ready, W_HALF * e)
                    load_weights(sp, e)
                sp.wait_ge(raw_in, 32 * (e + 1))
                sp.sem_inc(raw_ready, 1)
                if e == 2:
                    sp.wait_ge(lists_ready, 1)
                if e >= 2:
                    done = sp.value_load(first_i[0:1, e - 1:e], min_val=1, max_val=SLOTS)
                    sp.wait_ge(y_b, done)
                    load_biases(sp, e)
                sp.wait_ge(bias_in, 32 * max(e + 1, 2))
                sp.sem_inc(w_ready, 1)
            sp.sem_inc(raw_ready, 1)
            sp.wait_ge(acc_in, 16 * MAIN)
            second = sp.value_load(more_i[0:1, 0:1], min_val=0, max_val=1)
            with sp.If(second > 0):
                sp.wait_ge(acc_in, 16 * SLOTS)
            with sp.Else():
                sp.nop()
            sp.dma_start(out.rearrange("n d -> (n d)").rearrange("(r c) -> r c", r=80),
                         acc_table[0:NODES, :].rearrange("n d -> (n d)").rearrange("(r c) -> r c", r=80)
                         ).then_inc(out_in, 16)
            sp.wait_ge(out_in, 16)

        @block.gpsimd
        def _(pool):
            step = Chain(pool, pool_chain)
            nc.gpsimd.iota(iota_i[:], pattern=[[1, P]], base=0, channel_multiplier=0).then_inc(consts_made, 1)
            nc.gpsimd.iota(part_i[:], pattern=[[1, 1]], base=0, channel_multiplier=1).then_inc(consts_made, 1)
            nc.gpsimd.iota(tokid_i[:], pattern=[[TILE, TILES]], base=0, channel_multiplier=1).then_inc(consts_made, 1)
            step(nc.gpsimd.memset(ident[:], 0.0))
            nc.gpsimd.affine_select(out=ident[:], in_=ident[:], compare_op=ALU.not_equal, fill=1.0, base=0,
                                    pattern=[[-1, P]], channel_multiplier=1).then_inc(consts_made, 1)
            nc.gpsimd.memset(ones[:], 1.0).then_inc(consts_made, 1)
            step(nc.gpsimd.memset(below[:], 1.0))
            nc.gpsimd.affine_select(out=below[:], in_=below[:], compare_op=ALU.is_gt, fill=0.0, base=0,
                                    pattern=[[1, P]], channel_multiplier=-1).then_inc(consts_made, 1)
            step(nc.gpsimd.memset(blocks[:], 0.0))
            for b in range(P // HEAD_DIM):
                s = slice(b * HEAD_DIM, (b + 1) * HEAD_DIM)
                step(nc.gpsimd.memset(blocks[s, s], 1.0))
            nc.gpsimd.memset(xT_t[:], 0.0).then_inc(consts_made, 1)
            nc.gpsimd.memset(tiny[:], 1e-30).then_inc(tiny_made, 1)
            nc.gpsimd.memset(qT[:, :, NODES:NODES_PAD], 0.0).then_inc(consts_made, 1)
            nc.gpsimd.memset(hT[:], 0.0).then_inc(h_updates, 1)
            nc.gpsimd.memset(ctx_acc[:], 0.0).then_inc(mx_acc, 1)
            nc.gpsimd.memset(k_acc[:], 0.0).then_inc(mx_kacc, 1)

            pool.wait_ge(b_edge_in, 16)
            for c in range(CHUNKS - 1):
                pool.wait_ge(xn_ready, CHUNK_TILES * (c + 1))
                if c >= 2:
                    pool.wait_ge(rows_stored[c % 2], 32 * (c // 2))
                nc.gpsimd.tensor_tensor(table_stage[0:TILE, c % 2], xs[0:TILE, c * CHUNK_TILES:(c + 1) * CHUNK_TILES],
                                        b_edge[0:TILE].unsqueeze(1).to_broadcast([TILE, CHUNK_TILES, DIM]), ALU.add
                                        ).then_inc(rows_ready, 1)
            for c in range(2):
                pool.wait_ge(rows_stored[c], 32 * ((CHUNKS + 1 - c) // 2))
            gather_nodes(pool, 0, 0, True)
            gather_nodes(pool, 1, 1, True)
            with pool.Fori(0, BODIES) as i:
                gather_nodes(pool, 2 * i + 2, 0, False)
                gather_nodes(pool, 2 * i + 3, 1, False)
            pool.wait_ge(tables_ready, 3)
            again = pool.value_load(miss_i[0:1, 0:1], min_val=0, max_val=1)
            with pool.If(again > 0):
                with pool.Fori(0, WINDOWS) as w:
                    n0 = (w + 1) * GROUPS
                    gather_nodes(pool, n0, 0, False)
                    gather_nodes(pool, n0 + 1, 1, False)
                    with pool.Fori(0, BODIES) as i:
                        gather_nodes(pool, n0 + 2 * i + 2, 0, False)
                        gather_nodes(pool, n0 + 2 * i + 3, 1, False)
            with pool.Else():
                pool.nop()

            def add_attention(c, u):
                pool.wait_ge(y_relu, 2 * c + 2)
                nc.gpsimd.tensor_tensor(y_cur[:, u], y_cur[:, u], qT[:, :, bass.ds(c * (CHUNK_TILES * TILE), CHUNK_TILES * TILE)],
                                        ALU.add).then_inc(y_sum, 1)

            for c in range(CHUNKS):
                add_attention(c, c % 2)

            def split_weights(e):
                for q in range(W_HALF, W_PIECES):
                    pool.wait_ge(whi_ready, W_PIECES * e + q + 1)
                    nc.gpsimd.tensor_tensor(split_piece(e, q, True), raw[:, piece(q)], split_piece(e, q, False).bitcast(F32),
                                            ALU.subtract).then_inc(wpool_ready, 1)

            pool.wait_ge(y_sum, CHUNKS)
            for q in range(W_HALF):
                pool.wait_ge(whi_ready, q + 1)
                nc.gpsimd.tensor_tensor(split_piece(0, q, True), raw[:, piece(q)], split_piece(0, q, False).bitcast(F32),
                                        ALU.subtract).then_inc(wlo_ready, 1)
            split_weights(0)

            def weigh_slots(c, u, fresh):
                if not fresh:
                    pool.wait_ge(list_step, c - 1)
                ts_ = bass.ds(c * CHUNK_TILES, CHUNK_TILES)
                for s in range(2):
                    o = oa[0:TILE, u, s * CHUNK_TILES:(s + 1) * CHUNK_TILES]
                    pool.wait_ge(oh_made, 2 * c + s + 1)
                    for k, v in enumerate((tokid[0:TILE, ts_], rs[0:TILE, (4, 5)[s], ts_])):
                        nc.gpsimd.tensor_tensor(o[:, :, k * LIST:(k + 1) * LIST], oh[0:TILE, u, s],
                                                v.unsqueeze(2).to_broadcast([TILE, CHUNK_TILES, LIST]), ALU.mult
                                                ).then_inc(oa_ready, 1)

            for c in range(CHUNKS):
                weigh_slots(c, c % 2, c < 2)

            for u in range(2):
                pool.wait_ge(tk_stored[u], 32 * ((CHUNKS + 1 - u) // 2))
            pool.wait_ge(x1_stored, 32 * CHUNKS)
            pool.wait_ge(trash_stored, 16)
            pool.wait_ge(tok_ready, 1)

            def fetch(j, r, u, fresh):
                pool.wait_ge(tok_in[u], 16 * r)
                nc.gpsimd.tensor_copy(tokc[:, u:u + 1], tok_i[:, bass.ds(j, 1)]).then_inc(cur_ready, 1)
                pool.wait_ge(cur_ready, j + 1)
                if not fresh:
                    pool.wait_ge(tok_T, j - TOKS + 1)
                pool.sem_inc(pool_passed, 1)
                pool.indirect_dma_start(out=tok[:, u], out_offset=None, in_=token_table,
                                        in_offset=bass.IndirectOffsetOnAxis(ap=tokc[:, u:u + 1], axis=0)
                                        ).then_inc(tok_in[u], 16)

            def put(j, u, fresh=False):
                if not fresh:
                    pool.wait_ge(acc_in, 16 * j)
                nc.gpsimd.tensor_copy(rowc[:, u:u + 1], row_i[:, bass.ds(j, 1)]).then_inc(row_ready, 1)
                pool.wait_ge(row_ready, j + 1)
                pool.wait_ge(y_w, j + 1)
                pool.sem_inc(pool_passed, 1)
                pool.indirect_dma_start(out=acc_table, out_offset=bass.IndirectOffsetOnAxis(ap=rowc[:, u:u + 1], axis=0),
                                        in_=ys[:, u], in_offset=None, compute_op=ALU.add).then_inc(acc_in, 16)

            for k in range(TOKS):
                fetch(k, 0, k, True)
            pool.wait_ge(lists_ready, 1)

            def split_where_new(e_last, e_here):
                with pool.If(e_here > e_last):
                    split_weights(e_here + 1)
                with pool.Else():
                    pool.nop()

            e = experts_of(POOL, 0, TOKS)
            for k in range(TOKS):
                fetch(TOKS + k, 1, k, False)
                if k == 0:
                    split_weights(e[0] + 1)
                else:
                    split_where_new(e[k - 1], e[k])
                put(k, k % 2, k == 0)
            with pool.Fori(1, MAIN // TOKS - 1) as i:
                e = experts_of(POOL, TOKS * i - 1, TOKS + 1)
                for k in range(TOKS):
                    fetch(TOKS * (i + 1) + k, i + 1, k, False)
                    split_where_new(e[k], e[k + 1])
                    put(TOKS * i + k, k % 2)
            e = experts_of(POOL, MAIN - TOKS - 1, TOKS + 1)
            for k in range(TOKS):
                split_where_new(e[k], e[k + 1])
                put(MAIN - TOKS + k, k % 2)
            second = pool.value_load(more_i[0:1, 0:1], min_val=0, max_val=1)
            with pool.If(second > 0):
                e = experts_of(POOL, MAIN - 1, TOKS + 1)
                for k in range(TOKS):
                    fetch(MAIN + k, MAIN // TOKS, k, False)
                for k in range(TOKS):
                    split_where_new(e[k], e[k + 1])
                    put(MAIN + k, k % 2)
            with pool.Else():
                pool.nop()

        @block.tensor
        def _(pe):
            pe.wait_ge(consts_made, 8)
            pe.wait_ge(rel_ready, 1)
            nc.tensor.transpose(bank[6][0:1, 0:GROUPS], gstat[:, 0:1], ident[0:GROUPS, 0:GROUPS])
            nc.tensor.transpose(bank[6][0:1, P:P + GROUPS], gstat[:, 1:2], ident[0:GROUPS, 0:GROUPS]).then_inc(base_T, 1)
            for j in range(GT):
                nc.tensor.transpose(bank[4][:, j * GROUPS:(j + 1) * GROUPS], rel[:, j:GROUP:GT], ident[0:GROUPS, 0:GROUPS])
            for j in range(GT):
                last = nc.tensor.transpose(bank[5][:, j * GROUPS:(j + 1) * GROUPS], src_f[:, j:GROUP:GT], ident[0:GROUPS, 0:GROUPS])
            last.then_inc(ids_T, 1)
            pe.wait_ge(consts_in, CONST_DMAS * 16)
            for rb in range(8):
                for k in range(HALVES):
                    if rb < 2:
                        o = bank[0][:, k * 256 + rb * P:k * 256 + (rb + 1) * P]
                    elif rb < 6:
                        o = bank[1 + k][:, (rb - 2) * P:(rb - 1) * P]
                    else:
                        o = bank[3][:, k * 256 + (rb - 6) * P:k * 256 + (rb - 5) * P]
                    last = nc.tensor.transpose(o, w_natural[:, rb, k * P:(k + 1) * P], ident[:])
            last.then_inc(wT_ready, 1)
            pe.wait_ge(wT_copied, 4)
            pe.wait_ge(w_split, 2)
            pe.wait_ge(tables_ready, 3)

            def mix_transpose(t):
                pe.wait_ge(mx_in, t + 1)
                pe.wait_ge(mx_acc, t + 1)
                for k in range(HALVES):
                    last = nc.tensor.transpose(bank[7][:, k * P:k * P + TILE], xn_t[0:TILE, k * P:(k + 1) * P],
                                               ident[0:TILE, 0:TILE])
                last.then_inc(mx_T, 1)

            def mix_qkv(t):
                pe.wait_ge(mx_xT, t + 1)
                pe.wait_ge(mx_rk, t + 1)
                pe.wait_ge(mx_ek, t + 1)
                pe.wait_ge(mx_v, t + 1)
                for k in range(HALVES):
                    last = nc.tensor.matmul(bank[6][0:TILE, :], xT_t[:, k, 0:TILE], wkvT[:, k], start=(k == 0), stop=(k == 1))
                last.then_inc(mx_kv, 1)
                pe.wait_ge(h_updates, 3 * t + 3)
                for o in range(HALVES):
                    for k in range(HALVES):
                        last = nc.tensor.matmul(bank[7][:, o * P:(o + 1) * P], wqT[:, k, o * P:(o + 1) * P],
                                                xT_t[:, k], start=(k == 0), stop=(k == 1))
                last.then_inc(mx_q, 1)

            def mix_context(t):
                pe.wait_ge(mx_k, t + 2)
                pe.wait_ge(mx_v, t + 2)
                pe.wait_ge(mx_rq, t + 1)
                for h in range(HALVES):
                    s = slice(h * P, (h + 1) * P)
                    last = nc.tensor.matmul(bank[7][:, h * P:(h + 1) * P], v_t[0:TILE, s], k_t[0:TILE, s],
                                            start=True, stop=True)
                last.then_inc(mx_ctx, 1)

            def attn_den(c, more):
                if more:
                    pe.wait_ge(ao_ready, 2 * c - 2)
                for h in range(HALVES):
                    last = nc.tensor.matmul(bank[6 + h][:, 0:COLS], ksum_m[:, h], qT[:, h, bass.ds(c * COLS, COLS)],
                                            start=True, stop=True)
                last.then_inc(den_ps, 1)

            def attn_out(c, more):
                pe.wait_ge(qn_ready, c + 2)
                if more:
                    pe.wait_ge(den_out, 2 * (c + 2))
                for o in range(HALVES):
                    for h in range(HALVES):
                        last = nc.tensor.matmul(bank[6 + o][:, 0:COLS], attn_w[:, h, o * P:(o + 1) * P], qn[:, h],
                                                start=(h == 0), stop=(h == 1))
                    last.then_inc(ao_ps, 1)

            def edge_pass(n0, r0, fresh, phases):
                transpose_edges(pe, n0, r0, 0, fresh)
                transpose_edges(pe, n0 + 1, r0, 1, False)
                embed_edges(pe, n0, r0, 0, fresh)

                def body(i, riders):
                    n = n0 + 2 * i
                    transpose_edges(pe, n + 2, r0 + i + 1, 0, False)
                    embed_edges(pe, n + 1, r0 + i, 1, False)
                    if riders and riders[0]:
                        riders[0](i)
                    aggregate(pe, n, 0)
                    if riders and riders[1]:
                        riders[1](i)
                    transpose_edges(pe, n + 3, r0 + i + 1, 1, False)
                    embed_edges(pe, n + 2, r0 + i + 1, 0, False)
                    aggregate(pe, n + 1, 1)
                    if riders and riders[2]:
                        riders[2](i)

                for lo, hi, riders, between in phases:
                    with pe.Fori(lo, hi) as i:
                        body(i, riders)
                    if between:
                        between()
                n = n0 + GROUPS
                embed_edges(pe, n - 1, r0 + BODIES, 1, False)
                aggregate(pe, n - 2, 0)
                aggregate(pe, n - 1, 1)

            def attn_weights():
                pe.wait_ge(mx_kacc, TILES + 1)
                pe.wait_ge(mx_acc, TILES + 1)
                for h in range(HALVES):
                    last = nc.tensor.matmul(bank[7][:, h:h + 1], k_acc[0:TILE, h * P:(h + 1) * P], ones[0:TILE, 0:1],
                                            start=True, stop=True)
                last.then_inc(ksum_ps, 1)
                pe.wait_ge(ctx_masked, 4)
                pe.wait_ge(mx_rk, TILES + 1)
                pe.wait_ge(mx_ek, TILES + 1)
                pe.wait_ge(mx_v, TILES + 1)
                for h in range(HALVES):
                    last = nc.tensor.matmul(bank[6][:, h * DIM:(h + 1) * DIM], ctx_m[:, h], wpT[:, h], start=True, stop=True)
                last.then_inc(aw_ps, 1)
                pe.wait_ge(aw_ready, 1)
                attn_den(0, False)

            edge_pass(0, 0, True, [
                (0, TILES, (mix_transpose, mix_qkv, mix_context), attn_weights),
                (TILES, TILES + 1, (None, None, lambda i: attn_den(1, False)), None),
                (TILES + 1, BODIES - 1, (None, lambda i: attn_out(i - TILES - 1, True),
                                         lambda i: attn_den(i - TILES + 1, True)), None),
                (BODIES - 1, BODIES, (None, lambda i: attn_out(COL_CHUNKS - 2, True), None), None)])
            attn_out(COL_CHUNKS - 1, False)
            again = pe.value_load(miss_i[0:1, 0:1], min_val=0, max_val=1)
            with pe.If(again > 0):
                pe.wait_ge(pass_tables, 3)
                for j in range(GT):
                    last = nc.tensor.transpose(bank[4][:, j * GROUPS:(j + 1) * GROUPS], rel[:, j:GROUP:GT], ident[0:GROUPS, 0:GROUPS])
                last.then_inc(pass_T, 1)
                pe.wait_ge(pass_done, 1)
                with pe.Fori(0, WINDOWS) as w:
                    edge_pass((w + 1) * GROUPS, (w + 1) * (GROUPS // 2), False, [(0, BODIES, None, None)])
            with pe.Else():
                pe.nop()

            pe.wait_ge(edges_done, 2)

            def mlp1(c, u, fresh):
                for o in range(HALVES):
                    if not fresh:
                        pe.wait_ge(z1_ready, 2 * (c - 1) + o + 1)
                    for k in range(HALVES):
                        last = nc.tensor.matmul(bank[o][:, 0:COLS], w1[:, k, o * P:(o + 1) * P],
                                                hT[:, k, bass.ds(c * COLS, COLS)], start=(k == 0), stop=(k == 1))
                    last.then_inc(z1_ps, 1)

            def mlp2(c, u, fresh):
                pe.wait_ge(z1_ready, 2 * c + 2)
                for o in range(HALVES):
                    if not fresh:
                        pe.wait_ge(z2_ready, 2 * (c - 1) + o + 1)
                    for k in range(HALVES):
                        last = nc.tensor.matmul(bank[2 + o][:, 0:COLS], w2[:, k, o * P:(o + 1) * P], z1[:, u, k],
                                                start=(k == 0), stop=(k == 1))
                    last.then_inc(z2_ps, 1)

            mlp1(0, 0, True)
            mlp1(1, 1, False)
            mlp2(0, 0, True)
            with pe.Fori(0, (COL_CHUNKS - 3) // 2) as i:
                mlp1(2 * i + 2, 0, False)
                mlp2(2 * i + 1, 1, False)
                mlp1(2 * i + 3, 1, False)
                mlp2(2 * i + 2, 0, False)
            mlp1(COL_CHUNKS - 1, 0, False)
            mlp2(COL_CHUNKS - 2, 1, False)
            mlp2(COL_CHUNKS - 1, 0, False)

            def y_transpose(c, u, fresh):
                pe.wait_ge(y_sum, c + 1)
                if not fresh:
                    pe.wait_ge(x1_ready, 3 * c)
                for k in range(CHUNK_TILES):
                    for h in range(HALVES):
                        last = nc.tensor.transpose(bank[k // 2][0:TILE, (k % 2) * DIM + h * P:(k % 2) * DIM + (h + 1) * P],
                                                   y_cur[:, u, h, k * TILE:(k + 1) * TILE], ident[:])
                last.then_inc(y_T, 1)

            def row_transpose(c, u, fresh):
                pe.wait_ge(tk_ready, c + 1)
                if not fresh:
                    pe.wait_ge(tk_xT, 3 * c)
                for k in range(2 * CHUNK_TILES):
                    t, h = k // 2, k % 2
                    last = nc.tensor.transpose(bank[4 + k // 4][:, (k % 4) * TILE:(k % 4 + 1) * TILE],
                                               xn_cur[0:TILE, u, t, h * P:(h + 1) * P], ident[0:TILE, 0:TILE])
                last.then_inc(tk_T, 1)

            def route(c, u, fresh):
                pe.wait_ge(tk_xT, 3 * c + 3)
                if not fresh:
                    pe.wait_ge(tk_scaled, c - 1)
                for t in range(CHUNK_TILES):
                    for h in range(HALVES):
                        last = nc.tensor.matmul(bank[(7, 3)[u]][0:TILE, t * EXPERTS:(t + 1) * EXPERTS], xnT[:, u, t, h], wr[:, h],
                                                start=(h == 0), stop=(h == 1))
                last.then_inc(tk_lg, 1)

            for c in range(CHUNKS):
                if c == 0:
                    for k in range(3):
                        y_transpose(k, k % 2, k == 0)
                    row_transpose(0, 0, True)
                if c + 3 < CHUNKS:
                    y_transpose(c + 3, (c + 3) % 2, False)
                if c + 1 < CHUNKS:
                    row_transpose(c + 1, (c + 1) % 2, False)
                route(c, c % 2, c < 2)
            pe.wait_ge(cnt_ready, 1)
            cnt = rt[0:TILE, 2].rearrange("p t e -> p (t e)")
            nc.tensor.matmul(bank[0][0:TILE, 0:TILES * EXPERTS], below[0:TILE, 0:TILE], cnt, start=True, stop=True)
            nc.tensor.matmul(bank[0][0:P, 256:256 + TILES * EXPERTS], ones[0:TILE, :], cnt, start=True, stop=True
                             ).then_inc(rank_ps, 1)
            pe.wait_ge(list_zero, 1)
            zeros = eq[:].rearrange("p h c -> p (h c)")
            nc.tensor.matmul(bank[1][:, 0:2 * LIST], zeros[:, 0:P], zeros[:, 0:2 * LIST], start=True, stop=False,
                             skip_group_check=True)

            def collect(c, u):
                pe.wait_ge(ob_ready, 2 * c + 2)
                pe.wait_ge(oa_ready, 4 * c + 4)
                for t in range(2 * CHUNK_TILES):
                    last = nc.tensor.matmul(bank[1][:, 0:2 * LIST], ob[0:TILE, u, t], oa[0:TILE, u, t],
                                            start=False, stop=True, skip_group_check=True)
                last.then_inc(list_step, 1)

            for c in range(CHUNKS):
                collect(c, c % 2)

            pe.wait_ge(lists_ready, 1)

            def slot_transpose(j, u, r, fresh):
                pe.wait_ge(tok_in[u], 16 * (r + 1))
                if not fresh:
                    pe.wait_ge(xeT_half, 2 * j)
                for k in range(HALVES):
                    last = nc.tensor.transpose(bank[0][:, k * P:(k + 1) * P], tok[:, u, k * P:(k + 1) * P], ident[:])
                last.then_inc(tok_T, 1)

            def slot_up(j, u, e, fresh):
                pe.wait_ge(xeT_low, j + 1)
                pe.wait_ge(w_ready, e + 1)
                pe.wait_ge(wlo_ready, W_HALF * e + W_HALF)
                pe.wait_ge(wpool_ready, W_HALF * e + W_HALF)
                par = e % 2
                for c in range(2):
                    if not fresh:
                        pe.wait_ge(hid_b, 2 * (j - 1) + c + 1)
                    w_set = wsplit[:, bass.ds(par, 1)].rearrange("p a c -> p (a c)")
                    for k in range(HALVES):
                        for m, (x, lo) in enumerate(((xeT_hi, 0), (xeT_hi, W_COLS), (xeT_lo, 0))):
                            w = w_set[:, lo + k * HIDDEN + c * 512:lo + k * HIDDEN + (c + 1) * 512]
                            last = nc.tensor.matmul(bank[1 + c][:], x[:, u, k], w,
                                                    start=(k == 0 and m == 0), stop=(k == 1 and m == 2))
                    last.then_inc(hid_ps, 1)

            def slot_hidden_transpose(j, u, fresh):
                for c in range(2):
                    pe.wait_ge(hid_g, 2 * j + c + 1)
                    if not fresh:
                        pe.wait_ge(hidT_low, 2 * (j - 1) + c + 1)
                    for k in range(4):
                        last = nc.tensor.transpose(bank[3 + c][:, k * P:(k + 1) * P],
                                                   hid[:, u, (4 * c + k) * P:(4 * c + k + 1) * P], ident[:])
                    last.then_inc(hidT_ps, 1)

            def slot_down(j, e, fresh):
                par = e % 2
                if not fresh:
                    pe.wait_ge(y_b, j)
                w_set = wsplit[:, bass.ds(par, 1)].rearrange("p a c -> p (a c)")
                for k in range(HIDDEN // P):
                    if k % 4 == 0:
                        pe.wait_ge(hidT_low, 2 * j + k // 4 + 1)
                    for m, (x, lo) in enumerate(((hidT_hi, 0), (hidT_hi, W_COLS), (hidT_lo, 0))):
                        lo += HALVES * HIDDEN + k * DIM
                        last = nc.tensor.matmul(bank[5][:, 0:DIM], x[:, k], w_set[:, lo:lo + DIM], start=(k == 0 and m == 0),
                                                stop=(k == HIDDEN // P - 1 and m == 2))
                last.then_inc(y_ps, 1)

            def slot_step(j, u, tok_u, r, e_here, e_next, fresh=False):
                slot_hidden_transpose(j, u, fresh)
                slot_up(j + 1, 1 - u, e_next, False)
                slot_transpose(j + 2, tok_u, r, False)
                slot_down(j, e_here, fresh)

            def slots(j0, n):
                fresh = j0 == 0
                e0, e1 = experts_of(PE, j0, 2)
                slot_transpose(j0, 0, j0 // TOKS, fresh)
                slot_up(j0, 0, e0, fresh)
                slot_transpose(j0 + 1, 1, j0 // TOKS, False)
                slot_step(j0, 0, 2, j0 // TOKS, e0, e1, fresh)
                if n > 4:
                    with pe.Fori(0, (n - 4) // 4) as i:
                        e = experts_of(PE, j0 + 4 * i + 1, 5)
                        for k in range(4):
                            slot_step(j0 + 4 * i + 1 + k, (k + 1) % 2, (k + 3) % TOKS, j0 // TOKS + i + (k + 3) // TOKS,
                                      e[k], e[k + 1])
                j = j0 + n - 3
                e0, e1, e2 = experts_of(PE, j, 3)
                slot_step(j, 1, TOKS - 1, (j0 + n) // TOKS - 1, e0, e1)
                slot_hidden_transpose(j + 1, 0, False)
                slot_up(j + 2, 1, e2, False)
                slot_down(j + 1, e1, False)
                slot_hidden_transpose(j + 2, 1, False)
                slot_down(j + 2, e2, False)

            slots(0, MAIN)
            second = pe.value_load(more_i[0:1, 0:1], min_val=0, max_val=1)
            with pe.If(second > 0):
                slots(MAIN, SLOTS - MAIN)
            with pe.Else():
                pe.nop()

        @block.scalar
        def _(act):
            loads = [
                (w_natural[:, 0:2], a["L0_mix_Wq"].rearrange("(r p) c -> p r c", p=P)),
                (w_natural[:, 2:6], a["L0_mix_Wkv"].rearrange("(r p) c -> p r c", p=P)),
                (w_natural[:, 6:8], a["L0_mix_Wproj"].rearrange("(r p) c -> p r c", p=P)),
                (w_edge[:], a["L0_gnn_W_edge"]),
                (w1[:], a["L0_gnn_W1"].rearrange("(k p) c -> p k c", p=P)),
                (w2[:], a["L0_gnn_W2"].rearrange("(k p) c -> p k c", p=P)),
            ]
            act.dma_start(b_edge[:], a["L0_gnn_b_edge"].partition_broadcast(P)).then_inc(b_edge_in, 16)
            for s, d in loads:
                act.dma_start(s, d).then_inc(consts_in, 16)
            act.wait_ge(tiny_made, 1)
            for c in range(CHUNKS):
                ts_ = slice(c * CHUNK_TILES, (c + 1) * CHUNK_TILES)
                act.wait_ge(var_ready, c + 1)
                nc.scalar.activation(ln[0:TILE, 3, ts_], ln[0:TILE, 2, ts_], ACT.Sqrt).then_inc(sd_ready, 1)
                act.wait_ge(ln_ready, c + 1)
                for t in range(c * CHUNK_TILES, (c + 1) * CHUNK_TILES):
                    nc.scalar.activation(xs[0:TILE, t], xs[0:TILE, t], ACT.Identity, bias=ln[0:TILE, 5, t:t + 1],
                                         scale=ln[0:TILE, 4, t:t + 1]).then_inc(xn_ready, 1)
            act.wait_ge(tables_ready, 1)
            for g in range(2):
                nc.scalar.copy(idx_cur[:, g], srcT[:, g]).then_inc(idx_ready, 1)
            act.wait_ge(wT_ready, 1)
            nc.scalar.copy(w_hi[:], w_edge[:]).then_inc(w_split, 1)
            nc.scalar.copy(wqT[:], bank[0][:].rearrange("p (k c) -> p k c", k=2)).then_inc(wT_copied, 1)
            for k in range(2):
                nc.scalar.copy(wkvT[:, k], bank[1 + k][:]).then_inc(wT_copied, 1)
            nc.scalar.copy(wpT[:], bank[3][:].rearrange("p (k c) -> p k c", k=2)).then_inc(wT_copied, 1)
            act.wait_ge(xn_ready, TILES)
            nc.scalar.preload_act_table(ACT.Exp)

            def mix_in(t):
                act.wait_ge(mx_T, t + 1)
                nc.scalar.copy(xn_t[0:TILE], xs[0:TILE, bass.ds(t, 1)].rearrange("p a d -> p (a d)")).then_inc(mx_in, 1)

            def mix_xT(t):
                act.wait_ge(mx_T, t + 2)
                act.wait_ge(mx_q, t + 1)
                nc.scalar.copy(xT_t[:, :, 0:TILE], by_half(bank[7])
                               ).then_inc(mx_xT, 1)

            def mix_exp(t):
                act.wait_ge(mx_kv, t + 1)
                act.wait_ge(mx_k, t + 1)
                act.wait_ge(mx_ctx, t + 1)
                nc.scalar.activation(ek[0:TILE], bank[6][0:TILE, 0:DIM], ACT.Exp).then_inc(mx_ek, 1)
                nc.scalar.copy(v_t[0:TILE], bank[6][0:TILE, DIM:2 * DIM]).then_inc(mx_v, 1)
                act.wait_ge(mx_q, t + 2)
                act.wait_ge(mx_qT, t + 1)
                nc.scalar.activation(eq[:], by_half(bank[7]),
                                     ACT.Exp).then_inc(mx_eq, 1)

            def attn_den(c, more):
                if more:
                    act.wait_ge(qn_ready, c)
                for h in range(HALVES):
                    act.wait_ge(den_ps, c + 1)
                    nc.scalar.activation(dinv[:, bass.ds(c % 2, 1), h].rearrange("p a n -> p (a n)"), bank[6 + h][:, 0:COLS],
                                         ACT.Identity, bias=tiny[:]).then_inc(den_out, 1)

            def attn_bias(c):
                for o in range(HALVES):
                    act.wait_ge(ao_ps, 2 * c + o + 1)
                    nc.scalar.activation(qT[:, o, bass.ds(c * COLS, COLS)], bank[6 + o][:, 0:COLS], ACT.Identity,
                                         bias=cvec[:, BPROJ, o:o + 1]).then_inc(ao_ready, 1)

            def edge_pass(n0, r0, phases, fresh):
                if not fresh:
                    for u in range(2):
                        for q in range(PAIRS):
                            act.wait_ge(xg_in[u][q], 32 * r0)
                        nc.scalar.copy(idx_cur[:, u], srcT[:, u]).then_inc(idx_ready, 1)
                copy_edges(act, n0, 0)
                copy_edges(act, n0 + 1, 1)
                relu_messages(act, 0, n0, r0, 0, True)

                def body(i, riders):
                    n = n0 + 2 * i
                    copy_edges(act, n + 2, 0)
                    if riders and riders[0]:
                        riders[0](i)
                    relu_messages(act, 2 * i + 1, n + 1, r0 + i, 1, True)
                    if riders and riders[1]:
                        riders[1](i)
                    copy_edges(act, n + 3, 1)
                    relu_messages(act, 2 * i + 2, n + 2, r0 + i + 1, 0, i_more)
                    if riders and riders[2]:
                        riders[2](i)

                for lo, hi, riders, between in phases:
                    i_more = True
                    if hi == BODIES:
                        with act.Fori(lo, hi - 1) as i:
                            body(i, riders)
                        i_more = False
                        body(hi - 1, riders)
                    else:
                        with act.Fori(lo, hi) as i:
                            body(i, riders)
                    if between:
                        between()
                relu_messages(act, GROUPS - 1, n0 + GROUPS - 1, r0 + BODIES, 1, False)

            def mix_middle(t):
                mix_xT(t)
                mix_exp(t)

            def copy_attn_w():
                act.wait_ge(aw_ps, 1)
                nc.scalar.copy(attn_w[:], bank[6][:].rearrange("p (h c) -> p h c", h=2)).then_inc(aw_ready, 1)

            edge_pass(0, 0, [(0, TILES, (mix_in, mix_middle, None), copy_attn_w),
                             (TILES, TILES + 1, (lambda i: attn_den(0, False), None, None), None),
                             (TILES + 1, BODIES, (lambda i: attn_den(i - TILES, True), lambda i: attn_bias(i - TILES - 1), None), None)], True)
            attn_bias(COL_CHUNKS - 1)
            again = act.value_load(miss_i[0:1, 0:1], min_val=0, max_val=1)
            with act.If(again > 0):
                with act.Fori(0, WINDOWS) as w:
                    edge_pass((w + 1) * GROUPS, (w + 1) * (GROUPS // 2), [(0, BODIES, None, None)], False)
            with act.Else():
                act.nop()

            def mlp1(c, u, fresh):
                for o in range(HALVES):
                    act.wait_ge(z1_ps, 2 * c + o + 1)
                    if not fresh:
                        act.wait_ge(z2_ps, 2 * (c - 1))
                    nc.scalar.activation(z1[:, u, o], bank[o][:, 0:COLS], ACT.Relu, bias=cvec[:, B1, o:o + 1]
                                         ).then_inc(z1_ready, 1)

            def mlp2(c, u):
                for o in range(HALVES):
                    act.wait_ge(z2_ps, 2 * c + o + 1)
                    nc.scalar.activation(hT[:, o, bass.ds(c * COLS, COLS)], bank[2 + o][:, 0:COLS], ACT.Identity,
                                         bias=cvec[:, B2, o:o + 1]).then_inc(z2_ready, 1)

            mlp1(0, 0, True)
            mlp1(1, 1, True)
            mlp2(0, 0)
            with act.Fori(0, (COL_CHUNKS - 3) // 2) as i:
                mlp1(2 * i + 2, 0, False)
                mlp2(2 * i + 1, 1)
                mlp1(2 * i + 3, 1, False)
                mlp2(2 * i + 2, 0)
            mlp1(COL_CHUNKS - 1, 0, False)
            mlp2(COL_CHUNKS - 2, 1)
            mlp2(COL_CHUNKS - 1, 0)
            act.wait_ge(bn_var, 1)
            nc.scalar.activation(bns[:, 1], bns[:, 0], ACT.Sqrt).then_inc(bn_sd, 1)
            act.wait_ge(bn_ready, 1)

            def y_activate(c, u, fresh):
                if not fresh:
                    act.wait_ge(y_T, c - 1)
                for o in range(HALVES):
                    nc.scalar.activation(y_cur[:, u, o], hT[:, o, bass.ds(c * (CHUNK_TILES * TILE), CHUNK_TILES * TILE)],
                                         ACT.Relu, bias=bns[:, 3, o:o + 1], scale=bns[:, 2, o:o + 1]).then_inc(y_relu, 1)

            def normalise(c, r, u, fresh):
                ts_ = bass.ds(c * CHUNK_TILES, CHUNK_TILES)
                act.wait_ge(l2_var, c + 1)
                nc.scalar.activation(ln[0:TILE, 6:8, ts_], ln[0:TILE, 2:4, ts_], ACT.Sqrt).then_inc(l2_sd, 1)
                act.wait_ge(l2_ready, c + 1)
                if not fresh:
                    act.wait_ge(tk_stored[u], 32 * r)
                    act.wait_ge(tk_T, c - 1)
                for k in range(CHUNK_TILES):
                    t = c * CHUNK_TILES + k
                    last = nc.scalar.activation(xn_cur[0:TILE, u, k], xs[0:TILE, bass.ds(t, 1)].rearrange("p a d -> p (a d)"),
                                                ACT.Identity, bias=ln[0:TILE, 5, bass.ds(t, 1)],
                                                scale=ln[0:TILE, 4, bass.ds(t, 1)])
                last.then_inc(tk_ready, 1)

            def copy_rows(c, u, fresh):
                act.wait_ge(tk_T, c + 1)
                if not fresh:
                    act.wait_ge(tk_lg, c - 1)
                flat = xnT[:, u].rearrange("p t h c -> p (t h) c")
                for b, m in enumerate((4, 4, 2)):
                    nc.scalar.copy(flat[:, 4 * b:4 * b + m], bank[4 + b][:, 0:m * TILE].rearrange("p (m c) -> p m c", m=m)
                                   ).then_inc(tk_xT, 1)

            for c in range(2):
                y_activate(c, c, True)
            for c in range(CHUNKS):
                if c + 2 < CHUNKS:
                    y_activate(c + 2, c % 2, False)
                normalise(c, c // 2, c % 2, c < 2)
                if c >= 1:
                    copy_rows(c - 1, (c - 1) % 2, c < 3)
            copy_rows(CHUNKS - 1, (CHUNKS - 1) % 2, False)
            act.wait_ge(gate_in, 1)
            nc.scalar.activation(rs[0:TILE, 3], rs[0:TILE, 2], ACT.Exp).then_inc(gate_exp, 1)
            nc.scalar.preload_act_table(ACT.Gelu)

            def split_weights(e, j):
                act.wait_ge(raw_ready, e + 1)
                if j is not None:
                    act.wait_ge(y_ps, j)
                for q in range(W_PIECES):
                    nc.scalar.copy(split_piece(e, q, False), raw[:, piece(q)]).then_inc(whi_ready, 1)

            act.wait_ge(y_sum, CHUNKS)
            act.wait_ge(tk_ready, CHUNKS)
            act.wait_ge(x1_stats, CHUNKS)
            act.wait_ge(x1_stored, 32 * CHUNKS)
            split_weights(0, None)

            act.wait_ge(lists_ready, 1)

            def slot_gelu(j, u):
                for c in range(2):
                    s = hid[:, u, c * 512:(c + 1) * 512]
                    act.wait_ge(hid_b, 2 * j + c + 1)
                    nc.scalar.activation(s, s, ACT.Gelu).then_inc(hid_g, 1)

            def slot_copy(j, fresh):
                for c in range(2):
                    act.wait_ge(hidT_ps, 2 * j + c + 1)
                    if not fresh:
                        act.wait_ge(y_ps, j)
                    nc.scalar.copy(hidT_hi[:, 4 * c:4 * c + 4], bank[3 + c][:].rearrange("p (k c) -> p k c", k=4)
                                   ).then_inc(hidT_high, 1)

            def slot_high(j, u, fresh):
                act.wait_ge(xeT_half, 2 * j + 2)
                if not fresh:
                    act.wait_ge(hid_ps, 2 * (j - 1))
                nc.scalar.copy(xeT_hi[:, u], xeT[:, u]).then_inc(xe_hi, 1)

            def slot_weigh(j, u, fresh):
                act.wait_ge(y_b, j + 1)
                nc.scalar.activation(ys[:, u], ys[:, u], ACT.Identity, scale=slot_f[:, 1, bass.ds(j, 1)]).then_inc(y_w, 1)

            def slot_step(j, u, e_last, e_here, fresh=False):
                slot_copy(j, fresh)
                if e_last is None:
                    split_weights(e_here + 1, None)
                else:
                    with act.If(e_here > e_last):
                        split_weights(e_here + 1, j)
                    with act.Else():
                        act.nop()
                slot_gelu(j + 1, 1 - u)
                slot_high(j + 2, u, False)
                slot_weigh(j, u, fresh)

            def slots(j0, n):
                fresh = j0 == 0
                slot_high(j0, 0, fresh)
                slot_gelu(j0, 0)
                slot_high(j0 + 1, 1, fresh)
                e = [None, *experts_of(ACT_ENGINE, j0, 1)] if fresh else experts_of(ACT_ENGINE, j0 - 1, 2)
                slot_step(j0, 0, e[0], e[1], fresh)
                if n > 4:
                    with act.Fori(0, (n - 4) // 4) as i:
                        e = experts_of(ACT_ENGINE, j0 + 4 * i, 5)
                        for k in range(4):
                            slot_step(j0 + 4 * i + 1 + k, (k + 1) % 2, e[k], e[k + 1])
                j = j0 + n - 3
                e = experts_of(ACT_ENGINE, j - 1, 4)
                slot_step(j, 1, e[0], e[1])
                slot_copy(j + 1, False)
                with act.If(e[2] > e[1]):
                    split_weights(e[2] + 1, j + 1)
                with act.Else():
                    act.nop()
                slot_gelu(j + 2, 1)
                slot_weigh(j + 1, 0, False)
                slot_copy(j + 2, False)
                with act.If(e[3] > e[2]):
                    split_weights(e[3] + 1, j + 2)
                with act.Else():
                    act.nop()
                slot_weigh(j + 2, 1, False)

            slots(0, MAIN)
            second = act.value_load(more_i[0:1, 0:1], min_val=0, max_val=1)
            with act.If(second > 0):
                slots(MAIN, SLOTS - MAIN)
            with act.Else():
                act.nop()

        @block.vector
        def _(dve):
            step = Chain(dve, dve_chain)
            for s in (mx_rk, mx_ek, mx_v, mx_T, mx_q, mx_k, mx_ctx, mx_qT, qn_ready):
                dve.sem_inc(s, 1)

            def moments_to_ln(chain, t, n):
                s = st[0:TILE, bass.ds(t, n)].rearrange("p t s -> p s t")
                L = ln[0:TILE, :, bass.ds(t, n)]
                chain(nc.vector.tensor_tensor(L[:, 0], s[:, 1], s[:, 4], ALU.subtract))
                chain(nc.vector.tensor_tensor(L[:, 1], s[:, 1], s[:, 4], ALU.add))
                chain(nc.vector.tensor_tensor(L[:, 0], L[:, 0], L[:, 0], ALU.mult))
                chain(nc.vector.tensor_tensor(L[:, 2], s[:, 2], s[:, 5], ALU.add))
                chain(nc.vector.scalar_tensor_tensor(out=L[:, 2], in0=L[:, 2], scalar=4.0 / DIM, in1=L[:, 0],
                                                     op0=ALU.mult, op1=ALU.add))
                chain(nc.vector.tensor_scalar(L[:, 2], L[:, 2], 0.25, LN_EPS, ALU.mult, ALU.add))

            nc.vector.memset(dst_i, FAR).then_inc(ids_memset, 1)
            nc.vector.memset(src_i, 0).then_inc(ids_memset, 1)
            def norm_of_x(c):
                dve.wait_ge(x_in[c], 32)
                ts_ = slice(c * CHUNK_TILES, (c + 1) * CHUNK_TILES)
                for t in range(c * CHUNK_TILES, (c + 1) * CHUNK_TILES):
                    last = nc.vector.bn_stats(st[0:TILE, t], xs[0:TILE, t])
                step(last)
                moments_to_ln(step, c * CHUNK_TILES, CHUNK_TILES)
                dve.sem_inc(var_ready, 1)
                dve.wait_ge(sd_ready, c + 1)
                step(nc.vector.reciprocal(ln[0:TILE, 4, ts_], ln[0:TILE, 3, ts_]))
                nc.vector.scalar_tensor_tensor(out=ln[0:TILE, 5, ts_], in0=ln[0:TILE, 1, ts_], scalar=-0.5,
                                               in1=ln[0:TILE, 4, ts_], op0=ALU.mult, op1=ALU.mult).then_inc(ln_ready, 1)

            norm_of_x(0)
            dve.wait_ge(ids_in, 64)
            step(nc.vector.tensor_copy(dst_f, dst_i))
            step(nc.vector.tensor_reduce(gstat[:, 0:1], dst_f, AX.X, ALU.min))
            step(nc.vector.tensor_scalar(gstat[:, 0:1], gstat[:, 0:1], 0.0, float(NODES - 1), ALU.max, ALU.min))
            step(nc.vector.tensor_scalar(rel, dst_f, gstat[:, 0:1], None, ALU.subtract))
            step(nc.vector.scalar_tensor_tensor(out=src_f, in0=dst_f, scalar=float(FAR), in1=rel,
                                                op0=ALU.is_lt, op1=ALU.mult))
            step(nc.vector.tensor_reduce(gstat[:, 1:2], src_f, AX.X, ALU.max))
            step(nc.vector.tensor_copy(src_f, src_i))
            nc.vector.memset(gstat[:, 2:3], 0.0).then_inc(rel_ready, 1)

            norm_of_x(1)
            dve.wait_ge(consts_made, 8)
            step(nc.vector.tensor_copy(iota_f[:], iota_i[:]))
            step(nc.vector.tensor_copy(part_f[:], part_i[:]))
            step(nc.vector.tensor_copy(tokid[:], tokid_i[:]))
            dve.wait_ge(ids_T, 1)
            nc.vector.tensor_copy(srcT[:], bank[5][:, 0:GT * GROUPS].rearrange("p (j g) -> p g j", j=GT)
                                  ).then_inc(tables_ready, 1)
            step(nc.vector.tensor_copy(relT[:], bank[4][:, 0:GT * GROUPS].rearrange("p (j g) -> p g j", j=GT)))
            step(nc.vector.tensor_copy(base_row[:, 0:GROUPS], bank[6][0:1, 0:GROUPS]))
            step(nc.vector.tensor_reduce(gstat[0:1, 3:4], bank[6][0:1, P:P + GROUPS], AX.X, ALU.max))
            nc.vector.tensor_scalar(miss_i[:], gstat[0:1, 3:4], float(WINDOW), None, ALU.is_ge).then_inc(tables_ready, 1)
            nc.vector.memset(gstat[:, 2:3], 0.0).then_inc(tables_ready, 1)
            dve.wait_ge(tables_ready, 3)
            for c in range(2, CHUNKS):
                norm_of_x(c)
            dve.wait_ge(b_edge_in, 16)
            dve.wait_ge(xn_ready, TILES)
            dve.wait_ge(rows_stored[0], 64)
            dve.wait_ge(rows_ready, CHUNKS - 1)
            nc.vector.tensor_tensor(table_stage[0:TILE, 0], xs[0:TILE, TILES - CHUNK_TILES:TILES],
                                    b_edge[0:TILE].unsqueeze(1).to_broadcast([TILE, CHUNK_TILES, DIM]), ALU.add
                                    ).then_inc(rows_ready, 1)
            dve.wait_ge(consts_in, CONST_DMAS * 16)
            step(nc.vector.tensor_scalar(eps1[:], eps1[:], 1.0, None, ALU.add))
            dve.wait_ge(wT_ready, 1)
            dve.wait_ge(w_split, 1)
            nc.vector.tensor_tensor(w_lo[:], w_edge[:], w_hi[:].bitcast(F32), ALU.subtract).then_inc(w_split, 1)

            def mix_h(t, h_count):
                dve.wait_ge(mx_xT, t + 1)
                dve.wait_ge(h_updates, h_count)
                w = hT[:, :, bass.ds(t * TILE, TILE)]
                nc.vector.scalar_tensor_tensor(out=w, in0=by_half(bank[7]),
                                               scalar=eps1[:], in1=w, op0=ALU.mult, op1=ALU.add).then_inc(h_updates, 1)

            def mix_elu(t):
                dve.wait_ge(mx_v, t + 2)
                dve.wait_ge(mx_ctx, t + 1)
                dve.wait_ge(mx_kacc, t + 1)
                nc.vector.tensor_scalar(k_t[0:TILE], bank[6][0:TILE, 0:DIM], 0.0, None, ALU.max).then_inc(mx_rk, 1)
                dve.wait_ge(mx_rk, t + 2)
                nc.vector.scalar_tensor_tensor(out=k_t[0:TILE], in0=ek[0:TILE], scalar=1.0, in1=k_t[0:TILE],
                                               op0=ALU.min, op1=ALU.add).then_inc(mx_k, 1)
                dve.wait_ge(mx_kacc, t + 1)
                dve.wait_ge(mx_k, t + 2)
                nc.vector.tensor_tensor(k_acc[0:TILE], k_acc[0:TILE], k_t[0:TILE], ALU.add).then_inc(mx_kacc, 1)
                dve.wait_ge(mx_eq, t + 1)
                dve.wait_ge(mx_qT, t + 1)
                nc.vector.tensor_scalar(rq[:], by_half(bank[7]),
                                        0.0, None, ALU.max).then_inc(mx_rq, 1)
                dve.wait_ge(mx_rq, t + 1)
                nc.vector.scalar_tensor_tensor(out=qT[:, :, bass.ds(t * TILE, TILE)], in0=eq[:], scalar=1.0, in1=rq[:],
                                               op0=ALU.min, op1=ALU.add).then_inc(mx_qT, 1)

            def mix_context(t):
                dve.wait_ge(mx_ctx, t + 2)
                dve.wait_ge(mx_acc, t + 1)
                nc.vector.tensor_tensor(ctx_acc[:], ctx_acc[:], bank[7][:, 0:2 * P], ALU.add).then_inc(mx_acc, 1)

            def mask_context():
                dve.wait_ge(mx_acc, TILES + 1)
                dve.wait_ge(ksum_ps, 1)
                for h in range(HALVES):
                    nc.vector.tensor_tensor(ctx_m[:, h], ctx_acc[:, h * P:(h + 1) * P], blocks[:], ALU.mult
                                            ).then_inc(ctx_masked, 1)
                    nc.vector.tensor_scalar(ksum_m[:, h], blocks[:], bank[7][:, h:h + 1], None, ALU.mult
                                            ).then_inc(ctx_masked, 1)

            def attn_inverse(c, k):
                n = COLS // 2
                d = dinv[:, bass.ds(c % 2, 1), k // 2, k % 2 * n:(k % 2 + 1) * n].rearrange("p a n -> p (a n)")
                dve.wait_ge(den_out, 2 * c + 2)
                nc.vector.reciprocal(d, d).then_inc(den_inv, 1)

            def attn_norm(c, more):
                dve.wait_ge(den_inv, PIECES * (c + 1))
                if more:
                    dve.wait_ge(ao_ps, 2 * c)
                nc.vector.scalar_tensor_tensor(out=qn, in0=dinv[:, bass.ds(c % 2, 1)].rearrange("p a h n -> p (a h) n"),
                                               scalar=1e6, in1=qT[:, :, bass.ds(c * COLS, COLS)],
                                               op0=ALU.min, op1=ALU.mult).then_inc(qn_ready, 1)

            def attn_riders(more):
                piece = lambda k: lambda i: attn_inverse(i - TILES, k)
                return (None, piece(0), piece(1), piece(2), piece(3), lambda i: attn_norm(i - TILES, more))

            def edge_pass(n0, r0, start_of, h_of, phases):
                split_edges(dve, n0, 0)
                split_edges(dve, n0 + 1, 1)
                mark_window(dve, 0, 0)
                add_nodes(dve, n0, r0, 0)

                def body(i, riders, per_body, h0, lo):
                    n = n0 + 2 * i
                    h = h0 + (i - lo) * per_body
                    split_edges(dve, n + 2, 0)
                    add_nodes(dve, n + 1, r0 + i, 1)
                    mark_window(dve, 2 * i + 1, 1)
                    if riders and riders[1]:
                        riders[1](i)
                    s0 = start_of(2 * i)
                    add_window(dve, n, 0, s0, h)
                    dve.wait_ge(h_updates, h + 1)
                    dve.sem_inc(agg_read, 1)
                    h = h + 1
                    if riders:
                        if riders[0]:
                            riders[0](i, h)
                            h = h + 1
                        if riders[2]:
                            riders[2](i)
                    split_edges(dve, n + 3, 1)
                    add_nodes(dve, n + 2, r0 + i + 1, 0)
                    if riders:
                        riders[3](i)
                    mark_window(dve, 2 * i + 2, 0)
                    if riders and riders[4]:
                        riders[4](i)
                    s1 = start_of(2 * i + 1)
                    add_window(dve, n + 1, 1, s1, h)
                    dve.wait_ge(h_updates, h + 1)
                    dve.sem_inc(agg_read, 1)
                    if riders and riders[5]:
                        riders[5](i)

                h0 = h_of
                for lo, hi, riders, between in phases:
                    per_body = 3 if riders and riders[0] else 2
                    with dve.Fori(lo, hi) as i:
                        body(i, riders, per_body, h0, lo)
                    h0 = h0 + (hi - lo) * per_body
                    if between:
                        between()
                n = n0 + GROUPS
                mark_window(dve, GROUPS - 1, 1)
                add_nodes(dve, n - 1, r0 + BODIES, 1)
                for k in range(2):
                    add_window(dve, n - 2 + k, k, start_of(GROUPS - 2 + k), h0 + k)
                    dve.wait_ge(h_updates, h0 + k + 1)
                    dve.sem_inc(agg_read, 1)
                return h0 + 2

            def own_window(g):
                return dve.value_load(base_row[0:1, bass.ds(g, 1)], min_val=0, max_val=NODES - 1)

            dve.sem_inc(agg_read, 1)
            dve.wait_ge(h_updates, 1)
            h_end = edge_pass(0, 0, own_window, 1, [
                (0, TILES, (mix_h, None, None, mix_elu, None, mix_context), mask_context),
                (TILES, TILES + 1, attn_riders(False), None),
                (TILES + 1, BODIES, attn_riders(True), None)])
            again = dve.value_load(miss_i[0:1, 0:1], min_val=0, max_val=1)
            with dve.If(again > 0):
                nc.vector.tensor_scalar(rel, rel, float(WINDOW), None, ALU.is_ge).then_inc(pass_tables, 1)
                dve.wait_ge(pass_tables, 1)
                nc.vector.scalar_tensor_tensor(out=rel, in0=dst_f, scalar=float(4 * FAR), in1=rel,
                                               op0=ALU.add, op1=ALU.mult).then_inc(pass_tables, 1)
                dve.wait_ge(pass_tables, 2)
                nc.vector.tensor_scalar(rel, rel, float(4 * FAR), None, ALU.subtract).then_inc(pass_tables, 1)
                dve.wait_ge(pass_tables, 3)
                dve.wait_ge(pass_T, 1)
                nc.vector.tensor_copy(relT[:], bank[4][:, 0:GT * GROUPS].rearrange("p (j g) -> p g j", j=GT)
                                      ).then_inc(pass_done, 1)
                with dve.Fori(0, WINDOWS) as w:
                    dve.wait_ge(pass_done, w + 1)
                    h1 = h_end + w * GROUPS
                    edge_pass((w + 1) * GROUPS, (w + 1) * (GROUPS // 2), lambda g: w * WINDOW, h1, [(0, BODIES, None, None)])
                    nc.vector.tensor_scalar(relT[:], relT[:], float(WINDOW), None, ALU.subtract).then_inc(pass_done, 1)
            with dve.Else():
                dve.nop()
            nc.vector.memset(eq[:], 0.0).then_inc(edges_done, 1)
            nc.vector.memset(ek[:], 0.0).then_inc(edges_done, 1)

            for c in range(COL_CHUNKS):
                dve.wait_ge(z2_ready, 2 * c + 2)
                for o in range(HALVES):
                    last = nc.vector.bn_stats(bn[:, o, c], hT[:, o, c * COLS:min((c + 1) * COLS, NODES)])
            step(last)
            for o in range(HALVES):
                last = nc.vector.bn_aggr(mv[:, o], bn[:, o])
            step(last)
            nc.vector.tensor_scalar(bns[:, 0], mv[:, :, 1], LN_EPS, None, ALU.add).then_inc(bn_var, 1)
            dve.wait_ge(bn_sd, 1)
            step(nc.vector.reciprocal(bns[:, 1], bns[:, 1]))
            step(nc.vector.tensor_tensor(bns[:, 2], bns[:, 1], cvec[:, GAMMA], ALU.mult))
            step(nc.vector.tensor_tensor(bns[:, 0], bns[:, 2], mv[:, :, 0], ALU.mult))
            nc.vector.tensor_tensor(bns[:, 3], cvec[:, BETA], bns[:, 0], ALU.subtract).then_inc(bn_ready, 1)
            dve.wait_ge(x_again, 32 * CHUNKS)
            def residual(c):
                dve.wait_ge(y_T, c + 1)
                for b, m in enumerate((2, 2, 1)):
                    rows = xs[0:TILE, bass.ds(c * CHUNK_TILES + 2 * b, m)]
                    nc.vector.tensor_tensor(rows, bank[b][0:TILE, 0:m * DIM].rearrange("p (m d) -> p m d", m=m), rows,
                                            ALU.add).then_inc(x1_ready, 1)
                dve.wait_ge(x1_ready, 3 * c + 3)
                for k in range(CHUNK_TILES):
                    t = c * CHUNK_TILES + k
                    last = nc.vector.bn_stats(st[0:TILE, bass.ds(t, 1)].rearrange("p a s -> p (a s)"),
                                              xs[0:TILE, bass.ds(t, 1)].rearrange("p a d -> p (a d)"))
                last.then_inc(x1_stats, 1)
                dve.wait_ge(x1_stats, c + 1)

            def norm_of_rows(c):
                chain = Chain(dve, l2_chain, c * L2_STEPS)
                ts_ = bass.ds(c * CHUNK_TILES, CHUNK_TILES)
                L = [ln[0:TILE, k, ts_] for k in range(8)]
                moments_to_ln(chain, c * CHUNK_TILES, CHUNK_TILES)
                chain(nc.vector.reciprocal(L[3], L[2]))
                chain(nc.vector.scalar_tensor_tensor(out=L[3], in0=L[2], scalar=LN_EPS, in1=L[3],
                                                     op0=ALU.subtract, op1=ALU.mult))
                nc.vector.tensor_scalar(L[3], L[3], LN_EPS, None, ALU.add).then_inc(l2_var, 1)
                dve.wait_ge(l2_sd, c + 1)
                chain(nc.vector.tensor_tensor(L[0], L[6], L[7], ALU.mult))
                chain(nc.vector.reciprocal(L[4], L[0]))
                nc.vector.scalar_tensor_tensor(out=L[5], in0=L[1], scalar=-0.5, in1=L[4],
                                               op0=ALU.mult, op1=ALU.mult).then_inc(l2_ready, 1)
                assert chain.n == L2_STEPS

            def scale_logits(c):
                dve.wait_ge(tk_lg, c + 1)
                back = ln[0:TILE, 7, bass.ds(c * CHUNK_TILES, CHUNK_TILES)].unsqueeze(2).to_broadcast([TILE, CHUNK_TILES, EXPERTS])
                nc.vector.tensor_tensor(logits[0:TILE, bass.ds(c * CHUNK_TILES, CHUNK_TILES)],
                                        bank[(7, 3)[c % 2]][0:TILE, 0:CHUNK_TILES * EXPERTS].rearrange("p (t e) -> p t e", e=EXPERTS),
                                        back, ALU.mult).then_inc(tk_scaled, 1)

            for c in range(CHUNKS):
                residual(c)
                norm_of_rows(c)
                if c >= 3:
                    scale_logits(c - 3)
            for c in range(CHUNKS - 3, CHUNKS - 1):
                scale_logits(c)
            step(nc.vector.tensor_scalar(part_f[:], part_f[:], float(NODES), None, ALU.add))
            step(nc.vector.tensor_scalar(tokid[:], tokid[:], 1.0, None, ALU.add))
            step(nc.vector.tensor_scalar(ex[:, 0], iota_f[:, 0:EXPERTS], -1.0, float(EXPERTS), ALU.mult, ALU.add))
            nc.vector.memset(ej[:], 0.0).then_inc(list_zero, 1)
            scale_logits(CHUNKS - 1)
            dve.wait_ge(tk_scaled, CHUNKS)

            shape = [TILE, TILES, EXPERTS]
            R, S, lg = rt[0:TILE], rs[0:TILE], logits[0:TILE]
            by_t = lambda v: v.unsqueeze(2).to_broadcast(shape)
            by_e = lambda v: v.unsqueeze(1).to_broadcast(shape)
            step(nc.vector.tensor_tensor(lg, lg, by_e(br[0:TILE]), ALU.add))
            for s, src in ((0, lg), (1, R[:, 3])):
                if s == 1:
                    step(nc.vector.scalar_tensor_tensor(out=R[:, 3], in0=R[:, 0], scalar=-1e30, in1=lg,
                                                        op0=ALU.mult, op1=ALU.add))
                step(nc.vector.tensor_reduce(S[:, s], src, AX.X, ALU.max))
                step(nc.vector.tensor_tensor(R[:, 4], src, by_t(S[:, s]), ALU.is_equal))
                step(nc.vector.tensor_tensor(R[:, 4], R[:, 4], by_e(ex[0:TILE, 0]), ALU.mult))
                step(nc.vector.tensor_reduce(S[:, 6], R[:, 4], AX.X, ALU.max))
                step(nc.vector.tensor_tensor(R[:, s], R[:, 4], by_t(S[:, 6]), ALU.is_equal))
            nc.vector.tensor_tensor(R[:, 2], R[:, 0], R[:, 1], ALU.add).then_inc(cnt_ready, 1)
            nc.vector.tensor_tensor(S[:, 2], S[:, 1], S[:, 0], ALU.subtract).then_inc(gate_in, 1)
            dve.wait_ge(gate_exp, 1)
            step(nc.vector.tensor_scalar(S[:, 4], S[:, 3], 1.0, None, ALU.add))
            step(nc.vector.reciprocal(S[:, 4], S[:, 4]))
            step(nc.vector.tensor_tensor(S[:, 5], S[:, 3], S[:, 4], ALU.mult))
            dve.wait_ge(rank_ps, 1)
            total = bank[0][0:TILE, 256:256 + TILES * EXPERTS].rearrange("p (t e) -> p t e", e=EXPERTS)
            rank = bank[0][0:TILE, 0:TILES * EXPERTS].rearrange("p (t e) -> p t e", e=EXPERTS)
            for e in range(EXPERTS):
                last = nc.vector.tensor_tensor_scan(R[:, 5, :, e], ones[0:TILE, 0:TILES], total[:, :, e], 0.0,
                                                    ALU.mult, ALU.add)
            step(last)
            X = ex[0:TILE]
            step(nc.vector.tensor_scalar(X[:, 2], R[:, 5, TILES - 1], float(P - 1), float(P), ALU.add, ALU.max))
            step(nc.vector.tensor_copy(exi[0:TILE], X[:, 2]))
            step(nc.vector.tensor_scalar(exi[0:TILE], exi[0:TILE], 7, None, ALU.logical_shift_right))
            step(nc.vector.tensor_copy(X[:, 3], exi[0:TILE]))
            step(nc.vector.tensor_tensor_scan(X[:, 4], ones[0:TILE, 0:EXPERTS], X[:, 3], 0.0, ALU.mult, ALU.add))
            step(nc.vector.tensor_tensor(X[:, 5], X[:, 4], X[:, 3], ALU.subtract))
            step(nc.vector.tensor_scalar(X[:, 2], X[:, 5], float(P), None, ALU.mult))
            step(nc.vector.tensor_tensor(R[:, 5], R[:, 5], total, ALU.subtract))
            step(nc.vector.tensor_tensor(R[:, 5], R[:, 5], rank, ALU.add))
            step(nc.vector.tensor_tensor(R[:, 5], R[:, 5], by_e(X[:, 2]), ALU.add))
            for s in range(2):
                step(nc.vector.tensor_tensor(R[:, 4], R[:, s], R[:, 5], ALU.mult))
                step(nc.vector.tensor_reduce(S[:, 6], R[:, 4], AX.X, ALU.add))
                step(nc.vector.tensor_copy(rsi[0:TILE, 0], S[:, 6]))
                step(nc.vector.tensor_scalar(rsi[0:TILE, 1], rsi[0:TILE, 0], 7, None, ALU.logical_shift_right))
                step(nc.vector.tensor_copy(S[:, 8 if s == 0 else 1], rsi[0:TILE, 1]))
                step(nc.vector.tensor_scalar(rsi[0:TILE, 1], rsi[0:TILE, 0], P - 1, None, ALU.bitwise_and))
                step(nc.vector.tensor_copy(S[:, 9 if s == 0 else 2], rsi[0:TILE, 1]))
            def mark_slots(c, u, fresh):
                if not fresh:
                    dve.wait_ge(oa_ready, 4 * c - 4)
                    dve.wait_ge(list_step, c - 1)
                ts_ = bass.ds(c * CHUNK_TILES, CHUNK_TILES)
                for s in range(2):
                    narrow = [TILE, CHUNK_TILES, LIST]
                    nc.vector.tensor_tensor(oh[0:TILE, u, s], iota_f[0:TILE, 0:LIST].unsqueeze(1).to_broadcast(narrow),
                                            S[:, (8, 1)[s], ts_].unsqueeze(2).to_broadcast(narrow), ALU.is_equal
                                            ).then_inc(oh_made, 1)
                for s in range(2):
                    wide = [TILE, CHUNK_TILES, P]
                    nc.vector.tensor_tensor(ob[0:TILE, u, s * CHUNK_TILES:(s + 1) * CHUNK_TILES],
                                            iota_f[0:TILE].unsqueeze(1).to_broadcast(wide),
                                            S[:, (9, 2)[s], ts_].unsqueeze(2).to_broadcast(wide), ALU.is_equal
                                            ).then_inc(ob_ready, 1)

            for c in range(CHUNKS):
                mark_slots(c, c % 2, c < 2)
            for e in range(1, EXPERTS):
                step(nc.vector.scalar_tensor_tensor(out=ej[0:1, 0], in0=iota_f[0:1, 0:SLOTS], scalar=ex[0:1, 5, e:e + 1],
                                                    in1=ej[0:1, 0], op0=ALU.is_ge, op1=ALU.add))
            step(nc.vector.tensor_copy(ej_i[:, 3:3 + SLOTS], ej[0:1, 0]))
            step(nc.vector.tensor_copy(first_i[:], ex[0:1, 5]))
            step(nc.vector.tensor_scalar(more_i[:], ex[0:1, 4, EXPERTS - 1:EXPERTS], float(MAIN), None, ALU.is_gt))
            dve.wait_ge(list_step, CHUNKS)
            step(nc.vector.tensor_copy(slot_f[:, 0:2], bank[1][:, 0:2 * LIST].rearrange("p (a s) -> p a s", a=2)))
            step(nc.vector.tensor_scalar(slot_f[:, 2], slot_f[:, 0], 1.0, 0.0, ALU.subtract, ALU.max))
            nc.vector.tensor_copy(tok_i[:], slot_f[:, 2]).then_inc(tok_ready, 1)
            step(nc.vector.tensor_scalar(slot_f[:, 0], slot_f[:, 0], 0.0, part_f[:], ALU.is_equal, ALU.mult))
            step(nc.vector.tensor_tensor(slot_f[:, 0], slot_f[:, 0], slot_f[:, 2], ALU.add))
            nc.vector.tensor_copy(row_i[:], slot_f[:, 0]).then_inc(lists_ready, 1)

            def slot_scale(j, u, e, fresh):
                dve.wait_ge(tok_T, j + 1)
                if not fresh:
                    dve.wait_ge(xeT_low, j - 1)
                for k in range(HALVES):
                    g = ln_g[:, bass.ds(e, 1), k]
                    b = ln_b[:, bass.ds(e, 1), k]
                    nc.vector.tensor_scalar(xeT[:, u, k], bank[0][:, k * P:(k + 1) * P], g, b, ALU.mult, ALU.add
                                            ).then_inc(xeT_half, 1)

            def slot_bias(j, u, e, fresh):
                for c in range(2):
                    dve.wait_ge(hid_ps, 2 * j + c + 1)
                    if not fresh:
                        dve.wait_ge(hidT_ps, 2 * (j - 1))
                    b1 = bias[:, bass.ds(e % 2, 1), c * 512:(c + 1) * 512].rearrange("p a c -> p (a c)")
                    nc.vector.tensor_tensor(hid[:, u, c * 512:(c + 1) * 512], bank[1 + c][:], b1, ALU.add).then_inc(hid_b, 1)

            def slot_copy(j, fresh):
                for c in range(2):
                    dve.wait_ge(hidT_high, 2 * j + c + 1)
                    if not fresh:
                        dve.wait_ge(y_ps, j)
                    nc.vector.tensor_tensor(hidT_lo[:, 4 * c:4 * c + 4], bank[3 + c][:].rearrange("p (k c) -> p k c", k=4),
                                            hidT_hi[:, 4 * c:4 * c + 4].bitcast(F32), ALU.subtract).then_inc(hidT_low, 1)

            def slot_low(j, u, fresh):
                dve.wait_ge(xe_hi, j + 1)
                if not fresh:
                    dve.wait_ge(hid_ps, 2 * (j - 1))
                nc.vector.tensor_tensor(xeT_lo[:, u], xeT[:, u], xeT_hi[:, u].bitcast(F32), ALU.subtract).then_inc(xeT_low, 1)

            def split_weights(e):
                for q in range(W_HALF):
                    dve.wait_ge(whi_ready, W_PIECES * e + q + 1)
                    nc.vector.tensor_tensor(split_piece(e, q, True), raw[:, piece(q)], split_piece(e, q, False).bitcast(F32),
                                            ALU.subtract).then_inc(wlo_ready, 1)

            def split_where_new(e_last, e_here):
                if e_last is None:
                    split_weights(e_here + 1)
                else:
                    with dve.If(e_here > e_last):
                        split_weights(e_here + 1)
                    with dve.Else():
                        dve.nop()

            def slot_out(j, u, e, fresh):
                dve.wait_ge(y_ps, j + 1)
                if not fresh:
                    dve.wait_ge(row_ready, j)
                b2 = bias[:, bass.ds(e % 2, 1), HIDDEN:HIDDEN + DIM].rearrange("p a c -> p (a c)")
                nc.vector.tensor_tensor(ys[:, u], bank[5][:, 0:DIM], b2, ALU.add).then_inc(y_b, 1)

            def slot_step(j, u, e, fresh=False):
                slot_copy(j, fresh)
                split_where_new(e[0], e[1])
                slot_bias(j + 1, 1 - u, e[2], False)
                slot_scale(j + 2, u, e[3], False)
                slot_low(j + 2, u, False)
                slot_out(j, u, e[1], fresh)

            def slots(j0, n):
                fresh = j0 == 0
                e = [None, *experts_of(DVE, j0, 3)] if fresh else experts_of(DVE, j0 - 1, 4)
                slot_scale(j0, 0, e[1], fresh)
                slot_low(j0, 0, fresh)
                slot_bias(j0, 0, e[1], fresh)
                slot_scale(j0 + 1, 1, e[2], fresh)
                slot_low(j0 + 1, 1, fresh)
                slot_step(j0, 0, e, fresh)
                if n > 4:
                    with dve.Fori(0, (n - 4) // 4) as i:
                        e = experts_of(DVE, j0 + 4 * i, 7)
                        for k in range(4):
                            slot_step(j0 + 4 * i + 1 + k, (k + 1) % 2, e[k:k + 4])
                j = j0 + n - 3
                e = experts_of(DVE, j - 1, 4)
                slot_step(j, 1, e)
                slot_copy(j + 1, False)
                split_where_new(e[1], e[2])
                slot_bias(j + 2, 1, e[3], False)
                slot_out(j + 1, 0, e[2], False)
                slot_copy(j + 2, False)
                split_where_new(e[2], e[3])
                slot_out(j + 2, 1, e[3], False)

            slots(0, MAIN)
            second = dve.value_load(more_i[0:1, 0:1], min_val=0, max_val=1)
            with dve.If(second > 0):
                slots(MAIN, SLOTS - MAIN)
            with dve.Else():
                dve.nop()


_INS = ['x', 'src', 'dst', 'edge_attr_128', 'L0_gnn_W_edge', 'L0_gnn_b_edge', 'L0_gnn_W1', 'L0_gnn_b1', 'L0_gnn_W2',
        'L0_gnn_b2', 'L0_gnn_eps', 'L0_gnn_gamma', 'L0_gnn_beta', 'L0_mix_Wq', 'L0_mix_Wkv', 'L0_mix_Wproj',
        'L0_mix_bproj', 'L0_ffn_Wr', 'L0_ffn_br', 'L0_ffn_ln_g', 'L0_ffn_ln_b', 'L0_ffn_W1', 'L0_ffn_b1', 'L0_ffn_W2',
        'L0_ffn_b2']


def kernel(**inputs):
    import numpy as _np
    import concourse.bacc as _bacc
    from concourse import mybir as _mybir
    from concourse.bass_utils import run_bass_kernel_spmd as _run

    nc = _bacc.Bacc("TRN2", target_bir_lowering=False, num_devices=1)
    arrays, args = {}, {}
    for name in _INS:
        a = _np.ascontiguousarray(inputs[name])
        arrays[f"in_{name}"] = a
        args[name] = nc.dram_tensor(f"in_{name}", a.shape, _mybir.dt.from_np(a.dtype), kind="ExternalInput").ap()
    out = nc.dram_tensor("out_0", (NODES, DIM), F32, kind="ExternalOutput").ap()
    build(nc, args, out)
    r = _run(nc, [arrays], core_ids=[0])
    return r.results[0]["out_0"]
```
